# Optimizing a Trainium2 kernel written in Bass

```python
import numpy as np
import jax
import jax.numpy as jnp

def _softmax(x, axis=-1):
    return jax.nn.softmax(x, axis=axis)

def _gelu(x):
    return jax.nn.gelu(x, approximate=True)

def _silu(x):
    return jax.nn.silu(x)

def _sigmoid(x):
    return jax.nn.sigmoid(x)

def _layernorm(x, axis=-1, eps=1e-05):
    m = jnp.mean(x, axis=axis, keepdims=True)
    v = jnp.var(x, axis=axis, keepdims=True)
    return (x - m) / jnp.sqrt(v + eps)

def _scatter_add(tgt, idx, src, axis=0):
    return tgt.at[idx].add(src)

def _segment_sum(src, seg, n):
    return jax.ops.segment_sum(src, seg, n)
kernel_name = 'mk_adaln_d1_jaxref_r4_0504c2'

def setup_inputs(seed: int=0):
    np.random.seed(seed)
    _w = jnp.asarray

    def _L0_attn_setup():
        import jax, jax.numpy as jnp
        import numpy as np
        N_HEAD = 8
        HEAD = 64
        RATIO = 2
        DEG = 2
        N_EMBD = 256
        QKV = (RATIO + 2) * N_HEAD * HEAD

        def _rope(t):
            B, T, h, d = t.shape
            div = 2.0 * np.pi / float(T) ** (np.arange(0, d, 2, dtype=np.float32) / d)
            ang = jnp.arange(T, dtype=jnp.float32)[:, None] * jnp.asarray(div)[None, :]
            sin = jnp.repeat(jnp.sin(ang), 2, axis=-1)[None, :, None, :]
            cos = jnp.repeat(jnp.cos(ang), 2, axis=-1)[None, :, None, :]
            x1 = t[..., ::2]
            x2 = t[..., 1::2]
            rot = jnp.stack((-x2, x1), axis=-1).reshape(t.shape)
            return t * cos + rot * sin
        key = jax.random.key(seed)
        k1, k2, k3 = jax.random.split(key, 3)
        B, T = (1, 512)
        x = jax.random.normal(k1, (B, T, N_EMBD), dtype=jnp.float32)
        w_attn = jax.random.normal(k2, (N_EMBD, QKV + N_HEAD), dtype=jnp.float32) * N_EMBD ** (-0.5)
        w_proj = jax.random.normal(k3, (RATIO * N_HEAD * HEAD, N_EMBD), dtype=jnp.float32) * (RATIO * N_HEAD * HEAD) ** (-0.5)
        ln_w = jnp.ones((HEAD,), dtype=jnp.float32)
        return {'x': x, 'w_attn': w_attn, 'w_proj': w_proj, 'ln_w': ln_w}
    _L0_attn_in = _L0_attn_setup()

    def _L0_ffn_setup():
        import jax, jax.numpy as jnp
        import numpy as np
        E = 8
        TOP_K = 2
        CAP_FACTOR = 1.25
        MIN_CAP = 4
        SCORE_SCALE = 1.0

        def _ffn(x, w1, b1, w2, b2):
            return jax.nn.gelu(x @ w1 + b1, approximate=False) @ w2 + b2
        key = jax.random.key(seed)
        ks = jax.random.split(key, 6)
        B, S, D, I = (4, 512, 256, 1024)
        std = 0.02
        return {'x': jax.random.normal(ks[0], (B, S, D), jnp.float32), 'Wr': jax.random.normal(ks[1], (E, D), jnp.float32) * std, 'W1': jax.random.normal(ks[2], (E, D, I), jnp.float32) * std, 'b1': jnp.zeros((E, I), jnp.float32), 'W2': jax.random.normal(ks[3], (E, I, D), jnp.float32) * std, 'b2': jnp.zeros((E, D), jnp.float32), 'fw1': jax.random.normal(ks[4], (D, I), jnp.float32) * std, 'fb1': jnp.zeros((I,), jnp.float32), 'fw2': jax.random.normal(ks[5], (I, D), jnp.float32) * std, 'fb2': jnp.zeros((D,), jnp.float32)}
    _L0_ffn_in = _L0_ffn_setup()
    _L0_c = _w((lambda *s: np.random.randn(*s).astype(np.float32) * 0.05)(2, 256))
    _L0_wmod = _w((lambda *s: np.random.randn(*s).astype(np.float32) * 0.05)(256, 6 * 256) * 256 ** (-0.5))
    _d = {'L0_attn_x': _L0_attn_in['x'], 'L0_attn_w_attn': _L0_attn_in['w_attn'], 'L0_attn_w_proj': _L0_attn_in['w_proj'], 'L0_attn_ln_w': _L0_attn_in['ln_w'], 'L0_ffn_Wr': _L0_ffn_in['Wr'], 'L0_ffn_W1': _L0_ffn_in['W1'], 'L0_ffn_b1': _L0_ffn_in['b1'], 'L0_ffn_W2': _L0_ffn_in['W2'], 'L0_ffn_b2': _L0_ffn_in['b2'], 'L0_ffn_fw1': _L0_ffn_in['fw1'], 'L0_ffn_fb1': _L0_ffn_in['fb1'], 'L0_ffn_fw2': _L0_ffn_in['fw2'], 'L0_ffn_fb2': _L0_ffn_in['fb2'], 'L0_c': _L0_c, 'L0_wmod': _L0_wmod}
    _x0 = _d['L0_attn_x']
    _d['L0_attn_x'] = jax.random.normal(jax.random.fold_in(jax.random.key(seed), 1), (2, 2048, 256), dtype=_x0.dtype)
    del _x0
    return _d

def reference(L0_attn_x, L0_attn_w_attn, L0_attn_w_proj, L0_attn_ln_w, L0_ffn_Wr, L0_ffn_W1, L0_ffn_b1, L0_ffn_W2, L0_ffn_b2, L0_ffn_fw1, L0_ffn_fb1, L0_ffn_fw2, L0_ffn_fb2, L0_c, L0_wmod):

    def _L0_attn_ref(x, w_attn, w_proj, ln_w):
        import jax, jax.numpy as jnp
        import numpy as np
        N_HEAD = 8
        HEAD = 64
        RATIO = 2
        DEG = 2
        N_EMBD = 256
        QKV = (RATIO + 2) * N_HEAD * HEAD

        def _rope(t):
            B, T, h, d = t.shape
            div = 2.0 * np.pi / float(T) ** (np.arange(0, d, 2, dtype=np.float32) / d)
            ang = jnp.arange(T, dtype=jnp.float32)[:, None] * jnp.asarray(div)[None, :]
            sin = jnp.repeat(jnp.sin(ang), 2, axis=-1)[None, :, None, :]
            cos = jnp.repeat(jnp.cos(ang), 2, axis=-1)[None, :, None, :]
            x1 = t[..., ::2]
            x2 = t[..., 1::2]
            rot = jnp.stack((-x2, x1), axis=-1).reshape(t.shape)
            return t * cos + rot * sin
        B, T, C = x.shape
        h, d, r = (N_HEAD, HEAD, RATIO)
        hq = r * h
        qkvg = x @ w_attn
        q = qkvg[..., :hq * d].reshape(B, T, hq, d)
        k = qkvg[..., hq * d:(hq + h) * d].reshape(B, T, h, d)
        v = qkvg[..., (hq + h) * d:QKV].reshape(B, T, h, d)
        log_g = jax.nn.log_sigmoid(6.906768 + qkvg[..., QKV:])
        q = _rope(q)
        k = _rope(k)
        k = jnp.repeat(k, r, axis=2)
        v = jnp.repeat(v, r, axis=2)
        log_G = jnp.repeat(jnp.cumsum(log_g, axis=1), r, axis=2).transpose(0, 2, 1)
        scale = 1.0 / d ** 0.5
        s = jnp.einsum('bthd,bshd->bhts', q, k) * scale
        logits = DEG * jnp.log(jnp.abs(s) + 1e-30) + log_G[:, :, :, None] - log_G[:, :, None, :]
        mask = jnp.tril(jnp.ones((T, T), dtype=bool))
        logits = jnp.where(mask, logits, -jnp.inf)
        m = jax.lax.stop_gradient(jnp.max(logits, axis=-1, keepdims=True))
        a = jnp.exp(logits - m)
        if DEG % 2 == 1:
            a = a * jnp.sign(s)
        a = jnp.where(mask, a, 0.0)
        num = jnp.einsum('bhts,bshd->bthd', a, v)
        den = jnp.sum(a, axis=-1).transpose(0, 2, 1)
        y = num / (den[..., None] + 1e-06)
        mu = jnp.mean(y, axis=-1, keepdims=True)
        var = jnp.mean((y - mu) ** 2, axis=-1, keepdims=True)
        y = (y - mu) / jnp.sqrt(var + 1e-09) * ln_w
        return y.reshape(B, T, hq * d) @ w_proj

    def _L0_ffn_ref(x, Wr, W1, b1, W2, b2, fw1, fb1, fw2, fb2):
        import jax, jax.numpy as jnp
        import numpy as np
        E = 8
        TOP_K = 2
        CAP_FACTOR = 1.25
        MIN_CAP = 4
        SCORE_SCALE = 1.0

        def _ffn(x, w1, b1, w2, b2):
            return jax.nn.gelu(x @ w1 + b1, approximate=False) @ w2 + b2
        B, S, D = x.shape
        T = B * S
        x_flat = x.reshape(T, D)
        logits = x_flat @ Wr.T * SCORE_SCALE
        probs = jax.nn.softmax(logits, axis=-1)
        topk_scores, topk_experts = jax.lax.top_k(probs, TOP_K)
        topk_scores = topk_scores / jnp.clip(topk_scores.sum(-1, keepdims=True), 1e-09, None)
        cap = max(int(CAP_FACTOR * (T * TOP_K / E)), MIN_CAP)
        y_fb = _ffn(x_flat, fw1, fb1, fw2, fb2)
        y_flat = jnp.zeros_like(x_flat)
        fallback = jnp.zeros((T,), bool)
        tok_ids = jnp.arange(T, dtype=jnp.int32)
        for e in range(E):
            match = topk_experts == e
            elig = match.any(-1) & ~fallback
            pos = jnp.cumsum(elig) - 1
            kept = elig & (pos < cap)
            overflow = elig & (pos >= cap)
            slot = jnp.where(kept, pos, cap)
            buf = jnp.zeros((cap + 1,), jnp.int32).at[slot].set(tok_ids)
            vmask = jnp.zeros((cap + 1,), bool).at[slot].set(kept)
            idx = buf[:cap]
            valid = vmask[:cap]
            x_e = x_flat[idx]
            y_e = _ffn(x_e, W1[e], b1[e], W2[e], b2[e])
            w_tok = (topk_scores * match).sum(-1)
            w = jnp.where(valid, w_tok[idx], 0.0)
            y_flat = y_flat.at[idx].add(y_e * w[:, None])
            y_flat = jnp.where(overflow[:, None], y_fb, y_flat)
            fallback = fallback | overflow
        return y_flat.reshape(B, S, D)
    x = L0_attn_x
    mod = (_silu(L0_c) @ L0_wmod).reshape(L0_c.shape[0], 6, 1, -1)
    sa, ca, ga, sb, cb, gb = (mod[:, 0], mod[:, 1], mod[:, 2], mod[:, 3], mod[:, 4], mod[:, 5])
    ga = (2 * (ga >= 0) - 1) * jnp.maximum(jnp.abs(ga), 0.25)
    gb = (2 * (gb >= 0) - 1) * jnp.maximum(jnp.abs(gb), 0.25)
    h = _layernorm(x, axis=-1) * (1 + ca) + sa
    x = x + ga * _L0_attn_ref(h, L0_attn_w_attn, L0_attn_w_proj, L0_attn_ln_w)
    h = _layernorm(x, axis=-1) * (1 + cb) + sb
    x = x + gb * _L0_ffn_ref(h, L0_ffn_Wr, L0_ffn_W1, L0_ffn_b1, L0_ffn_W2, L0_ffn_b2, L0_ffn_fw1, L0_ffn_fb1, L0_ffn_fw2, L0_ffn_fb2)
    return x

_drawn_inputs = setup_inputs


def setup_inputs(seed=0):
    import zlib

    import numpy as np

    out = dict(_drawn_inputs(seed))
    spreads = {'L0_attn_ln_w': (1.0, 0.2),
     'L0_ffn_b1': (0.0, 0.8),
     'L0_ffn_b2': (0.0, 0.465),
     'L0_ffn_fb1': (0.0, 0.1),
     'L0_ffn_fb2': (0.0, 0.1)}
    factors = {'L0_ffn_W1': 3.015, 'L0_ffn_W2': 2.807}
    for name, (base, spread) in spreads.items():
        noise = np.random.default_rng([zlib.crc32(name.encode()), seed]).standard_normal(out[name].shape)
        drawn = base * np.exp(spread * noise) if base else spread * noise
        out[name] = jnp.asarray(drawn.astype(out[name].dtype))
    for name, factor in factors.items():
        out[name] = (out[name] * factor).astype(out[name].dtype)
    return out
```

```python
from contextlib import ExitStack

import concourse.bass as bass
from concourse import mybir
from concourse.alu_op_type import AluOpType as ALU

F32 = mybir.dt.float32
F32R = mybir.dt.float32r
U32 = mybir.dt.uint32
I32 = mybir.dt.int32
ACT = mybir.ActivationFunctionType
AX = mybir.AxisListType

P = 128
B, T, D = 2, 2048, 256
NTOK = B * T
NT = T // P
NTT = NTOK // P
KD = D // P
HEADS, KVH, HD = 16, 8, 64
QW, KW = HEADS * HD, KVH * HD
QKV = QW + 2 * KW
PAIRS = B * KVH
TB = 512
NB = T // TB
ST = TB // P
E, INNER, CAP = 8, 1024, 1280
KI = INNER // P
GATE_BIAS = 6.906768
LN_EPS = 1e-5
CREDIT = 16


def ready(k):
    return k + (CREDIT + 1)


def free(k, depth):
    return k + (CREDIT + 1 - depth)


class Program:

    def __init__(self, nc, ctx, tag):
        self.nc, self.ctx, self.tag, self.sems = nc, ctx, tag, []

    def sbuf(self, name, shape, dt=F32):
        return self.ctx.enter_context(self.nc.sbuf_tensor(f"{self.tag}_sb_{name}", shape, dt))

    def psum(self, name, shape, dt=F32):
        return self.ctx.enter_context(self.nc.psum_tensor(f"{self.tag}_ps_{name}", shape, dt))

    def sem(self, name):
        self.sems.append(self.nc.alloc_semaphore(f"{self.tag}_{name}"))
        return self.sems[-1]

    def give_back(self):
        def clear():
            with self.nc.Block() as block:
                @block.gpsimd
                def _(pool):
                    self.nc.clear_and_free_semaphores(self.sems)
        self.ctx.callback(clear)


def apart(eng, keep):
    eng.sem_inc(keep.passed, 1)


class Chain:

    def __init__(self, eng, sem, base=0):
        self.eng, self.sem, self.base, self.n = eng, sem, base, 0

    def link(self, ins):
        self.n += 1
        ins.then_inc(self.sem, 1)
        self.eng.wait_ge(self.sem, self.base + self.n)


def modulation(nc, keep, cond, wmod):
    with ExitStack() as ctx:
        m = Program(nc, ctx, "mod")
        cT = m.sbuf("cT", [P, B, KD])
        sT = m.sbuf("sT", [P, B, KD])
        sB = m.sbuf("sB", [P, B, KD, P])
        w = m.sbuf("w", [P, KD, 6 * D])
        pr = [m.psum(f"pr{i}", [P, 512]) for i in range(6)]
        pc = m.psum("pc", [P, 2 * KD, B])
        sem_in, silu_done, bcast_done, rows_done, cols_done, copied, chain = (
            m.sem(x) for x in ("in", "silu", "bcast", "rows", "cols", "copied", "chain"))
        block = ctx.enter_context(nc.Block())

        @block.sync
        def _(sp):
            for b in range(B):
                for k in range(KD):
                    sp.dma_start(cT[:, b, k:k + 1], cond[b, k * P:(k + 1) * P].rearrange("(p o) -> p o", o=1)).then_inc(sem_in, 16)
            sp.dma_start(w[:, :, :], wmod.rearrange("(k p) n -> p k n", p=P)).then_inc(sem_in, 16)

        @block.scalar
        def _(act):
            act.wait_ge(sem_in, 16 * (B * KD + 1))
            nc.scalar.activation(sT[:, :, :], cT[:, :, :], ACT.Silu).then_inc(silu_done, 1)

        @block.tensor
        def _(pe):
            pe.wait_ge(sem_in, 16 * (B * KD + 1))
            pe.wait_ge(silu_done, 1)
            for mm in range(2 * KD):
                for k in range(KD):
                    last = nc.tensor.matmul(pc[:, mm, :], w[:, k, mm * P:(mm + 1) * P], sT[:, :, k],
                                            start=(k == 0), stop=(k == KD - 1))
            last.then_inc(cols_done, 1)
            pe.wait_ge(bcast_done, 1)
            for b in range(B):
                for n in range(3):
                    for k in range(KD):
                        last = nc.tensor.matmul(pr[b * 3 + n][:, :], sB[:, b, k, :], w[:, k, n * 512:(n + 1) * 512],
                                                start=(k == 0), stop=(k == KD - 1))
            last.then_inc(rows_done, 1)

        @block.vector
        def _(dve):
            c = Chain(dve, chain)
            dve.wait_ge(silu_done, 1)
            nc.vector.tensor_copy(sB[:, :, :, :], sT[:, :, :, None].to_broadcast([P, B, KD, P])).then_inc(bcast_done, 1)
            dve.wait_ge(cols_done, 1)
            nc.vector.tensor_copy(keep.shift1[:, :, :], pc[:, 0:KD, :].rearrange("p k b -> p b k"))
            nc.vector.tensor_scalar(keep.scale1[:, :, :], pc[:, KD:2 * KD, :].rearrange("p k b -> p b k"), 1.0, None, ALU.add)
            dve.wait_ge(rows_done, 1)
            for b in range(B):
                for n in range(3):
                    c.link(nc.vector.tensor_copy(keep.mod[:, b, 2 * n:2 * n + 2, :],
                                                 pr[b * 3 + n][:, :].rearrange("p (s d) -> p s d", s=2)))
            for b in range(B):
                c.link(nc.vector.tensor_scalar(keep.mod[:, b, 4, :], keep.mod[:, b, 4, :], 1.0, None, ALU.add))
                for g in (2, 5):
                    c.link(nc.vector.tensor_scalar(keep.sign[:, :], keep.mod[:, b, g, :], 0.0, 2.0, ALU.is_ge, ALU.mult))
                    c.link(nc.vector.scalar_tensor_tensor(keep.mod[:, b, g, :], keep.mod[:, b, g, :], -1.0, keep.mod[:, b, g, :],
                                                          ALU.mult, ALU.max))
                    c.link(nc.vector.tensor_scalar(keep.mod[:, b, g, :], keep.mod[:, b, g, :], 0.25, None, ALU.max))
                    c.link(nc.vector.scalar_tensor_tensor(keep.mod[:, b, g, :], keep.sign[:, :], -1.0, keep.mod[:, b, g, :],
                                                          ALU.add, ALU.mult))


def project(nc, keep, x, w_attn, rope, q_rows, k_rows, v_cent, gate_logit):
    with ExitStack() as ctx:
        m = Program(nc, ctx, "proj")
        m.give_back()
        w = m.sbuf("w", [P, KD, QKV + KVH])
        w_hi = m.sbuf("w_hi", [P, KD, QKV], F32R)
        w_lo = m.sbuf("w_lo", [P, KD, QKV], F32R)
        w_mean = m.sbuf("w_mean", [P, 2, KD, KVH])
        tab = m.sbuf("tab", [P, 4, NT, HD])
        xt = m.sbuf("xt", [P, 2, D])
        st6 = m.sbuf("st6", [P, 6])
        mv = m.sbuf("mv", [P, 2, 2])
        rs = m.sbuf("rs", [P, 2, 2])
        xn = m.sbuf("xn", [P, 2, D])
        h = m.sbuf("h", [P, 2, KD, P])
        h_hi = m.sbuf("h_hi", [P, 2, KD, P], F32R)
        h_lo = m.sbuf("h_lo", [P, 2, KD, P], F32R)
        z = m.sbuf("z", [P, 3, KVH, HD])
        t1 = m.sbuf("t1", [P, 3, KVH, HD])
        t2 = m.sbuf("t2", [P, 3, KVH, HD])
        r = m.sbuf("r", [P, 3, KVH * HD])
        rT = m.sbuf("rT", [P, 3, 4, P])
        vt = m.sbuf("vt", [P, 2, KVH, HD])
        gs = m.sbuf("gs", [KVH, 2, P])
        eps = m.sbuf("eps", [P, 1])
        pc = [m.psum(f"pc{i}", [P, 512]) for i in range(4)]
        pr = [m.psum(f"pr{i}", [P, 4, P]) for i in range(2)]
        px = m.psum("px", [P, KD, P])
        pg = m.psum("pg", [KVH, P])
        w_in, mean_chain, w_hi_done, w_lo_done = m.sem("w_in"), m.sem("mean_chain"), m.sem("w_hi"), m.sem("w_lo")
        x_in = [m.sem(f"x_in{i}") for i in range(2)]
        var_done, std_done, rstd_done, xn_done, xnT_done, h_done, h_hi_done, h_lo_done = (
            m.sem(s) for s in ("var", "std", "rstd", "xn", "xnT", "h", "h_hi", "h_lo"))
        gate_mm, gate_out = m.sem("gate_mm"), m.sem("gate_out")
        chunk_mm, z_done, t1_done, t2_done, kr_done, qr_done, rot_done, rT_done, v_done = (
            m.sem(s) for s in ("chunk", "z", "t1", "t2", "kr", "qr", "rot", "rT", "v"))
        r_st = [m.sem(f"r_st{i}") for i in range(3)]
        v_st = [m.sem(f"v_st{i}") for i in range(2)]
        g_st = [m.sem(f"g_st{i}") for i in range(2)]
        ones_done, st_done = m.sem("ones"), m.sem("st")
        cols = [QW, 0, 512, QW + KW]
        x_t = x.rearrange("b (t p) d -> (b t) p d", p=P)
        block = ctx.enter_context(nc.Block())

        def turns(eng, turn):
            for n in range(2):
                turn(n, n % 2, True, n > 0, True)
            with eng.Fori(1, NTT // 2 - 1) as it:
                for p in range(2):
                    turn(it * 2 + p, p, True, True, True)
            for n in range(NTT - 2, NTT + 1):
                turn(n, n % 2, n < NTT, True, n + 1 < NTT)

        @block.sync
        def _(sp):
            sp.dma_start(w[:, :, :], w_attn.rearrange("(k p) n -> p k n", p=P)).then_inc(w_in, 16)
            sp.dma_start(tab[:, :, :, :], rope).then_inc(w_in, 16)
            for s in r_st + v_st + g_st:
                sp.sem_inc(s, 1)

            def rows(n, c):
                b, t = n // NT, n % NT
                dst, h0 = (k_rows, 0) if c == 0 else (q_rows, 8 * (c - 1))
                sp.wait_ge(rT_done, ready(n * 3 + c))
                apart(sp, keep)
                sp.dma_start(dst[b, h0:h0 + 8, :, bass.ds(t * P, P)].rearrange("(c hh) d t -> (hh d) c t", hh=2),
                             rT[:, c, :, :]).then_inc(r_st[c], 16)

            def turn(n, p, this, before, after):
                if this:
                    sp.wait_ge(gate_out, ready(n))
                    apart(sp, keep)
                    sp.dma_start(gate_logit[n // NT, :, bass.ds(n % NT * P, P)], gs[:, p, :]).then_inc(g_st[p], 16)
                if before:
                    rows(n - 1, 1)
                    rows(n - 1, 2)
                if this:
                    sp.wait_ge(v_done, ready(n))
                    apart(sp, keep)
                    sp.dma_start(v_cent[n // NT, :, :, n % NT, :].rearrange("j p d -> p j d"), vt[:, p, :, :]).then_inc(v_st[p], 16)
                    rows(n, 0)

            turns(sp, turn)
            for c in range(3):
                sp.wait_ge(r_st[c], 1 + 16 * NTT)
            for i in range(2):
                sp.wait_ge(v_st[i], 1 + 16 * (NTT // 2))
                sp.wait_ge(g_st[i], 1 + 16 * (NTT // 2))

        @block.scalar
        def _(act):
            for s in (std_done, h_done, h_hi_done, gate_out, z_done, rT_done, v_done):
                act.sem_inc(s, CREDIT)
            for i in range(2):
                act.dma_start(xt[:, i, :], x_t[i]).then_inc(x_in[i], 16)

            def std(n, p):
                act.wait_ge(var_done, ready(n))
                nc.scalar.activation(rs[:, p, 0:1], mv[:, p, 1:2], ACT.Sqrt, bias=eps[:, :]).then_inc(std_done, 1)

            def modulate(n, p):
                act.wait_ge(xnT_done, ready(n))
                act.wait_ge(chunk_mm, n * 4 + (CREDIT + 1 - 5))
                act.wait_ge(h_lo_done, free(n, 2))
                apart(act, keep)
                for k in range(KD):
                    last = nc.scalar.activation(h[:, p, k, :], px[:, k, :], ACT.Identity,
                                                scale=keep.scale1[:, n // NT, k:k + 1], bias=keep.shift1[:, n // NT, k:k + 1])
                last.then_inc(h_done, 1)
                act.wait_ge(h_done, ready(n))
                nc.scalar.activation(h_hi[:, p, :, :], h[:, p, :, :], ACT.Copy).then_inc(h_hi_done, 1)

            def evacuate(n, c):
                act.wait_ge(chunk_mm, ready(n * 4 + c))
                act.wait_ge(t1_done, free(n * 3 + c, 3))
                act.wait_ge(t2_done, free(n * 3 + c, 3))
                nc.scalar.activation(z[:, c, :, :], pc[c][:, :].rearrange("p (h d) -> p h d", d=HD), ACT.Copy).then_inc(z_done, 1)

            def turned(n, p, c):
                act.wait_ge(rot_done, ready(n * 3 + c))
                act.wait_ge(r_st[c], n * 16 + 1)
                nc.scalar.activation(rT[:, c, :, :], pr[(p + c) % 2][:, :, :], ACT.Copy).then_inc(rT_done, 1)

            act.wait_ge(w_in, 32)
            act.wait_ge(mean_chain, 5)
            for c in range(4):
                nc.scalar.activation(w_hi[:, :, cols[c]:cols[c] + 512], w[:, :, cols[c]:cols[c] + 512], ACT.Copy).then_inc(w_hi_done, 1)
            act.wait_ge(ones_done, 1)
            std(0, 0)
            modulate(0, 0)

            def turn(n, p, this, before, after):
                if this:
                    act.wait_ge(gate_mm, ready(n))
                    act.wait_ge(g_st[p], n // 2 * 16 + 1)
                    nc.scalar.activation(gs[:, p, :], pg[:, :], ACT.Copy).then_inc(gate_out, 1)
                    evacuate(n, 0)
                if after:
                    std(n + 1, 1 - p)
                if before:
                    turned(n - 1, 1 - p, 1)
                if this:
                    evacuate(n, 1)
                if before:
                    turned(n - 1, 1 - p, 2)
                if this:
                    act.wait_ge(xn_done, ready(n))
                    apart(act, keep)
                    act.dma_start(xt[:, p, :], x_t[(n + 2) % NTT]).then_inc(x_in[p], 16)
                    evacuate(n, 2)
                if after:
                    modulate(n + 1, 1 - p)
                if this:
                    act.wait_ge(chunk_mm, ready(n * 4 + 3))
                    act.wait_ge(v_st[p], n // 2 * 16 + 1)
                    nc.scalar.activation(vt[:, p, :, 0:HD - 1], pc[3][:, :].rearrange("p (h d) -> p h d", d=HD)[:, :, 0:HD - 1],
                                         ACT.Copy).then_inc(v_done, 1)
                    turned(n, p, 0)

            turns(act, turn)
            for i in range(2):
                act.wait_ge(x_in[i], 16 + 16 * (NTT // 2))

        @block.gpsimd
        def _(pool):
            for s in (t1_done, qr_done):
                pool.sem_inc(s, CREDIT)
            nc.gpsimd.memset(eps[:, :], LN_EPS)
            nc.gpsimd.memset(vt[:, :, :, HD - 1:HD], 1.0).then_inc(ones_done, 1)
            pool.wait_ge(w_in, 32)

            def cosine(n, c):
                k = n * 3 + c
                cos = tab[:, 2 if c == 0 else 0, n % NT, None, :].to_broadcast([P, KVH, HD])
                pool.wait_ge(z_done, ready(k))
                if c == 0:
                    pool.wait_ge(kr_done, free(n, 1))
                apart(pool, keep)
                nc.gpsimd.tensor_tensor(t1[:, c, :, :], z[:, c, :, :], cos, ALU.mult).then_inc(t1_done, 1)

            with pool.Fori(0, NTT) as n:
                cosine(n, 0)
                for c in range(1, 3):
                    k = n * 3 + c
                    cosine(n, c)
                    pool.wait_ge(t1_done, ready(k))
                    pool.wait_ge(t2_done, ready(k))
                    pool.wait_ge(rot_done, free(k, 3))
                    nc.gpsimd.tensor_tensor(r[:, c, :].rearrange("p (h d) -> p h d", d=HD), t1[:, c, :, :], t2[:, c, :, :],
                                            ALU.add).then_inc(qr_done, 1)

        @block.vector
        def _(dve):
            for s in (var_done, st_done, rstd_done, xn_done, t2_done, kr_done, h_lo_done):
                dve.sem_inc(s, CREDIT)
            dve.wait_ge(w_in, 32)
            c_ = Chain(dve, mean_chain)
            vw = w[:, :, QW + KW:QKV].rearrange("p k (h d) -> p k h d", d=HD)
            for k in range(KD):
                c_.link(nc.vector.reduce_sum(w_mean[:, 0, k, :], vw[:, k, :, :], AX.X))
            c_.link(nc.vector.tensor_scalar(w_mean[:, 1, :, :], w_mean[:, 0, :, :], -1.0 / HD, None, ALU.mult))
            for k in range(KD):
                c_.link(nc.vector.tensor_tensor(vw[:, k, :, :], vw[:, k, :, :],
                                                w_mean[:, 1, k, :, None].to_broadcast([P, KVH, HD]), ALU.add))

            def variance(n, p):
                dve.wait_ge(x_in[p], n // 2 * 16 + 16)
                nc.vector.bn_stats(st6[:, :], xt[:, p, :]).then_inc(st_done, 1)
                dve.wait_ge(st_done, ready(n))
                apart(dve, keep)
                nc.vector.bn_aggr(mv[:, p, :], st6[:, :]).then_inc(var_done, 1)

            def norm(n, p):
                dve.wait_ge(std_done, ready(n))
                nc.vector.reciprocal(rs[:, p, 1:2], rs[:, p, 0:1]).then_inc(rstd_done, 1)
                dve.wait_ge(rstd_done, ready(n))
                dve.wait_ge(xnT_done, free(n, 2))
                nc.vector.tensor_scalar(xn[:, p, :], xt[:, p, :], mv[:, p, 0:1], rs[:, p, 1:2],
                                        ALU.subtract, ALU.mult).then_inc(xn_done, 1)

            def rest(n, p):
                dve.wait_ge(h_hi_done, ready(n))
                nc.vector.tensor_tensor(h_lo[:, p, :, :], h[:, p, :, :], h_hi[:, p, :, :].bitcast(F32), ALU.subtract).then_inc(h_lo_done, 1)

            def sine(n, c):
                k = n * 3 + c
                sin = tab[:, 3 if c == 0 else 1, n % NT, :]
                dve.wait_ge(z_done, ready(k))
                if c:
                    dve.wait_ge(qr_done, free(n * 2 + c - 1, 2))
                else:
                    dve.wait_ge(kr_done, free(n, 1))
                nc.vector.tensor_tensor(t2[:, c, :, 0::2], z[:, c, :, 1::2],
                                        sin[:, None, 0::2].to_broadcast([P, KVH, HD // 2]), ALU.mult)
                nc.vector.tensor_tensor(t2[:, c, :, 1::2], z[:, c, :, 0::2],
                                        sin[:, None, 1::2].to_broadcast([P, KVH, HD // 2]), ALU.mult).then_inc(t2_done, 1)

            variance(0, 0)
            for c in range(4):
                dve.wait_ge(w_hi_done, c + 1)
                nc.vector.tensor_tensor(w_lo[:, :, cols[c]:cols[c] + 512], w[:, :, cols[c]:cols[c] + 512],
                                        w_hi[:, :, cols[c]:cols[c] + 512].bitcast(F32), ALU.subtract).then_inc(w_lo_done, 1)
            norm(0, 0)
            rest(0, 0)

            def turn(n, p, this, before, after):
                if after:
                    variance(n + 1, 1 - p)
                if this:
                    sine(n, 0)
                if after:
                    norm(n + 1, 1 - p)
                if this:
                    sine(n, 1)
                    dve.wait_ge(t1_done, ready(n * 3))
                    dve.wait_ge(t2_done, ready(n * 3))
                    dve.wait_ge(rot_done, free(n * 3, 3))
                    nc.vector.tensor_tensor(r[:, 0, :].rearrange("p (h d) -> p h d", d=HD), t1[:, 0, :, :], t2[:, 0, :, :],
                                            ALU.add).then_inc(kr_done, 1)
                    sine(n, 2)
                if after:
                    rest(n + 1, 1 - p)

            turns(dve, turn)

        @block.tensor
        def _(pe):
            for s in (xnT_done, gate_mm, chunk_mm, rot_done):
                pe.sem_inc(s, CREDIT)
            pe.wait_ge(w_in, 32)

            def transpose_in(n, p):
                pe.wait_ge(xn_done, ready(n))
                pe.wait_ge(h_done, free(n, 1))
                for k in range(KD):
                    last = nc.tensor.transpose(px[:, k, :], xn[:, p, k * P:(k + 1) * P], keep.ident[:, :])
                last.then_inc(xnT_done, 1)

            def chunk(n, p, c):
                if c < 3:
                    pe.wait_ge(z_done, free(n * 3 + c, 3))
                else:
                    pe.wait_ge(v_done, free(n, 1))
                at = slice(cols[c], cols[c] + 512)
                terms = [(a, b, k) for a, b in ((h_hi, w_hi), (h_lo, w_hi), (h_hi, w_lo)) for k in range(KD)]
                for i, (a, b, k) in enumerate(terms):
                    last = nc.tensor.matmul(pc[c][:, :], a[:, p, k, :], b[:, k, at], start=(i == 0), stop=(i == len(terms) - 1))
                last.then_inc(chunk_mm, 1)

            def rotated(n, p, c):
                if c:
                    pe.wait_ge(qr_done, ready(n * 2 + c - 1))
                else:
                    pe.wait_ge(kr_done, ready(n))
                pe.wait_ge(rT_done, free(n * 3 + c, 2))
                for j in range(4):
                    last = nc.tensor.transpose(pr[(p + c) % 2][:, j, :], r[:, c, j * P:(j + 1) * P], keep.ident[:, :])
                last.then_inc(rot_done, 1)

            transpose_in(0, 0)
            pe.wait_ge(w_lo_done, 4)

            def turn(n, p, this, before, after):
                if this:
                    pe.wait_ge(h_lo_done, ready(n))
                    pe.wait_ge(gate_out, free(n, 1))
                    for k in range(KD):
                        last = nc.tensor.matmul(pg[:, :], w[:, k, QKV:QKV + KVH], h[:, p, k, :], start=(k == 0), stop=(k == KD - 1))
                    last.then_inc(gate_mm, 1)
                    chunk(n, p, 0)
                if before:
                    rotated(n - 1, 1 - p, 1)
                if this:
                    chunk(n, p, 1)
                if before:
                    rotated(n - 1, 1 - p, 2)
                if this:
                    chunk(n, p, 2)
                if after:
                    transpose_in(n + 1, 1 - p)
                if this:
                    chunk(n, p, 3)
                    rotated(n, p, 0)

            turns(pe, turn)


def decays(nc, keep, gate_logit, half_log):
    CH = P // PAIRS
    CL = T // CH
    with ExitStack() as ctx:
        m = Program(nc, ctx, "dec")
        names = ("x", "mag", "e", "w", "lnw", "u", "sc")
        g = {s: m.sbuf(s, [P, CL]) for s in names}
        inv = m.sbuf("inv", [P, CL])
        one = m.sbuf("one", [P, CL])
        tot = m.sbuf("tot", [P, 1])
        pt = m.psum("pt", [P, 1])
        pn = [m.psum(f"pn{i}", [P, P]) for i in range(CL // P)]
        x_in, mag_done, e_done, w_done, ln_done, scan_done, carry_mm, sum_done, turned, stored, chain = (
            m.sem(s) for s in ("x_in", "mag", "e", "w", "ln", "scan", "carry", "sum", "turned", "stored", "chain"))
        block = ctx.enter_context(nc.Block())

        @block.sync
        def _(sp):
            sp.dma_start(g["x"][:, :], gate_logit.rearrange("b h (c t) -> (b h c) t", t=CL)).then_inc(x_in, 16)
            sp.wait_ge(sum_done, 1)
            sp.dma_start(half_log.rearrange("r (c t) -> (r c) t", t=CL), g["sc"][:, :]).then_inc(stored, 16)
            sp.wait_ge(stored, 16)

        @block.scalar
        def _(act):
            act.wait_ge(mag_done, 1)
            nc.scalar.activation(g["e"][:, :], g["mag"][:, :], ACT.Exp, scale=-1.0).then_inc(e_done, 1)
            act.wait_ge(w_done, 1)
            nc.scalar.activation(g["lnw"][:, :], g["w"][:, :], ACT.Ln).then_inc(ln_done, 1)
            act.wait_ge(turned, 1)
            for i in range(CL // P):
                nc.scalar.activation(keep.neg_half[:, :, i::CL // P],
                                     pn[i][:, :].rearrange("p (r c) -> p r c", r=PAIRS), ACT.Copy, scale=-1.0)

        @block.vector
        def _(dve):
            c = Chain(dve, chain)
            c.link(nc.vector.memset(one[:, :], 1.0))
            dve.wait_ge(x_in, 16)
            c.link(nc.vector.tensor_scalar(g["x"][:, :], g["x"][:, :], GATE_BIAS, None, ALU.add))
            nc.vector.scalar_tensor_tensor(g["mag"][:, :], g["x"][:, :], -1.0, g["x"][:, :], ALU.mult, ALU.max).then_inc(mag_done, 1)
            dve.wait_ge(e_done, 1)
            nc.vector.tensor_scalar(g["w"][:, :], g["e"][:, :], 1.0, None, ALU.add).then_inc(w_done, 1)
            dve.wait_ge(w_done, 1)
            c.link(nc.vector.reciprocal(inv[:, :], g["w"][:, :]))
            c.link(nc.vector.scalar_tensor_tensor(g["u"][:, :], g["w"][:, :], -1.0, g["e"][:, :], ALU.add, ALU.subtract))
            c.link(nc.vector.tensor_tensor(g["u"][:, :], g["u"][:, :], inv[:, :], ALU.mult))
            dve.wait_ge(ln_done, 1)
            c.link(nc.vector.tensor_tensor(g["u"][:, :], g["u"][:, :], g["lnw"][:, :], ALU.subtract))
            c.link(nc.vector.scalar_tensor_tensor(g["u"][:, :], g["x"][:, :], 0.0, g["u"][:, :], ALU.min, ALU.add))
            c.link(nc.vector.tensor_scalar(g["u"][:, :], g["u"][:, :], 0.5, None, ALU.mult))
            c.link(nc.vector.tensor_tensor_scan(g["mag"][:, :], one[:, :], g["u"][:, :], 0.0, ALU.mult, ALU.add))
            nc.vector.tensor_copy(tot[:, :], g["mag"][:, CL - 1:CL]).then_inc(scan_done, 1)
            dve.wait_ge(carry_mm, 1)
            c.link(nc.vector.tensor_copy(tot[:, :], pt[:, :]))
            nc.vector.tensor_scalar(g["sc"][:, :], g["mag"][:, :], tot[:, :], None, ALU.add).then_inc(sum_done, 1)

        @block.tensor
        def _(pe):
            pe.wait_ge(scan_done, 1)
            nc.tensor.matmul(pt[:, :], keep.before[:, :], tot[:, :], start=True, stop=True).then_inc(carry_mm, 1)
            pe.wait_ge(sum_done, 1)
            for i in range(CL // P):
                last = nc.tensor.transpose(pn[i][:, :], g["sc"][:, i * P:(i + 1) * P], keep.ident[:, :])
            last.then_inc(turned, 1)


GUARD = 1e-15


def attention_steps():
    off = {i: [("off", i, s) for s in range(ST * i)] for i in range(1, NB)}
    diag = {i: [("diag", i, j) for j in range(ST)] for i in range(NB)}
    steps = []
    for n, st in enumerate(off[3]):
        if n == 5:
            steps.append(("max", 1, 0))
        steps.append(st)
        if n % 3 == 2:
            steps.append(diag[0][n // 3])
    for n, st in enumerate(off[2]):
        steps.append(st)
        if n < ST:
            steps.append(diag[3][n])
        if n == 2:
            steps.append(("max", 0, 0))
    for n, st in enumerate(off[1]):
        steps.append(st)
        if n == 1:
            steps.append(("max", 3, 0))
        steps.append(diag[2][n])
    steps += diag[1][:3] + [("max", 2, 0)] + diag[1][3:]
    return steps


def attend(nc, keep, q_rows, k_rows, v_cent, half_log, num_rows, x_slots):
    steps = attention_steps()
    N = len(steps)
    squares = [n for n in range(N) if steps[n][0] != "max"]
    diags = [n for n in range(N) if steps[n][0] == "diag"]
    maxes = [n for n in range(N) if steps[n][0] == "max"]
    sq_of = {n: g for g, n in enumerate(squares)}
    mul_of = {n: d for d, n in enumerate(diags)}
    m_of = {n: r for r, n in enumerate(maxes)}
    NS, ND = len(squares), len(diags)

    def due(n):
        kind, _, j = steps[n]
        return min(n + (2.5 if kind == "off" else 4.5), N + 1.3)

    use_order = sorted(squares, key=lambda n: (due(n), n))
    use_of = {n: u for u, n in enumerate(use_order)}
    done_order = (0, 3, 2, 1)
    done_of = {i: d for d, i in enumerate(done_order)}
    last_off = {i: n for n in range(N) for k, i, _ in [steps[n]] if k == "off"}
    last_use = {i: n for n in use_order for k, i, _ in [steps[n]]}
    max_step = {steps[n][1]: n for n in maxes}
    after = {n: [] for n in range(N)}
    off_at = {(i, s): n for n in range(N) for k, i, s in [steps[n]] if k == "off"}
    diag_at = {(i, s): n for n in range(N) for k, i, s in [steps[n]] if k == "diag"}
    for j in range(ST):
        after[off_at[3, 4 + j]].append(("decay", 3, j))
        after[off_at[2, 1 + j]].append(("decay", 2, j))
        after[off_at[1, j]].append(("decay", 1, j))
        after[diag_at[1, j]].append(("decay", 0, j))
    after[diag_at[2, 3]].append(("factors", 0, 0))
    QCH = 1024
    QCN = 2 * T // QCH
    for c in range(QCN):
        after[off_at[[(3, 10), (3, 11), (2, 0), (2, 1)][c]]].append(("split_q", c, 0))
    for c in range(2):
        after[off_at[2, 5 + c]].append(("split_k", c, 0))
    A, R = 5, 3
    HI, LO = 2 * QCN + 2, QCN + 2
    decay_base = {0: 0, 3: ST, 2: 2 * ST, 1: 3 * ST}
    assert N % 2 == 0 and NS % A == 0 and list(decay_base) == list(done_order)
    assert all(sq_of[n] < sq_of[k] for n, k in zip(diags, diags[1:]))

    def off_slot(i, p):
        return (NB - 1 - i + p) % 2

    def off_before(q, i):
        return q * NB + done_of[i + 2] if i + 2 < NB else (q - 1) * NB + done_of[i - 1]

    def own_slot(i):
        return done_of[i] % 2

    def acc_slot(i, p):
        return {3: (0, 0), 0: (1, 2), 2: (2, 1), 1: (1, 2)}[i][p]

    with ExitStack() as ctx:
        m = Program(nc, ctx, "att")
        q_sb = [m.sbuf(f"q{i}", [P, 2 * T]) for i in range(2)]
        k_sb = [m.sbuf(f"k{i}", [P, 2, T]) for i in range(2)]
        v_sb = [m.sbuf(f"v{i}", [P, NT, HD]) for i in range(2)]
        hb = [m.sbuf(f"hb{i}", [P, T]) for i in range(2)]
        nh = m.sbuf("nh", [P, 2, NT])
        nfull = m.sbuf("nfull", [P, 2, NT])
        f = m.sbuf("f", [P, 2, NB - 1, NT - ST])
        fg = m.sbuf("fg", [P, 2, NB - 1, NT - ST])
        neg2 = m.sbuf("neg2", [P, 2, NB])
        guard = m.sbuf("guard", [P, 1])
        head = m.sbuf("head", [P, 2, QCH], F32R)
        et = m.sbuf("et", [P, 2, TB])
        dec = m.sbuf("dec", [P, 2, ST, TB])
        a = m.sbuf("a", [P, A, 2, TB])
        acc = m.sbuf("acc", [P, R, 2, TB])
        part = m.sbuf("part", [P, TB])
        num = m.sbuf("num", [P, 2, TB])
        zero = m.sbuf("zero", [P, D])
        s_ps = [m.psum(f"s{i}", [P, 2, TB]) for i in range(2)]
        off_ps = [m.psum(f"off{i}", [P, TB]) for i in range(2)]
        dg_ps = [m.psum(f"dg{i}", [P, TB]) for i in range(2)]
        zero_done, zero_st, guard_done = m.sem("zero"), m.sem("zero_st"), m.sem("guard")
        pair_in = [m.sem(f"pair_in{i}") for i in range(2)]
        num_st = [m.sem(f"num_st{i}") for i in range(2)]
        hi_done, lo_done, prep_done, et_done, exp_done, dec_done = (m.sem(s) for s in ("hi", "lo", "prep", "et", "exp", "dec"))
        s_done, sq_done, mul_done, av_done, max_done, row_done, num_done, scaled, part_done = (
            m.sem(s) for s in ("s", "sq", "mul", "av", "max", "row", "num", "scaled", "part"))
        block = ctx.enter_context(nc.Block())

        @block.sync
        def _(sp):
            for i in range(2):
                sp.sem_inc(num_st[i], 1)

            def load(q, p):
                b, j = q // KVH, q % KVH
                for half in range(2):
                    at = slice(half * HD, (half + 1) * HD)
                    sp.dma_start(q_sb[p][at, :].rearrange("d (h t) -> d h t", h=2),
                                 q_rows[b, bass.ds(j * 2, 2), :, :].rearrange("h d t -> d h t")).then_inc(pair_in[p], 16)
                    sp.dma_start(k_sb[p][at, 1, :], k_rows[b, j, :, :]).then_inc(pair_in[p], 16)
                sp.dma_start(v_sb[p][:, :, :], v_cent[b, j, :, :, :]).then_inc(pair_in[p], 16)
                sp.dma_start(hb[p][:, :], half_log[q, None, :].to_broadcast([P, T])).then_inc(pair_in[p], 16)

            load(0, 0)
            sp.wait_ge(zero_done, 1)
            slots = x_slots.rearrange("(r p) d -> r p d", p=P)
            with sp.Fori(0, E * CAP // P // 8) as r:
                sp.dma_start(slots[bass.ds(r * 8, 8)].rearrange("r p d -> p r d"),
                             zero[:, None, :].to_broadcast([P, 8, D])).then_inc(zero_st, 16)
            with sp.Fori(0, PAIRS // 2) as it:
                for p in range(2):
                    q = it * 2 + p
                    sp.wait_ge(av_done, ready(q * NS - 1))
                    sp.wait_ge(lo_done, ready(q * LO + LO - 1))
                    apart(sp, keep)
                    load((q + 1) % PAIRS, 1 - p)
                    for d, i in enumerate(done_order):
                        sp.wait_ge(num_done, ready(q * NB + d))
                        apart(sp, keep)
                        sp.dma_start(num_rows[q, :, i * TB:(i + 1) * TB], num[:, d % 2, :]).then_inc(num_st[d % 2], 16)
            for i in range(2):
                sp.wait_ge(num_st[i], 1 + 16 * PAIRS * NB // 2)
            sp.wait_ge(zero_st, 16 * (E * CAP // P // 8))

        def split(eng, act, q, p, what, c):
            if what == "split_q":
                at = slice(c * QCH, (c + 1) * QCH)
                lower, upper = q_sb[p][0:HD, at], q_sb[p][HD:P, at]
                if act:
                    eng.wait_ge(lo_done, ready(q * LO + c - 2) if c >= 2 else ready(q * LO - 4 + c))
                    nc.scalar.activation(head[HD:P, c % 2, :], upper, ACT.Copy).then_inc(hi_done, 1)
                    nc.scalar.activation(lower.bitcast(F32R), lower, ACT.Copy).then_inc(hi_done, 1)
                else:
                    eng.wait_ge(hi_done, ready(q * HI + 2 * c + 1))
                    both = q_sb[p][:, at]
                    nc.gpsimd.tensor_tensor(both.bitcast(F32R), both, head[:, c % 2, :].bitcast(F32), ALU.subtract).then_inc(lo_done, 1)
            else:
                at = slice(c * (T // 2), (c + 1) * (T // 2))
                first, second = k_sb[p][:, 0, at], k_sb[p][:, 1, at]
                if act:
                    nc.scalar.activation(first.bitcast(F32R), second, ACT.Copy).then_inc(hi_done, 1)
                else:
                    eng.wait_ge(hi_done, ready(q * HI + 2 * QCN + c))
                    nc.gpsimd.tensor_tensor(second.bitcast(F32R), second, first, ALU.subtract).then_inc(lo_done, 1)

        @block.gpsimd
        def _(pool):
            for s in (dec_done, mul_done, lo_done):
                pool.sem_inc(s, CREDIT)
            nc.gpsimd.memset(head[:, :, :].bitcast(F32), 0.0)
            nc.gpsimd.memset(guard[:, :], GUARD).then_inc(guard_done, 1)
            nc.gpsimd.memset(zero[:, :], 0.0).then_inc(zero_done, 1)

            def mask(q, i, j):
                pool.wait_ge(exp_done, ready(q * ND + decay_base[i] + j))
                apart(pool, keep)
                tile = dec[:, own_slot(i), j, 0:P]
                nc.gpsimd.affine_select(out=tile, in_=tile, compare_op=ALU.is_ge, fill=0.0, base=0,
                                        pattern=[[1, P]], channel_multiplier=-1).then_inc(dec_done, 1)

            pool.wait_ge(pair_in[0], 96)
            for c in range(QCN):
                split(pool, False, 0, 0, "split_q", c)
            for c in range(2):
                split(pool, False, 0, 0, "split_k", c)
            for j in range(ST):
                mask(0, 0, j)
            with pool.Fori(0, PAIRS // 2) as it:
                for p in range(2):
                    q = it * 2 + p
                    for n in range(N):
                        kind, i, j = steps[n]
                        if kind == "diag":
                            g = sq_of[n]
                            pool.wait_ge(dec_done, ready(q * ND + decay_base[i] + j))
                            pool.wait_ge(sq_done, ready(q * NS + g))
                            x = a[:, g % A, :, j * P:TB]
                            nc.gpsimd.tensor_tensor(x, x, dec[:, own_slot(i), j, None, 0:TB - j * P].to_broadcast([P, 2, TB - j * P]),
                                                    ALU.mult).then_inc(mul_done, 1)
                        for what, i_, c in after[n]:
                            if what == "decay":
                                mask(q + 1 if i_ == 0 else q, i_, c)
                            elif what != "factors":
                                split(pool, False, q + 1, 1 - p, what, i_)

        @block.scalar
        def _(act):
            for s in (hi_done, prep_done, et_done, exp_done, sq_done):
                act.sem_inc(s, CREDIT)

            def factors(q, p):
                k = q % PAIRS
                nc.scalar.activation(nh[:, p, :], keep.neg_half[:, k, :], ACT.Copy)
                nc.scalar.activation(nfull[:, p, :], keep.neg_half[:, k, :], ACT.Copy, scale=2.0).then_inc(prep_done, 1)
                act.wait_ge(prep_done, ready(q * 3))
                for i in range(1, NB):
                    last = nc.scalar.activation(f[:, p, i - 1, 0:ST * i], nh[:, p, 0:ST * i], ACT.Exp,
                                                bias=hb[p][:, i * TB:i * TB + 1])
                last.then_inc(prep_done, 1)
                act.wait_ge(prep_done, ready(q * 3 + 1))
                for i in range(1, NB):
                    nc.scalar.activation(fg[:, p, i - 1, 0:ST * i], f[:, p, i - 1, 0:ST * i], ACT.Copy, scale=GUARD)
                nc.scalar.activation(neg2[:, p, :], hb[p][:, 0::TB], ACT.Copy, scale=-2.0).then_inc(prep_done, 1)

            def query_factor(q, p, i):
                act.wait_ge(prep_done, ready(q * 3 + 2))
                act.wait_ge(num_done, ready(off_before(q, i)))
                nc.scalar.activation(et[:, off_slot(i, p), :], hb[p][:, i * TB:(i + 1) * TB], ACT.Exp, scale=2.0,
                                     bias=neg2[:, p, i:i + 1]).then_inc(et_done, 1)

            def decay(q, p, i, j):
                d = decay_base[i]
                if j == 0:
                    act.wait_ge(mul_done, ready(q * ND + d - ST - 1))
                w = TB - j * P
                nc.scalar.activation(dec[:, own_slot(i), j, 0:w], hb[p][:, i * TB + j * P:(i + 1) * TB], ACT.Exp,
                                     scale=2.0, bias=nfull[:, p, i * ST + j:i * ST + j + 1]).then_inc(exp_done, 1)

            act.wait_ge(guard_done, 1)
            act.wait_ge(pair_in[0], 96)
            for c in range(QCN):
                split(act, True, 0, 0, "split_q", c)
            for c in range(2):
                split(act, True, 0, 0, "split_k", c)
            factors(0, 0)
            act.wait_ge(prep_done, ready(2))
            for j in range(ST):
                decay(0, 0, 0, j)
            with act.Fori(0, PAIRS // 2) as it:
                for p in range(2):
                    q = it * 2 + p
                    for n in range(N):
                        kind, i, s = steps[n]
                        if kind != "max":
                            g = sq_of[n]
                            last = use_of[squares[(g - A) % NS]] + (q if g >= A else q - 1) * NS
                            act.wait_ge(av_done, ready(last))
                            act.wait_ge(max_done, ready(last))
                            act.wait_ge(s_done, ready(q * N + n))
                            if kind == "off":
                                nc.scalar.activation(a[:, g % A, :, :], s_ps[n % 2][:, :, :], ACT.Square,
                                                     scale=f[:, p, i - 1, s:s + 1], bias=fg[:, p, i - 1, s:s + 1]).then_inc(sq_done, 1)
                                if s == 0:
                                    query_factor(q, p, i)
                            else:
                                nc.scalar.activation(a[:, g % A, :, s * P:TB], s_ps[n % 2][:, :, s * P:TB], ACT.Square,
                                                     bias=guard[:, :]).then_inc(sq_done, 1)
                        for what, i_, c in after[n]:
                            if what == "decay":
                                if i_ == 0:
                                    decay(q + 1, 1 - p, 0, c)
                                else:
                                    decay(q, p, i_, c)
                            elif what == "factors":
                                factors(q + 1, 1 - p)
                                act.wait_ge(prep_done, ready((q + 1) * 3 + 2))
                            else:
                                if what == "split_q" and i_ == 0:
                                    act.wait_ge(pair_in[1 - p], it * 96 + 96 * (1 + p))
                                split(act, True, q + 1, 1 - p, what, i_)

        @block.vector
        def _(dve):
            for s in (max_done, row_done, num_done, scaled, part_done):
                dve.sem_inc(s, CREDIT)
            for i in range(R):
                last = nc.vector.memset(acc[:, i, :, :], 0.0)
            last.then_inc(part_done, 1)
            dve.wait_ge(part_done, CREDIT + 1)

            def maximum(q, p, n):
                kind, i, s = steps[n]
                g, u = sq_of[n], use_of[n]
                if kind == "off":
                    dve.wait_ge(sq_done, ready(q * NS + g))
                else:
                    dve.wait_ge(mul_done, ready(q * ND + mul_of[n]))
                x = acc[:, acc_slot(i, p), :, :]
                c = s * P if kind == "diag" else 0
                if s == 0 and (kind == "off" or i == 0):
                    nc.vector.tensor_copy(x, a[:, g % A, :, :]).then_inc(max_done, 1)
                else:
                    before = max(use_of[k] for k in squares if steps[k][1] == i and use_of[k] < u)
                    dve.wait_ge(max_done, ready(q * NS + before))
                    if kind == "diag" and s == 0:
                        dve.wait_ge(scaled, ready(q * (NB - 1) + NB - 1 - i))
                    nc.vector.tensor_tensor(x[:, :, c:TB], x[:, :, c:TB], a[:, g % A, :, c:TB], ALU.max).then_inc(max_done, 1)
                if last_off.get(i) == n:
                    dve.wait_ge(max_done, ready(q * NS + u))
                    dve.wait_ge(et_done, ready(q * (NB - 1) + NB - 1 - i))
                    nc.vector.tensor_tensor(x, x, et[:, off_slot(i, p), None, :].to_broadcast([P, 2, TB]), ALU.mult).then_inc(scaled, 1)

            def total(q, p, i):
                d = done_of[i]
                dve.wait_ge(av_done, ready(q * NS + use_of[last_use[i]]))
                own = dg_ps[own_slot(i)]
                dve.wait_ge(num_st[d % 2], (q * (NB // 2) + d // 2) * 16 + 1)
                if i == 0:
                    nc.vector.tensor_copy(num[:, d % 2, :], own[:, :]).then_inc(num_done, 1)
                else:
                    nc.vector.tensor_tensor(part[:, :], off_ps[off_slot(i, p)][:, :], et[:, off_slot(i, p), :], ALU.mult).then_inc(part_done, 1)
                    dve.wait_ge(part_done, ready(q * (NB - 1) + d))
                    nc.vector.tensor_tensor(num[:, d % 2, :], part[:, :], own[:, :], ALU.add).then_inc(num_done, 1)

            def rows(q, n, pair):
                i = steps[n][1]
                dve.wait_ge(s_done, ready(q * N + n))
                apart(dve, keep)
                nc.vector.tensor_reduce(keep.row_max[:, pair, i * ST:(i + 1) * ST, :].rearrange("p c h -> p h c"),
                                        s_ps[n % 2][:, :, :].rearrange("p h (c k) -> p h c k", k=P), AX.X, ALU.max).then_inc(row_done, 1)

            todo = [(due(n), 0, n) for n in use_order]
            todo += [(due(last_use[i]) + 1.7, 1, i) for i in range(NB)]
            todo += [(n + 1.6, 2, n) for n in maxes]
            todo.sort()
            with dve.Fori(0, PAIRS // 2) as it:
                for p in range(2):
                    q = it * 2 + p
                    for _, what, x in todo:
                        if what == 0:
                            maximum(q, p, x)
                        elif what == 1:
                            total(q, p, x)
                        else:
                            rows(q, x, (q + PAIRS - 1) % PAIRS if steps[x][1] == 1 else q)
            dve.wait_ge(s_done, ready(PAIRS * N + 2))
            nc.vector.tensor_reduce(keep.row_max[:, PAIRS - 1, ST:2 * ST, :].rearrange("p c h -> p h c"),
                                    s_ps[0][:, :, :].rearrange("p h (c k) -> p h c k", k=P), AX.X, ALU.max).then_inc(row_done, 1)

        @block.tensor
        def _(pe):
            for s in (s_done, av_done):
                pe.sem_inc(s, CREDIT)
            pe.wait_ge(part_done, CREDIT + 1)

            def turn_maxima(slot, ring):
                for h in range(2):
                    for c in range(ST):
                        last = nc.tensor.transpose(s_ps[slot][:, h, c * P:(c + 1) * P],
                                                   acc[:, ring, h, c * P:(c + 1) * P], keep.ident[:, :])
                last.then_inc(s_done, 1)

            def scores(q, p, n):
                kind, i, s = steps[n]
                k, pair = (n - 2) % N, q if n >= 2 else q - 1
                if steps[k][0] == "max":
                    pe.wait_ge(row_done, ready(pair * NB + m_of[k]))
                else:
                    pe.wait_ge(sq_done, ready(pair * NS + sq_of[k]))
                if kind == "max":
                    if i == 1:
                        pe.wait_ge(max_done, ready((q - 1) * NS + use_of[last_use[1]]))
                        turn_maxima(n % 2, acc_slot(1, 1 - p))
                    else:
                        pe.wait_ge(max_done, ready(q * NS + use_of[last_use[i]]))
                        turn_maxima(n % 2, acc_slot(i, p))
                    return
                if n == 0:
                    pe.wait_ge(hi_done, ready(q * HI + HI - 1))
                    pe.wait_ge(lo_done, ready(q * LO + LO - 1))
                key = s if kind == "off" else i * ST + s
                c = 0 if kind == "off" else s * P
                for h in range(2):
                    for hl in range(2):
                        last = nc.tensor.matmul(s_ps[n % 2][:, h, c:TB],
                                                k_sb[p][:, hl, key * P:(key + 1) * P].bitcast(F32R),
                                                q_sb[p][:, h * T + i * TB + c:h * T + (i + 1) * TB].bitcast(F32R),
                                                start=(hl == 0), stop=(hl == 1))
                last.then_inc(s_done, 1)

            def values(q, p, n):
                kind, i, s = steps[n]
                g = sq_of[n]
                key = s if kind == "off" else i * ST + s
                c = 0 if kind == "off" else s * P
                if s == 0:
                    d = done_of[i]
                    pe.wait_ge(num_done, free(q * NB + d, 2) if kind == "diag" else ready(off_before(q, i)))
                if kind == "off":
                    pe.wait_ge(sq_done, ready(q * NS + g))
                else:
                    pe.wait_ge(mul_done, ready(q * ND + mul_of[n]))
                ps = off_ps[off_slot(i, p)] if kind == "off" else dg_ps[own_slot(i)]
                for h in range(2):
                    last = nc.tensor.matmul(ps[h * HD:(h + 1) * HD, c:TB], v_sb[p][:, key, :], a[:, g % A, h, c:TB],
                                            start=(s == 0), stop=(s == (ST * i if kind == "off" else ST) - 1))
                last.then_inc(av_done, 1)

            AHEAD = 2
            todo = [(n, 0, n) for n in range(AHEAD, N)] + [(N + n, 1, n) for n in range(AHEAD)]
            todo += [(due(n), 2, n) for n in use_order]
            todo.sort()
            assert todo[0][1] == 0 or todo[0][0] > AHEAD - 1
            for n in range(AHEAD):
                scores(0, 0, n)
            with pe.Fori(0, PAIRS // 2) as it:
                for p in range(2):
                    q = it * 2 + p
                    for _, what, n in todo:
                        if what == 0:
                            scores(q, p, n)
                        elif what == 1:
                            scores(q + 1, 1 - p, n)
                        else:
                            values(q, p, n)
            pe.wait_ge(max_done, ready(PAIRS * NS - 1))
            turn_maxima(0, acc_slot(1, 1))


def close_attention(nc, keep, x, w_proj, ln_w, w_router, fold, num_rows, h2_rows):
    with ExitStack() as ctx:
        m = Program(nc, ctx, "close")
        w_raw = m.sbuf("w_raw", [P, KVH, D])
        w = m.sbuf("w", [P, KVH, D])
        fold_sb = m.sbuf("fold", [P, P])
        lnw = m.sbuf("lnw", [P, 1])
        wr = m.sbuf("wr", [P, KD, E])
        wr_raw = m.sbuf("wr_raw", [E, D])
        nT = m.sbuf("nT", [P, 2, KVH, P])
        xt = m.sbuf("xt", [P, 2, D])
        num = m.sbuf("num", [P, 2, HEADS, HD])
        sq = m.sbuf("sq", [P, HEADS, HD - 1])
        red = m.sbuf("red", [P, 8, HEADS])
        rinv = m.sbuf("rinv", [P, 2, HEADS])
        y = m.sbuf("y", [P, 2, HEADS, HD])
        yT = m.sbuf("yT", [P, 2, KVH, P])
        gx = m.sbuf("gx", [P, 2, D])
        st6 = m.sbuf("st6", [P, 6])
        mv = m.sbuf("mv", [P, 2, 2])
        rs = m.sbuf("rs", [P, 2, 2])
        xn = m.sbuf("xn", [P, 2, D])
        hs = m.sbuf("hs", [P, 2, D])
        h_st = m.sbuf("h_st", [P, 2, D])
        hT = m.sbuf("hT", [P, 2, KD, P])
        eps = m.sbuf("eps", [P, 1])
        pn = m.psum("pn", [P, HEADS, HD])
        py = m.psum("py", [P, KVH, P])
        pa = m.psum("pa", [P, D])
        ph = m.psum("ph", [P, KD, P])
        pl = m.psum("pl", [P, E])
        pw = m.psum("pw", [P, 2, D])
        w_in, scaled, fold_mm, folded, wr_mm, wr_done, eps_done = (
            m.sem(s) for s in ("w_in", "scaled", "fold_mm", "folded", "wr_mm", "wr", "eps"))
        n_in = [m.sem(f"n_in{i}") for i in range(2)]
        x_in = [m.sem(f"x_in{i}") for i in range(2)]
        h_out = [m.sem(f"h_out{i}") for i in range(2)]
        n_mm, num_done, sq_done, var_done, std_done, r_done, y_done, y_mm, yT_done, a_mm = (
            m.sem(s) for s in ("n_mm", "num", "sq", "var", "std", "r", "y", "y_mm", "yT", "a_mm"))
        gx_done, x1_done, var2_done, std2_done, xn_done, hs_done, h2_done, h_mm, hT_done, l_mm, l_done, head_chain, norm_chain = (
            m.sem(s) for s in ("gx", "x1", "var2", "std2", "xn", "hs", "h2", "h_mm", "hT", "l_mm", "l", "head_chain", "norm_chain"))
        x_t = x.rearrange("b (t p) d -> (b t) p d", p=P)
        num_t = num_rows.rearrange("(b j) p (t c) -> b t p j c", j=KVH, c=P)
        block = ctx.enter_context(nc.Block())

        def turns(eng, turn):
            for n in range(4):
                turn(n, n % 2, [n >= lag for lag in range(4)])
            with eng.Fori(2, NTT // 2) as it:
                for p in range(2):
                    turn(it * 2 + p, p, [True] * 4)
            for n in range(NTT, NTT + 3):
                turn(n, n % 2, [n - lag < NTT for lag in range(4)])

        @block.sync
        def _(sp):
            sp.dma_start(w_raw[:, :, :], w_proj.rearrange("(j p) n -> p j n", p=P)).then_inc(w_in, 16)
            sp.dma_start(fold_sb[:, :], fold).then_inc(w_in, 16)
            for h in range(2):
                sp.dma_start(lnw[h * HD:(h + 1) * HD, :], ln_w.rearrange("(d o) -> d o", o=1)).then_inc(w_in, 16)
            sp.dma_start(wr_raw[:, :], w_router).then_inc(w_in, 16)
            for p in range(2):
                sp.sem_inc(h_out[p], 1)
                sp.sem_inc(n_in[p], 1)
                sp.sem_inc(x_in[p], 1)
                sp.dma_start(nT[:, p, :, :], num_t[0, p]).then_inc(n_in[p], 16)
                sp.dma_start(xt[:, p, :], x_t[p]).then_inc(x_in[p], 16)

            def turn(n, p, there):
                if there[0]:
                    m_ = (n + 2) % NTT
                    sp.wait_ge(n_mm, ready(n))
                    apart(sp, keep)
                    sp.dma_start(nT[:, p, :, :], num_t[m_ // NT, m_ % NT]).then_inc(n_in[p], 16)
                if there[2]:
                    sp.wait_ge(h2_done, ready(n - 2))
                    apart(sp, keep)
                    sp.dma_start(h2_rows[n - 2], h_st[:, p, :]).then_inc(h_out[p], 16)
                if there[1]:
                    sp.wait_ge(x1_done, ready(n - 1))
                    apart(sp, keep)
                    sp.dma_start(xt[:, 1 - p, :], x_t[(n + 1) % NTT]).then_inc(x_in[1 - p], 16)

            turns(sp, turn)
            for p in range(2):
                sp.wait_ge(h_out[p], 1 + 16 * (NTT // 2))
                sp.wait_ge(n_in[p], 1 + 16 * (NTT // 2 + 1))
                sp.wait_ge(x_in[p], 1 + 16 * (NTT // 2 + 1))

        @block.scalar
        def _(act):
            for s in (sq_done, std_done, yT_done, std2_done, hT_done):
                act.sem_inc(s, CREDIT)
            act.wait_ge(eps_done, 1)

            def turn(n, p, there):
                if there[1]:
                    act.wait_ge(y_mm, ready(n - 1))
                    act.wait_ge(a_mm, free(n - 1, 2))
                    nc.scalar.activation(yT[:, 1 - p, :, :], py[:, :, :], ACT.Copy).then_inc(yT_done, 1)
                if there[0]:
                    act.wait_ge(num_done, ready(n))
                    act.wait_ge(var_done, free(n, 1))
                    nc.scalar.activation(sq[:, :, :], num[:, p, :, 0:HD - 1], ACT.Square).then_inc(sq_done, 1)
                if there[2]:
                    act.wait_ge(var2_done, ready(n - 2))
                    nc.scalar.activation(rs[:, p, 0:1], mv[:, p, 1:2], ACT.Sqrt, bias=eps[:, 0:1]).then_inc(std2_done, 1)
                if there[3]:
                    act.wait_ge(h_mm, ready(n - 3))
                    act.wait_ge(l_mm, free(n - 3, 2))
                    nc.scalar.activation(hT[:, 1 - p, :, :], ph[:, :, :], ACT.Copy).then_inc(hT_done, 1)
                if there[0]:
                    act.wait_ge(var_done, ready(n))
                    nc.scalar.activation(red[:, 6, :], red[:, 5, :], ACT.Sqrt).then_inc(std_done, 1)

            turns(act, turn)

        @block.gpsimd
        def _(pool):
            for s in (y_done, x1_done, hs_done, h2_done):
                pool.sem_inc(s, CREDIT)
            nc.gpsimd.memset(eps[:, 0:1], LN_EPS).then_inc(eps_done, 1)

            def turn(n, p, there):
                if there[0]:
                    pool.wait_ge(r_done, ready(n))
                    pool.wait_ge(y_mm, free(n, 2))
                    nc.gpsimd.tensor_tensor(y[:, p, :, :], num[:, p, :, :], rinv[:, p, :, None].to_broadcast([P, HEADS, HD]),
                                            ALU.mult).then_inc(y_done, 1)
                if there[1]:
                    pool.wait_ge(x_in[1 - p], (n - 1) // 2 * 16 + 17)
                    pool.wait_ge(gx_done, ready(n - 1))
                    apart(pool, keep)
                    nc.gpsimd.tensor_tensor(keep.x1[:, n - 1, :], xt[:, 1 - p, :], gx[:, 1 - p, :], ALU.add).then_inc(x1_done, 1)
                if there[2]:
                    b = (n - 2) // NT
                    pool.wait_ge(xn_done, ready(n - 2))
                    apart(pool, keep)
                    nc.gpsimd.tensor_tensor(hs[:, p, :], xn[:, p, :], keep.mod[:, b, 4, :], ALU.mult).then_inc(hs_done, 1)
                    pool.wait_ge(hs_done, ready(n - 2))
                    pool.wait_ge(h_mm, free(n - 2, 2))
                    pool.wait_ge(h_out[p], (n - 2) // 2 * 16 + 1)
                    apart(pool, keep)
                    nc.gpsimd.tensor_tensor(h_st[:, p, :], hs[:, p, :], keep.mod[:, b, 3, :], ALU.add).then_inc(h2_done, 1)

            turns(pool, turn)

        @block.vector
        def _(dve):
            for s in (num_done, var_done, r_done, gx_done, var2_done, xn_done, l_done):
                dve.sem_inc(s, CREDIT)
            dve.wait_ge(w_in, 80)
            nc.vector.tensor_scalar(w_raw[:, :, :], w_raw[:, :, :], lnw[:, :], None, ALU.mult).then_inc(scaled, 1)
            for g in range(KVH // 2):
                dve.wait_ge(fold_mm, g + 1)
                nc.vector.tensor_copy(w[:, 2 * g:2 * g + 2, :], pw[:, :, :]).then_inc(folded, 1)
            dve.wait_ge(wr_mm, 1)
            nc.vector.tensor_copy(wr[:, :, :], ph[:, :, 0:E]).then_inc(wr_done, 1)
            HEAD_OPS, NORM_OPS = 6, 2

            def turn(n, p, there):
                head = Chain(dve, head_chain, n * HEAD_OPS)
                norm = Chain(dve, norm_chain, (n - 2) * NORM_OPS)
                if there[0]:
                    b, t = n // NT, n % NT
                    row_max = keep.row_max[:, bass.ds(b * KVH, KVH), t, :]
                    dve.wait_ge(n_mm, ready(n))
                    apart(dve, keep)
                    head.link(nc.vector.scalar_tensor_tensor(red[:, 2, :].rearrange("p (j h) -> p j h", h=2), row_max, 1e-6,
                                                             pn[:, :, HD - 1].rearrange("p (j h) -> p j h", h=2), ALU.mult, ALU.add))
                    head.link(nc.vector.reciprocal(red[:, 3, :], red[:, 2, :]))
                    dve.wait_ge(y_done, free(n, 2))
                    nc.vector.tensor_tensor(num[:, p, :, :], pn[:, :, :], red[:, 3, :, None].to_broadcast([P, HEADS, HD]),
                                            ALU.mult).then_inc(num_done, 1)
                if there[2]:
                    dve.wait_ge(x1_done, ready(n - 2))
                    apart(dve, keep)
                    norm.link(nc.vector.bn_stats(st6[:, :], keep.x1[:, n - 2, :]))
                    apart(dve, keep)
                    nc.vector.bn_aggr(mv[:, p, :], st6[:, :]).then_inc(var2_done, 1)
                if there[0]:
                    dve.wait_ge(num_done, ready(n))
                    head.link(nc.vector.reduce_sum(red[:, 0, :], num[:, p, :, 0:HD - 1], AX.X))
                    head.link(nc.vector.tensor_tensor(red[:, 4, :], red[:, 0, :], red[:, 0, :], ALU.mult))
                    dve.wait_ge(sq_done, ready(n))
                    head.link(nc.vector.reduce_sum(red[:, 1, :], sq[:, :, :], AX.X))
                    head.link(nc.vector.tensor_tensor(red[:, 4, :], red[:, 4, :], red[:, 1, :], ALU.add))
                    nc.vector.tensor_scalar(red[:, 5, :], red[:, 4, :], 1.0 / HD, 1e-9, ALU.mult, ALU.add).then_inc(var_done, 1)
                    assert head.n == HEAD_OPS
                if there[2]:
                    dve.wait_ge(std2_done, ready(n - 2))
                    norm.link(nc.vector.reciprocal(rs[:, p, 1:2], rs[:, p, 0:1]))
                    dve.wait_ge(hs_done, free(n - 2, 2))
                    apart(dve, keep)
                    nc.vector.tensor_scalar(xn[:, p, :], keep.x1[:, n - 2, :], mv[:, p, 0:1], rs[:, p, 1:2],
                                            ALU.subtract, ALU.mult).then_inc(xn_done, 1)
                    assert norm.n == NORM_OPS
                if there[0]:
                    dve.wait_ge(std_done, ready(n))
                    nc.vector.reciprocal(rinv[:, p, :], red[:, 6, :]).then_inc(r_done, 1)
                if there[1]:
                    dve.wait_ge(a_mm, ready(n - 1))
                    dve.wait_ge(x1_done, free(n - 1, 2))
                    apart(dve, keep)
                    nc.vector.tensor_tensor(gx[:, 1 - p, :], pa[:, :], keep.mod[:, (n - 1) // NT, 2, :], ALU.mult).then_inc(gx_done, 1)
                if there[3]:
                    dve.wait_ge(l_mm, ready(n - 3))
                    apart(dve, keep)
                    nc.vector.tensor_copy(keep.logits[:, n - 3, :], pl[:, :]).then_inc(l_done, 1)

            turns(dve, turn)

        @block.tensor
        def _(pe):
            for s in (n_mm, y_mm, a_mm, h_mm, l_mm):
                pe.sem_inc(s, CREDIT)
            pe.wait_ge(w_in, 80)
            pe.wait_ge(scaled, 1)
            for g in range(KVH // 2):
                if g:
                    pe.wait_ge(folded, g)
                for i in range(2):
                    last = nc.tensor.matmul(pw[:, i, :], fold_sb[:, :], w_raw[:, 2 * g + i, :], start=True, stop=True)
                last.then_inc(fold_mm, 1)
            for k in range(KD):
                last = nc.tensor.transpose(ph[:, k, 0:E], wr_raw[:, k * P:(k + 1) * P], keep.ident[0:E, 0:E])
            last.then_inc(wr_mm, 1)
            pe.wait_ge(folded, KVH // 2)
            pe.wait_ge(wr_done, 1)

            def turn(n, p, there):
                if there[0]:
                    pe.wait_ge(n_in[p], n // 2 * 16 + 17)
                    pe.wait_ge(num_done, free(n, 1))
                    for j in range(KVH):
                        last = nc.tensor.transpose(pn[:, 2 * j:2 * j + 2, :], nT[:, p, j, :], keep.ident[:, :])
                    last.then_inc(n_mm, 1)
                if there[1]:
                    pe.wait_ge(y_done, ready(n - 1))
                    pe.wait_ge(yT_done, free(n - 1, 1))
                    for j in range(KVH):
                        last = nc.tensor.transpose(py[:, j, :], y[:, 1 - p, 2 * j:2 * j + 2, :], keep.ident[:, :])
                    last.then_inc(y_mm, 1)
                if there[3]:
                    pe.wait_ge(h2_done, ready(n - 3))
                    pe.wait_ge(hT_done, free(n - 3, 1))
                    for k in range(KD):
                        last = nc.tensor.transpose(ph[:, k, :], h_st[:, 1 - p, k * P:(k + 1) * P], keep.ident[:, :])
                    last.then_inc(h_mm, 1)
                if there[1]:
                    pe.wait_ge(yT_done, ready(n - 1))
                    pe.wait_ge(gx_done, free(n - 1, 1))
                    for j in range(KVH):
                        last = nc.tensor.matmul(pa[:, :], yT[:, 1 - p, j, :], w[:, j, :], start=(j == 0), stop=(j == KVH - 1))
                    last.then_inc(a_mm, 1)
                if there[3]:
                    pe.wait_ge(hT_done, ready(n - 3))
                    pe.wait_ge(l_done, free(n - 3, 1))
                    for k in range(KD):
                        last = nc.tensor.matmul(pl[:, :], hT[:, 1 - p, k, :], wr[:, k, :], start=(k == 0), stop=(k == KD - 1))
                    last.then_inc(l_mm, 1)

            turns(pe, turn)


def choose(nc, keep, upto, experts_row):
    SH = [P, NTT, E]
    FAR = float(1 << 20)
    with ExitStack() as ctx:
        m = Program(nc, ctx, "choose")
        tri = m.sbuf("tri", [P, P])
        ones = m.sbuf("ones", [P, P])
        er = m.sbuf("er", [P, E])
        ex = m.sbuf("ex", SH)
        pr = m.sbuf("pr", SH)
        tmp = m.sbuf("tmp", SH)
        hot = [m.sbuf(f"hot{i}", SH) for i in range(2)]
        match = m.sbuf("match", SH)
        kept = m.sbuf("kept", SH)
        place = m.sbuf("place", SH)
        r = {x: m.sbuf(x, [P, NTT]) for x in ("mx", "sum", "inv", "best", "s0", "s1", "elig", "run", "pos", "over", "keptk", "placek", "one")}
        lost = m.sbuf("lost", [P, 1])
        pos_ps = m.psum("pos", [P, NTT])
        tot_ps = m.psum("tot", [P, NTT])
        cnt_ps = m.psum("cnt", [P, 1])
        c_in, diff_done, exp_done, elig_done, count_mm, lost_done, lost_mm, chain = (
            m.sem(s) for s in ("in", "diff", "exp", "elig", "count", "lost", "lost_mm", "chain"))
        block = ctx.enter_context(nc.Block())

        @block.sync
        def _(sp):
            sp.dma_start(tri[:, :], upto).then_inc(c_in, 16)
            sp.dma_start(er[:, :], experts_row).then_inc(c_in, 16)

        @block.scalar
        def _(act):
            act.wait_ge(diff_done, 1)
            nc.scalar.activation(ex[:, :, :], tmp[:, :, :], ACT.Exp).then_inc(exp_done, 1)

        @block.tensor
        def _(pe):
            pe.wait_ge(c_in, 32)
            for e in range(E):
                pe.wait_ge(elig_done, e + 1)
                nc.tensor.matmul(pos_ps[:, :], tri[:, :], r["elig"][:, :], start=True, stop=True)
                nc.tensor.matmul(tot_ps[:, :], ones[:, :], r["elig"][:, :], start=True, stop=True).then_inc(count_mm, 1)
            pe.wait_ge(lost_done, 1)
            nc.tensor.matmul(cnt_ps[:, :], ones[:, :], lost[:, :], start=True, stop=True).then_inc(lost_mm, 1)

        @block.vector
        def _(dve):
            c = Chain(dve, chain)
            v = nc.vector

            def wide(x):
                return x[:, :, None].to_broadcast(SH)

            c.link(v.memset(ones[:, :], 1.0))
            c.link(v.memset(r["one"][:, :], 1.0))
            c.link(v.memset(keep.plain[:, :], 1.0))
            c.link(v.tensor_reduce(r["mx"][:, :], keep.logits[:, :, :], AX.X, ALU.max))
            v.tensor_tensor(tmp[:, :, :], keep.logits[:, :, :], wide(r["mx"]), ALU.subtract).then_inc(diff_done, 1)
            dve.wait_ge(exp_done, 1)
            c.link(v.reduce_sum(r["sum"][:, :], ex[:, :, :], AX.X))
            c.link(v.reciprocal(r["inv"][:, :], r["sum"][:, :]))
            c.link(v.tensor_tensor(pr[:, :, :], ex[:, :, :], wide(r["inv"]), ALU.mult))
            dve.wait_ge(c_in, 32)
            lane = er[:, None, :].to_broadcast(SH)
            for k in range(2):
                s = r["s0"] if k == 0 else r["s1"]
                c.link(v.tensor_reduce(s[:, :], pr[:, :, :], AX.X, ALU.max))
                c.link(v.tensor_tensor(tmp[:, :, :], pr[:, :, :], wide(s), ALU.is_equal))
                c.link(v.scalar_tensor_tensor(tmp[:, :, :], lane, -float(E), tmp[:, :, :], ALU.add, ALU.mult))
                c.link(v.tensor_reduce(r["best"][:, :], tmp[:, :, :], AX.X, ALU.min))
                c.link(v.tensor_scalar(r["best"][:, :], r["best"][:, :], float(E), None, ALU.add))
                c.link(v.tensor_tensor(hot[k][:, :, :], lane, wide(r["best"]), ALU.is_equal))
                if k == 0:
                    c.link(v.tensor_scalar(tmp[:, :, :], hot[0][:, :, :], -1.0, 1.0, ALU.mult, ALU.add))
                    c.link(v.tensor_tensor(pr[:, :, :], pr[:, :, :], tmp[:, :, :], ALU.mult))
                    c.link(v.tensor_tensor(pr[:, :, :], pr[:, :, :], hot[0][:, :, :], ALU.subtract))
            c.link(v.tensor_tensor(match[:, :, :], hot[0][:, :, :], hot[1][:, :, :], ALU.add))
            c.link(v.tensor_tensor(r["sum"][:, :], r["s0"][:, :], r["s1"][:, :], ALU.add))
            c.link(v.tensor_scalar(r["sum"][:, :], r["sum"][:, :], 1e-9, None, ALU.max))
            c.link(v.reciprocal(r["inv"][:, :], r["sum"][:, :]))
            for s in ("s0", "s1"):
                c.link(v.tensor_tensor(r[s][:, :], r[s][:, :], r["inv"][:, :], ALU.mult))
            for e in range(E):
                v.tensor_tensor(r["elig"][:, :], match[:, :, e], keep.plain[:, :], ALU.mult).then_inc(elig_done, 1)
                dve.wait_ge(count_mm, e + 1)
                c.link(v.tensor_tensor_scan(r["run"][:, :], r["one"][:, :], tot_ps[:, :], 0.0, ALU.mult, ALU.add))
                c.link(v.tensor_tensor(r["run"][:, :], r["run"][:, :], tot_ps[:, :], ALU.subtract))
                c.link(v.scalar_tensor_tensor(r["pos"][:, :], pos_ps[:, :], -1.0, r["run"][:, :], ALU.add, ALU.add))
                c.link(v.scalar_tensor_tensor(kept[:, :, e], r["pos"][:, :], float(CAP), r["elig"][:, :], ALU.is_lt, ALU.mult))
                c.link(v.tensor_scalar(place[:, :, e], r["pos"][:, :], float(e * CAP), None, ALU.add))
                c.link(v.tensor_tensor(r["over"][:, :], r["elig"][:, :], kept[:, :, e], ALU.subtract))
                c.link(v.tensor_tensor(keep.plain[:, :], keep.plain[:, :], r["over"][:, :], ALU.subtract))
            for k in range(2):
                c.link(v.tensor_tensor(tmp[:, :, :], hot[k][:, :, :], kept[:, :, :], ALU.mult))
                c.link(v.reduce_sum(r["keptk"][:, :], tmp[:, :, :], AX.X))
                c.link(v.tensor_tensor(tmp[:, :, :], tmp[:, :, :], place[:, :, :], ALU.mult))
                c.link(v.reduce_sum(r["placek"][:, :], tmp[:, :, :], AX.X))
                c.link(v.tensor_copy(keep.outof[:, :, k], r["placek"][:, :]))
                c.link(v.tensor_scalar(r["pos"][:, :], r["keptk"][:, :], -FAR, FAR, ALU.mult, ALU.add))
                c.link(v.tensor_tensor(keep.into[:, :, k], r["placek"][:, :], r["pos"][:, :], ALU.add))
                c.link(v.tensor_tensor(r["keptk"][:, :], r["keptk"][:, :], keep.plain[:, :], ALU.mult))
                c.link(v.tensor_tensor(keep.weight[:, k, :], r["keptk"][:, :], r["s0" if k == 0 else "s1"][:, :], ALU.mult))
            c.link(v.tensor_scalar(r["over"][:, :], keep.plain[:, :], -1.0, 1.0, ALU.mult, ALU.add))
            v.reduce_sum(lost[:, :], r["over"][:, :], AX.X).then_inc(lost_done, 1)
            dve.wait_ge(lost_mm, 1)
            c.link(v.tensor_copy(keep.flag[:, :], cnt_ps[:, :]))


def dispatch(nc, keep, h2_rows, x_slots):
    RING = 4
    with ExitStack() as ctx:
        m = Program(nc, ctx, "disp")
        h = [m.sbuf(f"h{i}", [P, D]) for i in range(RING)]
        idx = [[m.sbuf(f"idx{i}_{k}", [P, 1], I32) for k in range(2)] for i in range(RING)]
        h_in = [m.sem(f"h_in{i}") for i in range(RING)]
        sent = [m.sem(f"sent{i}") for i in range(RING)]
        idx_done = m.sem("idx")
        block = ctx.enter_context(nc.Block())

        @block.sync
        def _(sp):
            for i in range(RING):
                sp.dma_start(h[i][:, :], h2_rows[i]).then_inc(h_in[i], 16)
            with sp.Fori(1, NTT // RING) as it:
                for i in range(RING):
                    sp.wait_ge(sent[i], it * 32)
                    sp.dma_start(h[i][:, :], h2_rows[it * RING + i]).then_inc(h_in[i], 16)

        @block.scalar
        def _(act):
            act.sem_inc(idx_done, CREDIT)

            def places(n, i):
                for k in range(2):
                    last = nc.scalar.activation(idx[i][k][:, :], keep.into[:, n, k:k + 1], ACT.Copy)
                last.then_inc(idx_done, 1)

            for i in range(RING):
                places(i, i)
            with act.Fori(1, NTT // RING) as it:
                for i in range(RING):
                    act.wait_ge(sent[i], it * 32)
                    places(it * RING + i, i)

        @block.gpsimd
        def _(pool):
            with pool.Fori(0, NTT // RING) as it:
                for i in range(RING):
                    pool.wait_ge(h_in[i], it * 16 + 16)
                    pool.wait_ge(idx_done, ready(it * RING + i))
                    apart(pool, keep)
                    for k in range(2):
                        nc.gpsimd.indirect_dma_start(x_slots, bass.IndirectOffsetOnAxis(ap=idx[i][k][:, :].bitcast(U32), axis=0),
                                                     h[i][:, :], None, bounds_check=E * CAP - 1,
                                                     oob_is_err=False).then_inc(sent[i], 16)
            for i in range(RING):
                pool.wait_ge(sent[i], 32 * (NTT // RING))


def experts(nc, keep, w1, b1, w2, b2, x_slots, y_slots):
    XT = CAP // P
    GROUPS = [(0, 4), (4, 4), (8, 2)]
    NG = len(GROUPS)
    with ExitStack() as ctx:
        m = Program(nc, ctx, "ffn")
        w1_sb = [m.sbuf(f"w1_{i}", [P, KD, INNER]) for i in range(2)]
        w2_sb = [m.sbuf(f"w2_{i}", [P, KI, D]) for i in range(2)]
        b1_rows = m.sbuf("b1_rows", [E * KI, P])
        b1_cols = m.sbuf("b1_cols", [P, E * KI])
        b2_sb = [m.sbuf(f"b2_{i}", [P, D]) for i in range(2)]
        xs = [m.sbuf(f"xs{i}", [P, XT, D]) for i in range(2)]
        xT = m.sbuf("xT", [P, KD, CAP])
        hT = m.sbuf("hT", [P, 2, KI, 4 * P])
        ys = m.sbuf("ys", [P, 2, D])
        px = [m.psum(f"px{i}", [P, KD, P]) for i in range(2)]
        p1 = [m.psum(f"p1_{i}", [P, 4 * P]) for i in range(4)]
        p2 = [m.psum(f"p2_{i}", [P, D]) for i in range(2)]
        e_in = [m.sem(f"in{i}") for i in range(2)]
        y_st = [m.sem(f"y_st{i}") for i in range(2)]
        b1_in, b1_mm, b1_done = m.sem("b1_in"), m.sem("b1_mm"), m.sem("b1")
        xT_mm, xT_done, up_mm, up_done, y_mm, y_done = (m.sem(s) for s in ("xT_mm", "xT", "up_mm", "up", "y_mm", "y"))
        block = ctx.enter_context(nc.Block())

        @block.sync
        def _(sp):
            for i in range(2):
                sp.sem_inc(y_st[i], 1)

            def load(e, p):
                sp.dma_start(xs[p][:, :, :], x_slots[bass.ds(e * CAP, CAP), :].rearrange("(t p) d -> p t d", p=P)).then_inc(e_in[p], 16)
                sp.dma_start(w1_sb[p][:, :, :], w1[e].rearrange("(k p) n -> p k n", p=P)).then_inc(e_in[p], 16)
                sp.dma_start(w2_sb[p][:, :, :], w2[e].rearrange("(m p) n -> p m n", p=P)).then_inc(e_in[p], 16)
                sp.dma_start(b2_sb[p][:, :], b2[e, None, :].to_broadcast([P, D])).then_inc(e_in[p], 16)

            sp.dma_start(b1_rows[:, :], b1.rearrange("e (m p) -> (e m) p", p=P)).then_inc(b1_in, 16)
            load(0, 0)
            with sp.Fori(0, E // 2) as it:
                for p in range(2):
                    e = it * 2 + p
                    sp.wait_ge(y_done, ready(e * XT - 1))
                    load((e + 1) % E, 1 - p)
                    for t in range(XT):
                        sp.wait_ge(y_done, ready(e * XT + t))
                        sp.dma_start(y_slots[bass.ds(e * CAP + t * P, P), :], ys[:, t % 2, :]).then_inc(y_st[t % 2], 16)
            for i in range(2):
                sp.wait_ge(y_st[i], 1 + 16 * E * XT // 2)
            sp.wait_ge(e_in[0], 64 * (E // 2 + 1))

        @block.scalar
        def _(act):
            act.sem_inc(up_done, CREDIT)
            act.wait_ge(b1_done, 1)
            with act.Fori(0, E // 2) as it:
                for p in range(2):
                    e = it * 2 + p
                    for g, (t0, nt) in enumerate(GROUPS):
                        for k in range(KI):
                            u = (e * NG + g) * KI + k
                            act.wait_ge(up_mm, ready(u))
                            if k == 0:
                                if g >= 2:
                                    act.wait_ge(y_mm, ready(e * XT + GROUPS[g - 2][0] + GROUPS[g - 2][1] - 1))
                                else:
                                    prev = GROUPS[g + 1]
                                    act.wait_ge(y_mm, ready((e - 1) * XT + prev[0] + prev[1] - 1))
                            apart(act, keep)
                            nc.scalar.activation(hT[:, (p * NG + g) % 2, k, 0:nt * P], p1[(g * KI + k) % 4][:, 0:nt * P], ACT.Gelu,
                                                 bias=b1_cols[:, bass.ds(e * KI + k, 1)]).then_inc(up_done, 1)

        @block.vector
        def _(dve):
            for s in (xT_done, y_done):
                dve.sem_inc(s, CREDIT)
            dve.wait_ge(b1_mm, 1)
            nc.vector.tensor_copy(b1_cols[:, :], p2[0][:, 0:E * KI]).then_inc(b1_done, 1)
            with dve.Fori(0, E // 2) as it:
                for p in range(2):
                    e = it * 2 + p
                    dve.wait_ge(e_in[p], it * 64 + 64)
                    def outputs(g):
                        t0, nt = GROUPS[g]
                        for t in range(t0, t0 + nt):
                            dve.wait_ge(y_mm, ready(e * XT + t))
                            dve.wait_ge(y_st[t % 2], (e * XT // 2 + t // 2) * 16 + 1)
                            nc.vector.tensor_tensor(ys[:, t % 2, :], p2[t % 2][:, :], b2_sb[p][:, :], ALU.add).then_inc(y_done, 1)
                    for g, (t0, nt) in enumerate(GROUPS):
                        for t in range(t0, t0 + nt):
                            dve.wait_ge(xT_mm, ready(e * XT + t))
                            nc.vector.tensor_copy(xT[:, :, t * P:(t + 1) * P], px[t % 2][:, :, :]).then_inc(xT_done, 1)
                        if g >= 1:
                            outputs(g - 1)
                    outputs(NG - 1)

        @block.tensor
        def _(pe):
            for s in (xT_mm, up_mm, y_mm):
                pe.sem_inc(s, CREDIT)
            pe.wait_ge(b1_in, 16)
            nc.tensor.transpose(p2[0][:, 0:E * KI], b1_rows[:, :], keep.ident[0:E * KI, 0:E * KI]).then_inc(b1_mm, 1)
            pe.wait_ge(b1_done, 1)
            with pe.Fori(0, E // 2) as it:
                for p in range(2):
                    e = it * 2 + p
                    pe.wait_ge(e_in[p], it * 64 + 64)

                    def turn(t):
                        pe.wait_ge(xT_done, free(e * XT + t, 2))
                        for k in range(KD):
                            last = nc.tensor.transpose(px[t % 2][:, k, :], xs[p][:, t, k * P:(k + 1) * P], keep.ident[:, :])
                        last.then_inc(xT_mm, 1)

                    def up(g):
                        t0, nt = GROUPS[g]
                        pe.wait_ge(xT_done, ready(e * XT + t0 + nt - 1))
                        for j in range(KI):
                            u = (e * NG + g) * KI + j
                            pe.wait_ge(up_done, free(u, 4))
                            for k in range(KD):
                                last = nc.tensor.matmul(p1[(g * KI + j) % 4][:, 0:nt * P], w1_sb[p][:, k, j * P:(j + 1) * P],
                                                        xT[:, k, t0 * P:(t0 + nt) * P], start=(k == 0), stop=(k == KD - 1))
                            last.then_inc(up_mm, 1)

                    def down(g):
                        t0, nt = GROUPS[g]
                        pe.wait_ge(up_done, ready((e * NG + g) * KI + KI - 1))
                        for t in range(t0, t0 + nt):
                            pe.wait_ge(y_done, free(e * XT + t, 2))
                            for j in range(KI):
                                last = nc.tensor.matmul(p2[t % 2][:, :], hT[:, (p * NG + g) % 2, j, (t - t0) * P:(t - t0 + 1) * P],
                                                        w2_sb[p][:, j, :], start=(j == 0), stop=(j == KI - 1))
                            last.then_inc(y_mm, 1)

                    for t in range(GROUPS[0][1]):
                        turn(t)
                    for g in range(NG):
                        up(g)
                        if g + 1 < NG:
                            for t in range(GROUPS[g + 1][0], sum(GROUPS[g + 1])):
                                turn(t)
                        if g:
                            down(g - 1)
                    down(NG - 1)


def combine(nc, keep, y_slots, out):
    RING = 4
    with ExitStack() as ctx:
        m = Program(nc, ctx, "comb")
        rows = [[m.sbuf(f"rows{i}_{k}", [P, D]) for k in range(2)] for i in range(RING)]
        idx = [[m.sbuf(f"idx{i}_{k}", [P, 1], I32) for k in range(2)] for i in range(RING)]
        ta = m.sbuf("ta", [P, D])
        tb = m.sbuf("tb", [P, D])
        tc = m.sbuf("tc", [P, D])
        o = m.sbuf("o", [P, RING, D])
        got = [m.sem(f"got{i}") for i in range(RING)]
        o_st = [m.sem(f"o_st{i}") for i in range(RING)]
        idx_done, used, o_done, chain = m.sem("idx"), m.sem("used"), m.sem("o"), m.sem("chain")
        out_t = out.rearrange("b (t p) d -> (b t) p d", p=P)
        block = ctx.enter_context(nc.Block())

        @block.scalar
        def _(act):
            act.sem_inc(idx_done, CREDIT)
            with act.Fori(0, NTT // RING) as it:
                for i in range(RING):
                    n = it * RING + i
                    act.wait_ge(used, free(n, RING))
                    for k in range(2):
                        last = nc.scalar.activation(idx[i][k][:, :], keep.outof[:, n, k:k + 1], ACT.Copy)
                    last.then_inc(idx_done, 1)

        @block.gpsimd
        def _(pool):
            with pool.Fori(0, NTT // RING) as it:
                for i in range(RING):
                    n = it * RING + i
                    pool.wait_ge(idx_done, ready(n))
                    pool.wait_ge(used, free(n, RING))
                    apart(pool, keep)
                    for k in range(2):
                        nc.gpsimd.indirect_dma_start(rows[i][k][:, :], None, y_slots,
                                                     bass.IndirectOffsetOnAxis(ap=idx[i][k][:, :].bitcast(U32), axis=0),
                                                     bounds_check=E * CAP - 1, oob_is_err=True).then_inc(got[i], 16)

        @block.vector
        def _(dve):
            for s in (used, o_done):
                dve.sem_inc(s, CREDIT)
            with dve.Fori(0, NTT // RING) as it:
                for i in range(RING):
                    n = it * RING + i
                    c = Chain(dve, chain, n * 2)
                    dve.wait_ge(got[i], it * 32 + 32)
                    c.link(nc.vector.tensor_scalar(ta[:, :], rows[i][0][:, :], keep.weight[:, 0, bass.ds(n, 1)], None, ALU.mult))
                    nc.vector.scalar_tensor_tensor(tb[:, :], rows[i][1][:, :], keep.weight[:, 1, bass.ds(n, 1)], ta[:, :],
                                                   ALU.mult, ALU.add).then_inc(used, 1)
                    dve.wait_ge(used, ready(n))
                    c.link(nc.vector.tensor_tensor(tc[:, :], tb[:, :], keep.mod[:, n // NT, 5, :], ALU.mult))
                    dve.wait_ge(o_st[i], it * 16 + 1)
                    nc.vector.tensor_tensor(o[:, i, :], tc[:, :], keep.x1[:, n, :], ALU.add).then_inc(o_done, 1)

        @block.sync
        def _(sp):
            for i in range(RING):
                sp.sem_inc(o_st[i], 1)
            with sp.Fori(0, NTT // RING) as it:
                for i in range(RING):
                    n = it * RING + i
                    sp.wait_ge(o_done, ready(n))
                    sp.dma_start(out_t[n], o[:, i, :]).then_inc(o_st[i], 16)
            for i in range(RING):
                sp.wait_ge(o_st[i], 1 + 16 * (NTT // RING))


def fall_back(nc, keep, fw1, fb1, fw2, fb2, h2_rows, out):
    with ExitStack() as ctx:
        m = Program(nc, ctx, "fall")
        w1 = m.sbuf("w1", [P, KD, INNER])
        w2 = m.sbuf("w2", [P, KI, D])
        b1_rows = m.sbuf("b1_rows", [KI, P])
        b1_cols = m.sbuf("b1_cols", [P, KI])
        b2 = m.sbuf("b2", [P, D])
        x = m.sbuf("x", [P, D])
        o = m.sbuf("o", [P, D])
        xT = m.sbuf("xT", [P, KD, P])
        hT = m.sbuf("hT", [P, KI, P])
        y = m.sbuf("y", [P, D])
        missing = m.sbuf("missing", [P, NTT])
        px = m.psum("px", [P, KD, P])
        p1 = m.psum("p1", [P, KI, P])
        p2 = m.psum("p2", [P, D])
        w_in, t_in, t_st = m.sem("w_in"), m.sem("t_in"), m.sem("t_st")
        b1_mm, b1_done, xT_mm, xT_done, up_mm, up_done, y_mm, o_done, chain = (
            m.sem(s) for s in ("b1_mm", "b1", "xT_mm", "xT", "up_mm", "up", "y_mm", "o", "chain"))
        h_t = h2_rows
        out_t = out.rearrange("b (t p) d -> (b t) p d", p=P)
        block = ctx.enter_context(nc.Block())

        def overflowed(eng):
            return eng.If(eng.value_load(keep.flag[0:1, 0:1], min_val=0, max_val=NTOK) > 0)

        @block.sync
        def _(sp):
            with overflowed(sp):
                sp.dma_start(w1[:, :, :], fw1.rearrange("(k p) n -> p k n", p=P)).then_inc(w_in, 16)
                sp.dma_start(w2[:, :, :], fw2.rearrange("(m p) n -> p m n", p=P)).then_inc(w_in, 16)
                sp.dma_start(b1_rows[:, :], fb1.rearrange("(m p) -> m p", p=P)).then_inc(w_in, 16)
                sp.dma_start(b2[:, :], fb2[None, :].to_broadcast([P, D])).then_inc(w_in, 16)
                sp.sem_inc(t_st, 1)
                with sp.Fori(0, NTT) as n:
                    sp.wait_ge(t_st, n * 16 + 1)
                    sp.dma_start(x[:, :], h_t[n]).then_inc(t_in, 16)
                    sp.dma_start(o[:, :], out_t[n]).then_inc(t_in, 16)
                    sp.wait_ge(o_done, n + 1)
                    sp.dma_start(out_t[n], o[:, :]).then_inc(t_st, 16)
                sp.wait_ge(t_st, 1 + 16 * NTT)

        @block.scalar
        def _(act):
            with overflowed(act):
                act.wait_ge(b1_done, 1)
                with act.Fori(0, NTT) as n:
                    act.wait_ge(up_mm, n + 1)
                    for k in range(KI):
                        last = nc.scalar.activation(hT[:, k, :], p1[:, k, :], ACT.Gelu, bias=b1_cols[:, k:k + 1])
                    last.then_inc(up_done, 1)

        @block.vector
        def _(dve):
            with overflowed(dve):
                c = Chain(dve, chain)
                dve.wait_ge(b1_mm, 1)
                nc.vector.tensor_copy(b1_cols[:, :], px[:, 0, 0:KI]).then_inc(b1_done, 1)
                c.link(nc.vector.tensor_scalar(missing[:, :], keep.plain[:, :], -1.0, 1.0, ALU.mult, ALU.add))
                with dve.Fori(0, NTT) as n:
                    c = Chain(dve, chain, n * 3 + 1)
                    dve.wait_ge(xT_mm, n + 1)
                    nc.vector.tensor_copy(xT[:, :, :], px[:, :, :]).then_inc(xT_done, 1)
                    dve.wait_ge(y_mm, n + 1)
                    c.link(nc.vector.tensor_tensor(y[:, :], p2[:, :], b2[:, :], ALU.add))
                    c.link(nc.vector.tensor_scalar(y[:, :], y[:, :], missing[:, bass.ds(n, 1)], None, ALU.mult))
                    c.link(nc.vector.tensor_tensor(y[:, :], y[:, :], keep.mod[:, n // NT, 5, :], ALU.mult))
                    dve.wait_ge(t_in, n * 32 + 32)
                    nc.vector.tensor_tensor(o[:, :], o[:, :], y[:, :], ALU.add).then_inc(o_done, 1)

        @block.tensor
        def _(pe):
            with overflowed(pe):
                pe.wait_ge(w_in, 64)
                nc.tensor.transpose(px[:, 0, 0:KI], b1_rows[:, :], keep.ident[0:KI, 0:KI]).then_inc(b1_mm, 1)
                pe.wait_ge(b1_done, 1)
                with pe.Fori(0, NTT) as n:
                    pe.wait_ge(t_in, n * 32 + 32)
                    for k in range(KD):
                        last = nc.tensor.transpose(px[:, k, :], x[:, k * P:(k + 1) * P], keep.ident[:, :])
                    last.then_inc(xT_mm, 1)
                    pe.wait_ge(xT_done, n + 1)
                    for j in range(KI):
                        for k in range(KD):
                            last = nc.tensor.matmul(p1[:, j, :], w1[:, k, j * P:(j + 1) * P], xT[:, k, :], start=(k == 0), stop=(k == KD - 1))
                    last.then_inc(up_mm, 1)
                    pe.wait_ge(up_done, n + 1)
                    for j in range(KI):
                        last = nc.tensor.matmul(p2[:, :], hT[:, j, :], w2[:, j, :], start=(j == 0), stop=(j == KI - 1))
                    last.then_inc(y_mm, 1)


class Keep:
    pass


def build(nc, dr):
    with ExitStack() as ctx:
        keep = Keep()
        m = Program(nc, ctx, "keep")
        keep.weight = m.sbuf("weight", [P, 2, NTT])
        keep.into = m.sbuf("into", [P, NTT, 2], I32)
        keep.outof = m.sbuf("outof", [P, NTT, 2], I32)
        keep.plain = m.sbuf("plain", [P, NTT])
        keep.flag = m.sbuf("flag", [P, 1], I32)
        keep.ident = m.sbuf("ident", [P, P])
        keep.before = m.sbuf("before", [P, P])
        keep.mod = m.sbuf("mod", [P, B, 6, D])
        keep.sign = m.sbuf("sign", [P, D])
        keep.shift1 = m.sbuf("shift1", [P, B, KD])
        keep.scale1 = m.sbuf("scale1", [P, B, KD])
        keep.neg_half = m.sbuf("neg_half", [P, PAIRS, NT])
        keep.row_max = m.sbuf("row_max", [P, PAIRS, NT, 2])
        keep.logits = m.sbuf("logits", [P, NTT, E])
        scratch = lambda name, shape: nc.dram_tensor(name, shape, F32, kind="Internal").ap()
        q_rows = scratch("q_rows", (B, HEADS, HD, T))
        k_rows = scratch("k_rows", (B, KVH, HD, T))
        v_cent = scratch("v_cent", (B, KVH, P, NT, HD))
        gate_logit = scratch("gate_logit", (B, KVH, T))
        half_log = scratch("half_log", (PAIRS, T))
        x_slots = scratch("x_slots", (E * CAP, D))
        num_rows = scratch("num_rows", (PAIRS, P, T))
        constants(nc, keep, dr)
        modulation(nc, keep, dr["L0_c"], dr["L0_wmod"])
        project(nc, keep, dr["L0_attn_x"], dr["L0_attn_w_attn"], dr["rope"], q_rows, k_rows, v_cent, gate_logit)
        decays(nc, keep, gate_logit, half_log)
        attend(nc, keep, q_rows, k_rows, v_cent, half_log, num_rows, x_slots)
        keep.x1 = m.sbuf("x1", [P, NTT, D])
        h2_rows = scratch("h2_rows", (NTT, P, D))
        close_attention(nc, keep, dr["L0_attn_x"], dr["L0_attn_w_proj"], dr["L0_attn_ln_w"], dr["L0_ffn_Wr"], dr["fold"],
                        num_rows, h2_rows)
        y_slots = scratch("y_slots", (E * CAP, D))
        choose(nc, keep, dr["upto"], dr["experts"])
        dispatch(nc, keep, h2_rows, x_slots)
        experts(nc, keep, dr["L0_ffn_W1"], dr["L0_ffn_b1"], dr["L0_ffn_W2"], dr["L0_ffn_b2"], x_slots, y_slots)
        combine(nc, keep, y_slots, dr["out"])
        fall_back(nc, keep, dr["L0_ffn_fw1"], dr["L0_ffn_fb1"], dr["L0_ffn_fw2"], dr["L0_ffn_fb2"], h2_rows, dr["out"])


def constants(nc, keep, dr):
    with ExitStack() as ctx:
        m = Program(nc, ctx, "const")
        keep.passed = m.sem("passed")
        c_in = m.sem("in")
        block = ctx.enter_context(nc.Block())

        @block.sync
        def _(sp):
            sp.sem_inc(c_in, 16)
            sp.dma_start(keep.ident[:, :], dr["ident"]).then_inc(c_in, 16)
            sp.dma_start(keep.before[:, :], dr["before"]).then_inc(c_in, 16)
            sp.wait_ge(c_in, 48)


_INS = ['L0_attn_x', 'L0_attn_w_attn', 'L0_attn_w_proj', 'L0_attn_ln_w', 'L0_ffn_Wr', 'L0_ffn_W1', 'L0_ffn_b1',
        'L0_ffn_W2', 'L0_ffn_b2', 'L0_ffn_fw1', 'L0_ffn_fb1', 'L0_ffn_fw2', 'L0_ffn_fb2', 'L0_c', 'L0_wmod']


def shape_constants():
    import numpy as np
    div = (2.0 * np.pi / float(T) ** (np.arange(0, HD, 2, dtype=np.float32) / HD)).astype(np.float32)
    ang = (np.arange(T, dtype=np.float32)[:, None] * div[None, :]).astype(np.float64)
    cos = np.repeat(np.cos(ang), 2, axis=1)
    sin = np.repeat(np.sin(ang), 2, axis=1)
    sin[:, 0::2] *= -1.0
    scale = HD ** -0.5
    tab = np.stack([cos * scale, sin * scale, cos, sin]).astype(np.float32)
    rope = np.ascontiguousarray(tab.reshape(4, NT, P, HD).transpose(2, 0, 1, 3))
    r = np.arange(P)
    ch = P // PAIRS
    before = ((r[:, None] // ch == r[None, :] // ch) & (r[:, None] < r[None, :])).astype(np.float32)
    fold = np.eye(P, dtype=np.float32)
    for h in range(2):
        fold[h * HD + HD - 1, h * HD:(h + 1) * HD] -= 1.0
    upto = (r[:, None] <= r[None, :]).astype(np.float32)
    experts_row = np.ascontiguousarray(np.broadcast_to(np.arange(E, dtype=np.float32), (P, E)))
    return {"upto": upto, "experts": experts_row, "fold": fold, "rope": rope, "ident": np.eye(P, dtype=np.float32), "before": before}


def kernel(**inputs):
    import numpy as np
    import concourse.bacc as bacc
    from concourse.bass_utils import run_bass_kernel_spmd

    nc = bacc.Bacc("TRN2", target_bir_lowering=False, num_devices=1)
    arrays = {name: np.ascontiguousarray(inputs[name]) for name in _INS} | shape_constants()
    dr = {name: nc.dram_tensor(name, a.shape, mybir.dt.from_np(a.dtype), kind="ExternalInput").ap() for name, a in arrays.items()}
    dr["out"] = nc.dram_tensor("out", (B, T, D), F32, kind="ExternalOutput").ap()
    build(nc, dr)
    r = run_bass_kernel_spmd(nc, [arrays], core_ids=[0])
    return r.results[0]["out"]
```

```python
from contextlib import ExitStack

import concourse.bass as bass
from concourse import mybir
from concourse.alu_op_type import AluOpType as ALU

F32 = mybir.dt.float32
F32R = mybir.dt.float32r
U32 = mybir.dt.uint32
I32 = mybir.dt.int32
ACT = mybir.ActivationFunctionType
AX = mybir.AxisListType

P = 128
B, T, D = 2, 2048, 256
NTOK = B * T
NT = T // P
NTT = NTOK // P
KD = D // P
HEADS, KVH, HD = 16, 8, 64
QW, KW = HEADS * HD, KVH * HD
QKV = QW + 2 * KW
PAIRS = B * KVH
TB = 512
NB = T // TB
ST = TB // P
E, INNER, CAP = 8, 1024, 1280
KI = INNER // P
GATE_BIAS = 6.906768
LN_EPS = 1e-5
CREDIT = 16


def ready(k):
    return k + (CREDIT + 1)


def free(k, depth):
    return k + (CREDIT + 1 - depth)


class Program:

    def __init__(self, nc, ctx, tag):
        self.nc, self.ctx, self.tag, self.sems = nc, ctx, tag, []

    def sbuf(self, name, shape, dt=F32):
        return self.ctx.enter_context(self.nc.sbuf_tensor(f"{self.tag}_sb_{name}", shape, dt))

    def psum(self, name, shape, dt=F32):
        return self.ctx.enter_context(self.nc.psum_tensor(f"{self.tag}_ps_{name}", shape, dt))

    def sem(self, name):
        self.sems.append(self.nc.alloc_semaphore(f"{self.tag}_{name}"))
        return self.sems[-1]

    def give_back(self):
        def clear():
            with self.nc.Block() as block:
                @block.gpsimd
                def _(pool):
                    self.nc.clear_and_free_semaphores(self.sems)
        self.ctx.callback(clear)


def apart(eng, keep):
    eng.sem_inc(keep.passed, 1)


class Chain:

    def __init__(self, eng, sem, base=0):
        self.eng, self.sem, self.base, self.n = eng, sem, base, 0

    def link(self, ins):
        self.n += 1
        ins.then_inc(self.sem, 1)
        self.eng.wait_ge(self.sem, self.base + self.n)


def early_memory(nc, ctx):
    early = Keep()
    m = Program(nc, ctx, "early")
    early.w = m.sbuf("w", [P, KD, QKV + KVH])
    early.tab = m.sbuf("tab", [P, 4, NT, HD])
    early.basis = m.sbuf("basis", [P, P])
    early.xt = m.sbuf("xt", [P, 2, D])
    early.w_in = m.sem("w_in")
    early.x_in = [m.sem(f"x_in{i}") for i in range(2)]
    return early


def modulation(nc, keep, early, cond, wmod, x, w_attn, rope, basis):
    with ExitStack() as ctx:
        m = Program(nc, ctx, "mod")
        cT = m.sbuf("cT", [P, B, KD])
        sT = m.sbuf("sT", [P, B, KD])
        sB = m.sbuf("sB", [P, B, KD, P])
        w = m.sbuf("w", [P, KD, 6 * D])
        pr = [m.psum(f"pr{i}", [P, 512]) for i in range(6)]
        pc = m.psum("pc", [P, 2 * KD, B])
        sem_in, silu_done, bcast_done, rows_done, cols_done, copied, chain = (
            m.sem(x) for x in ("in", "silu", "bcast", "rows", "cols", "copied", "chain"))
        block = ctx.enter_context(nc.Block())

        @block.sync
        def _(sp):
            for b in range(B):
                for k in range(KD):
                    sp.dma_start(cT[:, b, k:k + 1], cond[b, k * P:(k + 1) * P].rearrange("(p o) -> p o", o=1)).then_inc(sem_in, 16)
            sp.dma_start(w[:, :, :], wmod.rearrange("(k p) n -> p k n", p=P)).then_inc(sem_in, 16)
            for i in range(2):
                sp.dma_start(early.xt[:, i, :], x[0, i * P:(i + 1) * P, :]).then_inc(early.x_in[i], 16)
            sp.dma_start(early.w[:, :, :], w_attn.rearrange("(k p) n -> p k n", p=P)).then_inc(early.w_in, 16)
            sp.dma_start(early.basis[:, :], basis).then_inc(early.w_in, 16)
            sp.dma_start(early.tab[:, :, :, :], rope).then_inc(early.w_in, 16)

        @block.scalar
        def _(act):
            act.wait_ge(sem_in, 16 * (B * KD + 1))
            nc.scalar.activation(sT[:, :, :], cT[:, :, :], ACT.Silu).then_inc(silu_done, 1)

        @block.tensor
        def _(pe):
            pe.wait_ge(sem_in, 16 * (B * KD + 1))
            pe.wait_ge(silu_done, 1)
            for mm in range(2 * KD):
                for k in range(KD):
                    last = nc.tensor.matmul(pc[:, mm, :], w[:, k, mm * P:(mm + 1) * P], sT[:, :, k],
                                            start=(k == 0), stop=(k == KD - 1))
            last.then_inc(cols_done, 1)
            pe.wait_ge(bcast_done, 1)
            for b in range(B):
                for n in range(3):
                    for k in range(KD):
                        last = nc.tensor.matmul(pr[b * 3 + n][:, :], sB[:, b, k, :], w[:, k, n * 512:(n + 1) * 512],
                                                start=(k == 0), stop=(k == KD - 1))
            last.then_inc(rows_done, 1)

        @block.vector
        def _(dve):
            c = Chain(dve, chain)
            dve.wait_ge(silu_done, 1)
            nc.vector.tensor_copy(sB[:, :, :, :], sT[:, :, :, None].to_broadcast([P, B, KD, P])).then_inc(bcast_done, 1)
            dve.wait_ge(cols_done, 1)
            nc.vector.tensor_copy(keep.shift1[:, :, :], pc[:, 0:KD, :].rearrange("p k b -> p b k"))
            nc.vector.tensor_scalar(keep.scale1[:, :, :], pc[:, KD:2 * KD, :].rearrange("p k b -> p b k"), 1.0, None, ALU.add)
            dve.wait_ge(rows_done, 1)
            for b in range(B):
                for n in range(3):
                    c.link(nc.vector.tensor_copy(keep.mod[:, b, 2 * n:2 * n + 2, :],
                                                 pr[b * 3 + n][:, :].rearrange("p (s d) -> p s d", s=2)))
            for b in range(B):
                c.link(nc.vector.tensor_scalar(keep.mod[:, b, 4, :], keep.mod[:, b, 4, :], 1.0, None, ALU.add))
                for g in (2, 5):
                    c.link(nc.vector.tensor_scalar(keep.sign[:, :], keep.mod[:, b, g, :], 0.0, 2.0, ALU.is_ge, ALU.mult))
                    c.link(nc.vector.scalar_tensor_tensor(keep.mod[:, b, g, :], keep.mod[:, b, g, :], -1.0, keep.mod[:, b, g, :],
                                                          ALU.mult, ALU.max))
                    c.link(nc.vector.tensor_scalar(keep.mod[:, b, g, :], keep.mod[:, b, g, :], 0.25, None, ALU.max))
                    c.link(nc.vector.scalar_tensor_tensor(keep.mod[:, b, g, :], keep.sign[:, :], -1.0, keep.mod[:, b, g, :],
                                                          ALU.add, ALU.mult))


def project(nc, keep, early, x, q_rows, k_rows, v_cent, gate_logit):
    with ExitStack() as ctx:
        m = Program(nc, ctx, "proj")
        m.give_back()
        w, tab, basis_sb, xt, w_in, x_in = early.w, early.tab, early.basis, early.xt, early.w_in, early.x_in
        w_hi = m.sbuf("w_hi", [P, KD, QKV], F32R)
        w_lo = m.sbuf("w_lo", [P, KD, QKV], F32R)
        wv_T = m.sbuf("wv_T", [P, KD, KW])
        st6 = m.sbuf("st6", [P, 6])
        mv = m.sbuf("mv", [P, 2, 2])
        rs = m.sbuf("rs", [P, 2, 2])
        xn = m.sbuf("xn", [P, 2, D])
        h = m.sbuf("h", [P, 2, KD, P])
        h_hi = m.sbuf("h_hi", [P, 2, KD, P], F32R)
        h_lo = m.sbuf("h_lo", [P, 2, KD, P], F32R)
        z = m.sbuf("z", [P, 3, KVH, HD])
        t1 = m.sbuf("t1", [P, 3, KVH, HD])
        t2 = m.sbuf("t2", [P, 3, KVH, HD])
        r = m.sbuf("r", [P, 3, KVH * HD])
        rT = m.sbuf("rT", [P, 3, 4, P])
        vt = m.sbuf("vt", [P, 2, KVH, HD])
        gs = m.sbuf("gs", [KVH, 2, P])
        eps = m.sbuf("eps", [P, 1])
        pc = [m.psum(f"pc{i}", [P, 512]) for i in range(4)]
        pr = [m.psum(f"pr{i}", [P, 4, P]) for i in range(2)]
        px = m.psum("px", [P, KD, P])
        pg = m.psum("pg", [KVH, P])
        wv_turned, wv_T_done, wv_mm, wv_done, w_hi_done, w_lo_done = (
            m.sem(s) for s in ("wv_turned", "wv_T", "wv_mm", "wv", "w_hi", "w_lo"))
        var_done, std_done, rstd_done, xn_done, xnT_done, h_done, h_hi_done, h_lo_done = (
            m.sem(s) for s in ("var", "std", "rstd", "xn", "xnT", "h", "h_hi", "h_lo"))
        gate_mm, gate_out = m.sem("gate_mm"), m.sem("gate_out")
        chunk_mm, z_done, t1_done, t2_done, kr_done, qr_done, rot_done, rT_done, v_done = (
            m.sem(s) for s in ("chunk", "z", "t1", "t2", "kr", "qr", "rot", "rT", "v"))
        r_st = [m.sem(f"r_st{i}") for i in range(3)]
        v_st = [m.sem(f"v_st{i}") for i in range(2)]
        g_st = [m.sem(f"g_st{i}") for i in range(2)]
        ones_done, st_done = m.sem("ones"), m.sem("st")
        cols = [QW, 0, 512, QW + KW]
        x_t = x.rearrange("b (t p) d -> (b t) p d", p=P)
        block = ctx.enter_context(nc.Block())

        def turns(eng, turn):
            for n in range(2):
                turn(n, n % 2, True, n > 0, True)
            with eng.Fori(1, NTT // 2 - 1) as it:
                for p in range(2):
                    turn(it * 2 + p, p, True, True, True)
            for n in range(NTT - 2, NTT + 1):
                turn(n, n % 2, n < NTT, True, n + 1 < NTT)

        @block.sync
        def _(sp):
            for s in r_st + v_st + g_st:
                sp.sem_inc(s, 1)

            def rows(n, c):
                b, t = n // NT, n % NT
                dst, h0 = (k_rows, 0) if c == 0 else (q_rows, 8 * (c - 1))
                sp.wait_ge(rT_done, ready(n * 3 + c))
                apart(sp, keep)
                sp.dma_start(dst[b, h0:h0 + 8, :, bass.ds(t * P, P)].rearrange("(c hh) d t -> (hh d) c t", hh=2),
                             rT[:, c, :, :]).then_inc(r_st[c], 16)

            def turn(n, p, this, before, after):
                if this:
                    sp.wait_ge(gate_out, ready(n))
                    apart(sp, keep)
                    sp.dma_start(gate_logit[n // NT, :, bass.ds(n % NT * P, P)], gs[:, p, :]).then_inc(g_st[p], 16)
                if before:
                    rows(n - 1, 1)
                    rows(n - 1, 2)
                if this:
                    sp.wait_ge(v_done, ready(n))
                    apart(sp, keep)
                    sp.dma_start(v_cent[n // NT, :, :, n % NT, :].rearrange("j p d -> p j d"), vt[:, p, :, :]).then_inc(v_st[p], 16)
                    rows(n, 0)

            turns(sp, turn)
            for c in range(3):
                sp.wait_ge(r_st[c], 1 + 16 * NTT)
            for i in range(2):
                sp.wait_ge(v_st[i], 1 + 16 * (NTT // 2))
                sp.wait_ge(g_st[i], 1 + 16 * (NTT // 2))

        @block.scalar
        def _(act):
            for s in (std_done, h_done, h_hi_done, gate_out, z_done, rT_done, v_done):
                act.sem_inc(s, CREDIT)
            def std(n, p):
                act.wait_ge(var_done, ready(n))
                nc.scalar.activation(rs[:, p, 0:1], mv[:, p, 1:2], ACT.Sqrt, bias=eps[:, :]).then_inc(std_done, 1)

            def modulate(n, p):
                act.wait_ge(xnT_done, ready(n))
                act.wait_ge(chunk_mm, n * 4 + (CREDIT + 1 - 5))
                act.wait_ge(h_lo_done, free(n, 2))
                apart(act, keep)
                for k in range(KD):
                    last = nc.scalar.activation(h[:, p, k, :], px[:, k, :], ACT.Identity,
                                                scale=keep.scale1[:, n // NT, k:k + 1], bias=keep.shift1[:, n // NT, k:k + 1])
                last.then_inc(h_done, 1)
                act.wait_ge(h_done, ready(n))
                nc.scalar.activation(h_hi[:, p, :, :], h[:, p, :, :], ACT.Copy).then_inc(h_hi_done, 1)

            def evacuate(n, c):
                act.wait_ge(chunk_mm, ready(n * 4 + c))
                act.wait_ge(t1_done, free(n * 3 + c, 3))
                act.wait_ge(t2_done, free(n * 3 + c, 3))
                nc.scalar.activation(z[:, c, :, :], pc[c][:, :].rearrange("p (h d) -> p h d", d=HD), ACT.Copy).then_inc(z_done, 1)

            def turned(n, p, c):
                act.wait_ge(rot_done, ready(n * 3 + c))
                act.wait_ge(r_st[c], n * 16 + 1)
                nc.scalar.activation(rT[:, c, :, :], pr[(p + c) % 2][:, :, :], ACT.Copy).then_inc(rT_done, 1)

            act.wait_ge(ones_done, 1)
            std(0, 0)
            act.wait_ge(w_in, 48)
            for c in range(4):
                if c == 2:
                    modulate(0, 0)
                if c == 3:
                    act.wait_ge(wv_done, 1)
                nc.scalar.activation(w_hi[:, :, cols[c]:cols[c] + 512], w[:, :, cols[c]:cols[c] + 512], ACT.Copy).then_inc(w_hi_done, 1)

            def turn(n, p, this, before, after):
                if this:
                    act.wait_ge(gate_mm, ready(n))
                    act.wait_ge(g_st[p], n // 2 * 16 + 1)
                    nc.scalar.activation(gs[:, p, :], pg[:, :], ACT.Copy).then_inc(gate_out, 1)
                    evacuate(n, 0)
                if after:
                    std(n + 1, 1 - p)
                if before:
                    turned(n - 1, 1 - p, 1)
                if this:
                    evacuate(n, 1)
                if before:
                    turned(n - 1, 1 - p, 2)
                if this:
                    act.wait_ge(xn_done, ready(n))
                    apart(act, keep)
                    act.dma_start(xt[:, p, :], x_t[(n + 2) % NTT]).then_inc(x_in[p], 16)
                    evacuate(n, 2)
                if after:
                    modulate(n + 1, 1 - p)
                if this:
                    act.wait_ge(chunk_mm, ready(n * 4 + 3))
                    act.wait_ge(v_st[p], n // 2 * 16 + 1)
                    nc.scalar.activation(vt[:, p, :, 0:HD - 1], pc[3][:, :].rearrange("p (h d) -> p h d", d=HD)[:, :, 0:HD - 1],
                                         ACT.Copy).then_inc(v_done, 1)
                    turned(n, p, 0)

            turns(act, turn)
            for i in range(2):
                act.wait_ge(x_in[i], 16 + 16 * (NTT // 2))

        @block.gpsimd
        def _(pool):
            for s in (t1_done, qr_done):
                pool.sem_inc(s, CREDIT)
            nc.gpsimd.memset(eps[:, :], LN_EPS)
            nc.gpsimd.memset(vt[:, :, :, HD - 1:HD], 1.0).then_inc(ones_done, 1)
            pool.wait_ge(w_in, 48)

            def cosine(n, c):
                k = n * 3 + c
                cos = tab[:, 2 if c == 0 else 0, n % NT, None, :].to_broadcast([P, KVH, HD])
                pool.wait_ge(z_done, ready(k))
                if c == 0:
                    pool.wait_ge(kr_done, free(n, 1))
                apart(pool, keep)
                nc.gpsimd.tensor_tensor(t1[:, c, :, :], z[:, c, :, :], cos, ALU.mult).then_inc(t1_done, 1)

            with pool.Fori(0, NTT) as n:
                cosine(n, 0)
                for c in range(1, 3):
                    k = n * 3 + c
                    cosine(n, c)
                    pool.wait_ge(t1_done, ready(k))
                    pool.wait_ge(t2_done, ready(k))
                    pool.wait_ge(rot_done, free(k, 3))
                    nc.gpsimd.tensor_tensor(r[:, c, :].rearrange("p (h d) -> p h d", d=HD), t1[:, c, :, :], t2[:, c, :, :],
                                            ALU.add).then_inc(qr_done, 1)

        @block.vector
        def _(dve):
            for s in (var_done, st_done, rstd_done, xn_done, t2_done, kr_done, h_lo_done):
                dve.sem_inc(s, CREDIT)
            def variance(n, p):
                dve.wait_ge(x_in[p], n // 2 * 16 + 16)
                nc.vector.bn_stats(st6[:, :], xt[:, p, :]).then_inc(st_done, 1)
                dve.wait_ge(st_done, ready(n))
                apart(dve, keep)
                nc.vector.bn_aggr(mv[:, p, :], st6[:, :]).then_inc(var_done, 1)

            def norm(n, p):
                dve.wait_ge(std_done, ready(n))
                nc.vector.reciprocal(rs[:, p, 1:2], rs[:, p, 0:1]).then_inc(rstd_done, 1)
                dve.wait_ge(rstd_done, ready(n))
                dve.wait_ge(xnT_done, free(n, 2))
                nc.vector.tensor_scalar(xn[:, p, :], xt[:, p, :], mv[:, p, 0:1], rs[:, p, 1:2],
                                        ALU.subtract, ALU.mult).then_inc(xn_done, 1)

            def rest(n, p):
                dve.wait_ge(h_hi_done, ready(n))
                nc.vector.tensor_tensor(h_lo[:, p, :, :], h[:, p, :, :], h_hi[:, p, :, :].bitcast(F32), ALU.subtract).then_inc(h_lo_done, 1)

            def sine(n, c):
                k = n * 3 + c
                sin = tab[:, 3 if c == 0 else 1, n % NT, :]
                dve.wait_ge(z_done, ready(k))
                if c:
                    dve.wait_ge(qr_done, free(n * 2 + c - 1, 2))
                else:
                    dve.wait_ge(kr_done, free(n, 1))
                nc.vector.tensor_tensor(t2[:, c, :, 0::2], z[:, c, :, 1::2],
                                        sin[:, None, 0::2].to_broadcast([P, KVH, HD // 2]), ALU.mult)
                nc.vector.tensor_tensor(t2[:, c, :, 1::2], z[:, c, :, 0::2],
                                        sin[:, None, 1::2].to_broadcast([P, KVH, HD // 2]), ALU.mult).then_inc(t2_done, 1)

            def weights_rest(c):
                dve.wait_ge(w_hi_done, c + 1)
                nc.vector.tensor_tensor(w_lo[:, :, cols[c]:cols[c] + 512], w[:, :, cols[c]:cols[c] + 512],
                                        w_hi[:, :, cols[c]:cols[c] + 512].bitcast(F32), ALU.subtract).then_inc(w_lo_done, 1)

            variance(0, 0)
            norm(0, 0)
            dve.wait_ge(wv_turned, 1)
            for k in range(KD):
                last = nc.vector.tensor_copy(wv_T[:, k, :], pc[k][:, :])
            last.then_inc(wv_T_done, 1)
            weights_rest(0)
            dve.wait_ge(wv_mm, 1)
            for k in range(KD):
                last = nc.vector.tensor_copy(w[:, k, QW + KW:QKV], pc[KD + k][:, :])
            last.then_inc(wv_done, 1)
            dve.wait_ge(wv_done, 1)
            rest(0, 0)
            for c in range(1, 4):
                weights_rest(c)

            def turn(n, p, this, before, after):
                if after:
                    variance(n + 1, 1 - p)
                if this:
                    sine(n, 0)
                if after:
                    norm(n + 1, 1 - p)
                if this:
                    sine(n, 1)
                    dve.wait_ge(t1_done, ready(n * 3))
                    dve.wait_ge(t2_done, ready(n * 3))
                    dve.wait_ge(rot_done, free(n * 3, 3))
                    nc.vector.tensor_tensor(r[:, 0, :].rearrange("p (h d) -> p h d", d=HD), t1[:, 0, :, :], t2[:, 0, :, :],
                                            ALU.add).then_inc(kr_done, 1)
                    sine(n, 2)
                if after:
                    rest(n + 1, 1 - p)

            turns(dve, turn)

        @block.tensor
        def _(pe):
            for s in (xnT_done, gate_mm, chunk_mm, rot_done):
                pe.sem_inc(s, CREDIT)
            pe.wait_ge(w_in, 48)
            for k in range(KD):
                for j in range(0, KW, P):
                    last = nc.tensor.transpose(pc[k][:, j:j + P], w[:, k, QW + KW + j:QW + KW + j + P], keep.ident[:, :])
            last.then_inc(wv_turned, 1)
            def transpose_in(n, p):
                pe.wait_ge(xn_done, ready(n))
                pe.wait_ge(h_done, free(n, 1))
                for k in range(KD):
                    last = nc.tensor.transpose(px[:, k, :], xn[:, p, k * P:(k + 1) * P], keep.ident[:, :])
                last.then_inc(xnT_done, 1)

            def chunk(n, p, c, first):
                if first:
                    pe.wait_ge(w_lo_done, c + 1)
                if c < 3:
                    pe.wait_ge(z_done, free(n * 3 + c, 3))
                else:
                    pe.wait_ge(v_done, free(n, 1))
                at = slice(cols[c], cols[c] + 512)
                terms = [(a, b, k) for a, b in ((h_hi, w_hi), (h_lo, w_hi), (h_hi, w_lo)) for k in range(KD)]
                for i, (a, b, k) in enumerate(terms):
                    last = nc.tensor.matmul(pc[c][:, :], a[:, p, k, :], b[:, k, at], start=(i == 0), stop=(i == len(terms) - 1))
                last.then_inc(chunk_mm, 1)

            def rotated(n, p, c):
                if c:
                    pe.wait_ge(qr_done, ready(n * 2 + c - 1))
                else:
                    pe.wait_ge(kr_done, ready(n))
                pe.wait_ge(rT_done, free(n * 3 + c, 2))
                for j in range(4):
                    last = nc.tensor.transpose(pr[(p + c) % 2][:, j, :], r[:, c, j * P:(j + 1) * P], keep.ident[:, :])
                last.then_inc(rot_done, 1)

            transpose_in(0, 0)
            pe.wait_ge(wv_T_done, 1)
            for k in range(KD):
                for j in range(0, KW, P):
                    last = nc.tensor.matmul(pc[KD + k][:, j:j + P], wv_T[:, k, j:j + P], basis_sb[:, :], start=True, stop=True)
            last.then_inc(wv_mm, 1)

            def turn(n, p, this, before, after):
                if this:
                    pe.wait_ge(h_lo_done, ready(n))
                    pe.wait_ge(gate_out, free(n, 1))
                    for k in range(KD):
                        last = nc.tensor.matmul(pg[:, :], w[:, k, QKV:QKV + KVH], h[:, p, k, :], start=(k == 0), stop=(k == KD - 1))
                    last.then_inc(gate_mm, 1)
                    chunk(n, p, 0, not before)
                if before:
                    rotated(n - 1, 1 - p, 1)
                if this:
                    chunk(n, p, 1, not before)
                if before:
                    rotated(n - 1, 1 - p, 2)
                if this:
                    chunk(n, p, 2, not before)
                if after:
                    transpose_in(n + 1, 1 - p)
                if this:
                    chunk(n, p, 3, not before)
                    rotated(n, p, 0)

            turns(pe, turn)


def decays(nc, keep, gate_logit, half_log):
    CH = P // PAIRS
    CL = T // CH
    with ExitStack() as ctx:
        m = Program(nc, ctx, "dec")
        names = ("x", "mag", "e", "w", "lnw", "u", "sc")
        g = {s: m.sbuf(s, [P, CL]) for s in names}
        inv = m.sbuf("inv", [P, CL])
        one = m.sbuf("one", [P, CL])
        tot = m.sbuf("tot", [P, 1])
        pt = m.psum("pt", [P, 1])
        pn = [m.psum(f"pn{i}", [P, P]) for i in range(CL // P)]
        x_in, mag_done, e_done, w_done, ln_done, scan_done, carry_mm, sum_done, turned, stored, chain = (
            m.sem(s) for s in ("x_in", "mag", "e", "w", "ln", "scan", "carry", "sum", "turned", "stored", "chain"))
        block = ctx.enter_context(nc.Block())

        @block.sync
        def _(sp):
            sp.dma_start(g["x"][:, :], gate_logit.rearrange("b h (c t) -> (b h c) t", t=CL)).then_inc(x_in, 16)
            sp.wait_ge(sum_done, 1)
            sp.dma_start(half_log.rearrange("r (c t) -> (r c) t", t=CL), g["sc"][:, :]).then_inc(stored, 16)
            sp.wait_ge(stored, 16)

        @block.scalar
        def _(act):
            act.wait_ge(mag_done, 1)
            nc.scalar.activation(g["e"][:, :], g["mag"][:, :], ACT.Exp, scale=-1.0).then_inc(e_done, 1)
            act.wait_ge(w_done, 1)
            nc.scalar.activation(g["lnw"][:, :], g["w"][:, :], ACT.Ln).then_inc(ln_done, 1)
            act.wait_ge(turned, 1)
            for i in range(CL // P):
                nc.scalar.activation(keep.neg_half[:, :, i::CL // P],
                                     pn[i][:, :].rearrange("p (r c) -> p r c", r=PAIRS), ACT.Copy, scale=-1.0)

        @block.vector
        def _(dve):
            c = Chain(dve, chain)
            c.link(nc.vector.memset(one[:, :], 1.0))
            dve.wait_ge(x_in, 16)
            c.link(nc.vector.tensor_scalar(g["x"][:, :], g["x"][:, :], GATE_BIAS, None, ALU.add))
            nc.vector.scalar_tensor_tensor(g["mag"][:, :], g["x"][:, :], -1.0, g["x"][:, :], ALU.mult, ALU.max).then_inc(mag_done, 1)
            dve.wait_ge(e_done, 1)
            nc.vector.tensor_scalar(g["w"][:, :], g["e"][:, :], 1.0, None, ALU.add).then_inc(w_done, 1)
            dve.wait_ge(w_done, 1)
            c.link(nc.vector.reciprocal(inv[:, :], g["w"][:, :]))
            c.link(nc.vector.scalar_tensor_tensor(g["u"][:, :], g["w"][:, :], -1.0, g["e"][:, :], ALU.add, ALU.subtract))
            c.link(nc.vector.tensor_tensor(g["u"][:, :], g["u"][:, :], inv[:, :], ALU.mult))
            dve.wait_ge(ln_done, 1)
            c.link(nc.vector.tensor_tensor(g["u"][:, :], g["u"][:, :], g["lnw"][:, :], ALU.subtract))
            c.link(nc.vector.scalar_tensor_tensor(g["u"][:, :], g["x"][:, :], 0.0, g["u"][:, :], ALU.min, ALU.add))
            c.link(nc.vector.tensor_scalar(g["u"][:, :], g["u"][:, :], 0.5, None, ALU.mult))
            c.link(nc.vector.tensor_tensor_scan(g["mag"][:, :], one[:, :], g["u"][:, :], 0.0, ALU.mult, ALU.add))
            nc.vector.tensor_copy(tot[:, :], g["mag"][:, CL - 1:CL]).then_inc(scan_done, 1)
            dve.wait_ge(carry_mm, 1)
            c.link(nc.vector.tensor_copy(tot[:, :], pt[:, :]))
            nc.vector.tensor_scalar(g["sc"][:, :], g["mag"][:, :], tot[:, :], None, ALU.add).then_inc(sum_done, 1)

        @block.tensor
        def _(pe):
            pe.wait_ge(scan_done, 1)
            nc.tensor.matmul(pt[:, :], keep.before[:, :], tot[:, :], start=True, stop=True).then_inc(carry_mm, 1)
            pe.wait_ge(sum_done, 1)
            for i in range(CL // P):
                last = nc.tensor.transpose(pn[i][:, :], g["sc"][:, i * P:(i + 1) * P], keep.ident[:, :])
            last.then_inc(turned, 1)


LATE = (2, 1)
M0 = 4
RING_A, LAG, ROWS, TOTAL = 8, 6.5, 0.6, 0.1
GUARD = 1e-15


def attention_steps():
    off = {i: [("off", i, s) for s in range(ST * i)] for i in range(1, NB)}
    diag = {i: [("diag", i, j) for j in range(ST)] for i in range(NB)}
    steps = []
    for n, st in enumerate(off[3]):
        if n in (1, 4):
            steps.append(("max", LATE[n // 4], 0))
        steps.append(st)
        if n in (5, 7, 9, 11):
            steps.append(diag[0][(n - 5) // 2])
    for n, st in enumerate(off[2]):
        steps.append(st)
        if 2 <= n < 2 + ST:
            steps.append(diag[3][n - 2])
        if n == M0:
            steps.append(("max", 0, 0))
    for n, st in enumerate(off[1]):
        steps.append(st)
        steps.append(diag[2][n])
        if n == 1:
            steps.append(("max", 3, 0))
    return steps + diag[1]


def attend(nc, keep, q_rows, k_rows, v_cent, half_log, num_rows, x_slots):
    steps = attention_steps()
    N = len(steps)
    squares = [n for n in range(N) if steps[n][0] != "max"]
    diags = [n for n in range(N) if steps[n][0] == "diag"]
    maxes = [n for n in range(N) if steps[n][0] == "max"]
    sq_of = {n: g for g, n in enumerate(squares)}
    mul_of = {n: d for d, n in enumerate(diags)}
    m_of = {n: r for r, n in enumerate(maxes)}
    NS, ND = len(squares), len(diags)

    AHEAD = 3

    def due(n):
        kind, _, j = steps[n]
        return min(n + (AHEAD + 0.5 if kind == "off" else LAG), N + AHEAD - 0.7)

    use_order = sorted(squares, key=lambda n: (due(n), n))
    use_of = {n: u for u, n in enumerate(use_order)}
    done_order = (0, 3, 2, 1)
    done_of = {i: d for d, i in enumerate(done_order)}
    last_off = {i: n for n in range(N) for k, i, _ in [steps[n]] if k == "off"}
    last_use = {i: n for n in use_order for k, i, _ in [steps[n]]}
    max_step = {steps[n][1]: n for n in maxes}
    after = {n: [] for n in range(N)}
    at = {st: n for n, st in enumerate(steps)}
    QCH = 1024
    QCN, KCN = 2 * T // QCH, 2
    for j in range(ST):
        after[at["off", 3, 1 + j]].append(("decay", 0, j))
        after[at[("off", 3, 6 + 2 * j) if j < 3 else ("off", 2, 1)]].append(("decay", 3, j))
        after[at["off", 2, 4 + j]].append(("decay", 2, j))
        after[at[("off", 1, 1 + j) if j < 3 else ("diag", 2, 3)]].append(("decay", 1, j))
    for c in range(KCN):
        after[at["off", 3, 9 + 2 * c]].append(("split_k", c))
    for c in range(QCN):
        after[at["off", 2, c]].append(("split_q", c))
    after[at["off", 1, 3]].append(("factors",))
    A, R, SR = RING_A, 3, 3
    HI, LO = QCN + KCN, QCN + KCN
    decay_base = {0: 0, 3: ST, 2: 2 * ST, 1: 3 * ST}
    assert N % 2 == 0 and NS % A == 0 and list(decay_base) == list(done_order)
    assert all(sq_of[n] < sq_of[k] for n, k in zip(diags, diags[1:]))

    def et_slot(i, p):
        return (NB - 1 - i + p) % 2

    def slot(n):
        return n % SR

    def slot_before(n):
        return (n - SR, 0) if n >= SR else (max(k for k in range(N) if slot(k) == slot(n)), 1)

    def own_slot(i):
        return done_of[i] % 2

    def acc_slot(i, p):
        return {3: (0, 0), 0: (1, 2), 2: (2, 1), 1: (1, 2)}[i][p]

    with ExitStack() as ctx:
        m = Program(nc, ctx, "att")
        q_sb = [m.sbuf(f"q{i}", [P, 2 * T]) for i in range(2)]
        k_sb = [m.sbuf(f"k{i}", [P, 2, T]) for i in range(2)]
        v_sb = [m.sbuf(f"v{i}", [P, NT, HD]) for i in range(2)]
        hb = [m.sbuf(f"hb{i}", [P, T]) for i in range(2)]
        nh = m.sbuf("nh", [P, 2, NT])
        nfull = m.sbuf("nfull", [P, 2, NT])
        f = m.sbuf("f", [P, 2, NB - 1, NT - ST])
        fg = m.sbuf("fg", [P, 2, NB - 1, NT - ST])
        neg2 = m.sbuf("neg2", [P, 2, NB])
        guard = m.sbuf("guard", [P, 1])
        head = m.sbuf("head", [P, 2, QCH], F32R)
        et = m.sbuf("et", [P, 2, TB])
        dec = m.sbuf("dec", [P, 2, ST, TB])
        a = m.sbuf("a", [P, A, 2, TB])
        acc = m.sbuf("acc", [P, R, 2, TB])
        part = m.sbuf("part", [P, 2, TB])
        num = m.sbuf("num", [P, 2, TB])
        zero = m.sbuf("zero", [P, D])
        s_ps = [m.psum(f"s{i}", [P, 2, TB]) for i in range(SR)]
        off_ps = m.psum("off", [P, TB])
        own_ps = m.psum("own", [P, TB])
        zero_done, zero_st, guard_done = m.sem("zero"), m.sem("zero_st"), m.sem("guard")
        pair_in = [m.sem(f"pair_in{i}") for i in range(2)]
        num_st = [m.sem(f"num_st{i}") for i in range(2)]
        up_done, hi_done, lo_done, prep_done, et_done, exp_done, dec_done = (m.sem(s) for s in ("up", "hi", "lo", "prep", "et", "exp", "dec"))
        s_done, sq_done, mul_done, av_done, max_done, row_done, num_done, scaled, part_done = (
            m.sem(s) for s in ("s", "sq", "mul", "av", "max", "row", "num", "scaled", "part"))
        block = ctx.enter_context(nc.Block())

        @block.sync
        def _(sp):
            for i in range(2):
                sp.sem_inc(num_st[i], 1)

            def load(q, p):
                b, j = q // KVH, q % KVH
                for half in range(2):
                    at = slice(half * HD, (half + 1) * HD)
                    sp.dma_start(q_sb[p][at, :].rearrange("d (h t) -> d h t", h=2),
                                 q_rows[b, bass.ds(j * 2, 2), :, :].rearrange("h d t -> d h t")).then_inc(pair_in[p], 16)
                    sp.dma_start(k_sb[p][at, 1, :], k_rows[b, j, :, :]).then_inc(pair_in[p], 16)
                sp.dma_start(v_sb[p][:, :, :], v_cent[b, j, :, :, :]).then_inc(pair_in[p], 16)
                sp.dma_start(hb[p][:, :], half_log[q, None, :].to_broadcast([P, T])).then_inc(pair_in[p], 16)

            load(0, 0)
            sp.wait_ge(zero_done, 1)
            slots = x_slots.rearrange("(r p) d -> r p d", p=P)
            with sp.Fori(0, E * CAP // P // 8) as r:
                sp.dma_start(slots[bass.ds(r * 8, 8)].rearrange("r p d -> p r d"),
                             zero[:, None, :].to_broadcast([P, 8, D])).then_inc(zero_st, 16)
            with sp.Fori(0, PAIRS // 2) as it:
                for p in range(2):
                    q = it * 2 + p
                    sp.wait_ge(av_done, ready(q * NS - 1))
                    sp.wait_ge(lo_done, ready(q * LO + LO - 1))
                    apart(sp, keep)
                    load((q + 1) % PAIRS, 1 - p)
                    for d, i in enumerate(done_order):
                        sp.wait_ge(num_done, ready(q * NB + d))
                        apart(sp, keep)
                        sp.dma_start(num_rows[q, :, i * TB:(i + 1) * TB], num[:, d % 2, :]).then_inc(num_st[d % 2], 16)
            for i in range(2):
                sp.wait_ge(num_st[i], 1 + 16 * PAIRS * NB // 2)
            sp.wait_ge(zero_st, 16 * (E * CAP // P // 8))

        def queries(p, c):
            return q_sb[p][:, c * QCH:(c + 1) * QCH]

        def keys(p, hl, c):
            return k_sb[p][:, hl, c * (T // KCN):(c + 1) * (T // KCN)]

        def split_up(q, p, what, c):
            if what == "split_q":
                nc.scalar.wait_ge(lo_done, ready(q * LO + KCN + c - 2 if c >= 2 else (q - 1) * LO + KCN + QCN - 2 + c))
                nc.scalar.activation(head[HD:P, c % 2, :], queries(p, c)[HD:P, :], ACT.Copy).then_inc(up_done, 1)

        def split_hi(q, p, what, c):
            if what == "split_k":
                nc.vector.tensor_copy(keys(p, 0, c).bitcast(F32R), keys(p, 1, c)).then_inc(hi_done, 1)
            else:
                nc.vector.tensor_copy(queries(p, c)[0:HD, :].bitcast(F32R), queries(p, c)[0:HD, :]).then_inc(hi_done, 1)

        def split_lo(q, p, what, c):
            if what == "split_k":
                nc.gpsimd.wait_ge(hi_done, ready(q * HI + c))
                nc.gpsimd.tensor_tensor(keys(p, 1, c).bitcast(F32R), keys(p, 1, c), keys(p, 0, c), ALU.subtract).then_inc(lo_done, 1)
            else:
                nc.gpsimd.wait_ge(hi_done, ready(q * HI + KCN + c))
                nc.gpsimd.wait_ge(up_done, ready(q * QCN + c))
                nc.gpsimd.tensor_tensor(queries(p, c).bitcast(F32R), queries(p, c), head[:, c % 2, :].bitcast(F32),
                                        ALU.subtract).then_inc(lo_done, 1)

        parts = [("split_k", c) for c in range(KCN)] + [("split_q", c) for c in range(QCN)]

        @block.gpsimd
        def _(pool):
            for s in (dec_done, mul_done, lo_done):
                pool.sem_inc(s, CREDIT)
            nc.gpsimd.memset(head[:, :, :].bitcast(F32), 0.0)
            nc.gpsimd.memset(guard[:, :], GUARD).then_inc(guard_done, 1)
            nc.gpsimd.memset(zero[:, :], 0.0).then_inc(zero_done, 1)

            def mask(q, i, j):
                pool.wait_ge(exp_done, ready(q * ND + decay_base[i] + j))
                apart(pool, keep)
                tile = dec[:, own_slot(i), j, 0:P]
                nc.gpsimd.affine_select(out=tile, in_=tile, compare_op=ALU.is_ge, fill=0.0, base=0,
                                        pattern=[[1, P]], channel_multiplier=-1).then_inc(dec_done, 1)

            pool.wait_ge(pair_in[0], 96)
            for what in parts:
                split_lo(0, 0, *what)
            with pool.Fori(0, PAIRS // 2) as it:
                for p in range(2):
                    q = it * 2 + p
                    for n in range(N):
                        kind, i, j = steps[n]
                        if kind == "diag":
                            g = sq_of[n]
                            pool.wait_ge(dec_done, ready(q * ND + decay_base[i] + j))
                            pool.wait_ge(sq_done, ready(q * NS + g))
                            x = a[:, g % A, :, j * P:TB]
                            nc.gpsimd.tensor_tensor(x, x, dec[:, own_slot(i), j, None, 0:TB - j * P].to_broadcast([P, 2, TB - j * P]),
                                                    ALU.mult).then_inc(mul_done, 1)
                        for what in after[n]:
                            if what[0] == "decay":
                                mask(q, *what[1:])
                            elif what in parts:
                                split_lo(q + 1, 1 - p, *what)

        @block.scalar
        def _(act):
            for s in (up_done, prep_done, et_done, exp_done, sq_done):
                act.sem_inc(s, CREDIT)

            def factors(q, p):
                k = q % PAIRS
                nc.scalar.activation(nh[:, p, :], keep.neg_half[:, k, :], ACT.Copy)
                nc.scalar.activation(nfull[:, p, :], keep.neg_half[:, k, :], ACT.Copy, scale=2.0).then_inc(prep_done, 1)
                act.wait_ge(prep_done, ready(q * 3))
                for i in range(1, NB):
                    last = nc.scalar.activation(f[:, p, i - 1, 0:ST * i], nh[:, p, 0:ST * i], ACT.Exp,
                                                bias=hb[p][:, i * TB:i * TB + 1])
                last.then_inc(prep_done, 1)
                act.wait_ge(prep_done, ready(q * 3 + 1))
                for i in range(1, NB):
                    nc.scalar.activation(fg[:, p, i - 1, 0:ST * i], f[:, p, i - 1, 0:ST * i], ACT.Copy, scale=GUARD)
                nc.scalar.activation(neg2[:, p, :], hb[p][:, 0::TB], ACT.Copy, scale=-2.0).then_inc(prep_done, 1)

            def query_factor(q, p, i):
                act.wait_ge(prep_done, ready(q * 3 + 2))
                act.wait_ge(part_done, free(q * (NB - 1) + NB - 1 - i + 1, 2))
                act.wait_ge(scaled, free(q * (NB - 1) + NB - 1 - i, 2))
                nc.scalar.activation(et[:, et_slot(i, p), :], hb[p][:, i * TB:(i + 1) * TB], ACT.Exp, scale=2.0,
                                     bias=neg2[:, p, i:i + 1]).then_inc(et_done, 1)

            def decay(q, p, i, j):
                d = decay_base[i]
                if j == 0:
                    act.wait_ge(mul_done, ready(q * ND + d - ST - 1))
                w = TB - j * P
                nc.scalar.activation(dec[:, own_slot(i), j, 0:w], hb[p][:, i * TB + j * P:(i + 1) * TB], ACT.Exp,
                                     scale=2.0, bias=nfull[:, p, i * ST + j:i * ST + j + 1]).then_inc(exp_done, 1)

            act.wait_ge(guard_done, 1)
            act.wait_ge(pair_in[0], 96)
            for what in parts:
                split_up(0, 0, *what)
            factors(0, 0)
            act.wait_ge(prep_done, ready(2))
            with act.Fori(0, PAIRS // 2) as it:
                for p in range(2):
                    q = it * 2 + p
                    for n in range(N):
                        kind, i, s = steps[n]
                        if kind != "max":
                            g = sq_of[n]
                            last = use_of[squares[(g - A) % NS]] + (q if g >= A else q - 1) * NS
                            act.wait_ge(av_done, ready(last))
                            act.wait_ge(max_done, ready(last))
                            act.wait_ge(s_done, ready(q * N + n))
                            if kind == "off":
                                nc.scalar.activation(a[:, g % A, :, :], s_ps[slot(n)][:, :, :], ACT.Square,
                                                     scale=f[:, p, i - 1, s:s + 1], bias=fg[:, p, i - 1, s:s + 1]).then_inc(sq_done, 1)
                                if s == 0:
                                    query_factor(q, p, i)
                            else:
                                nc.scalar.activation(a[:, g % A, :, s * P:TB], s_ps[slot(n)][:, :, s * P:TB], ACT.Square,
                                                     bias=guard[:, :]).then_inc(sq_done, 1)
                        for what in after[n]:
                            if what[0] == "decay":
                                decay(q, p, *what[1:])
                            elif what[0] == "factors":
                                factors(q + 1, 1 - p)
                                act.wait_ge(prep_done, ready((q + 1) * 3 + 2))
                            elif what in parts:
                                if what == parts[0]:
                                    act.wait_ge(pair_in[1 - p], it * 96 + 96 * (1 + p))
                                split_up(q + 1, 1 - p, *what)

        @block.vector
        def _(dve):
            for s in (hi_done, max_done, row_done, num_done, scaled, part_done):
                dve.sem_inc(s, CREDIT)
            for i in range(R):
                last = nc.vector.memset(acc[:, i, :, :], 0.0)
            last.then_inc(part_done, 1)
            dve.wait_ge(part_done, CREDIT + 1)
            dve.wait_ge(pair_in[0], 96)
            for what in parts:
                split_hi(0, 0, *what)

            def maximum(q, p, n):
                kind, i, s = steps[n]
                g, u = sq_of[n], use_of[n]
                if kind == "off":
                    dve.wait_ge(sq_done, ready(q * NS + g))
                else:
                    dve.wait_ge(mul_done, ready(q * ND + mul_of[n]))
                x = acc[:, acc_slot(i, p), :, :]
                c = s * P if kind == "diag" else 0
                if s == 0 and (kind == "off" or i == 0):
                    nc.vector.tensor_copy(x, a[:, g % A, :, :]).then_inc(max_done, 1)
                else:
                    before = max(use_of[k] for k in squares if steps[k][1] == i and use_of[k] < u)
                    dve.wait_ge(max_done, ready(q * NS + before))
                    if kind == "diag" and s == 0:
                        dve.wait_ge(scaled, ready(q * (NB - 1) + NB - 1 - i))
                    nc.vector.tensor_tensor(x[:, :, c:TB], x[:, :, c:TB], a[:, g % A, :, c:TB], ALU.max).then_inc(max_done, 1)
                if last_off.get(i) == n:
                    dve.wait_ge(max_done, ready(q * NS + u))
                    dve.wait_ge(et_done, ready(q * (NB - 1) + NB - 1 - i))
                    nc.vector.tensor_tensor(x, x, et[:, et_slot(i, p), None, :].to_broadcast([P, 2, TB]), ALU.mult).then_inc(scaled, 1)

            def before_own(q, p, i):
                dve.wait_ge(av_done, ready(q * NS + use_of[last_off[i]]))
                dve.wait_ge(et_done, ready(q * (NB - 1) + NB - 1 - i))
                dve.wait_ge(num_done, ready((q * NB + done_of[i] - 2) if done_of[i] > 1 else (q - 1) * NB + 2))
                nc.vector.tensor_tensor(part[:, et_slot(i, p), :], off_ps[:, :], et[:, et_slot(i, p), :], ALU.mult).then_inc(part_done, 1)

            def total(q, p, i):
                d = done_of[i]
                dve.wait_ge(av_done, ready(q * NS + use_of[last_use[i]]))
                dve.wait_ge(num_st[d % 2], (q * (NB // 2) + d // 2) * 16 + 1)
                if i == 0:
                    nc.vector.tensor_copy(num[:, d % 2, :], own_ps[:, :]).then_inc(num_done, 1)
                else:
                    dve.wait_ge(part_done, ready(q * (NB - 1) + d))
                    nc.vector.tensor_tensor(num[:, d % 2, :], part[:, et_slot(i, p), :], own_ps[:, :], ALU.add).then_inc(num_done, 1)

            def rows(q, n, pair):
                i = steps[n][1]
                dve.wait_ge(s_done, ready(q * N + n))
                apart(dve, keep)
                nc.vector.tensor_reduce(keep.row_max[:, pair, i * ST:(i + 1) * ST, :].rearrange("p c h -> p h c"),
                                        s_ps[slot(n)][:, :, :].rearrange("p h (c k) -> p h c k", k=P), AX.X, ALU.max).then_inc(row_done, 1)

            todo = [(due(n), 0, n) for n in use_order]
            todo += [(due(last_use[i]) + TOTAL, 1, i) for i in range(NB)]
            todo += [(due(last_off[i]) + 0.05, 4, i) for i in range(1, NB)]
            todo += [(n + ROWS, 2, n) for n in maxes]
            todo += [(n + 1.4, 3, what) for n in range(N) for what in after[n] if what in parts]
            todo.sort()
            with dve.Fori(0, PAIRS // 2) as it:
                for p in range(2):
                    q = it * 2 + p
                    for _, what, x in todo:
                        if what == 0:
                            maximum(q, p, x)
                        elif what == 1:
                            total(q, p, x)
                        elif what == 4:
                            before_own(q, p, x)
                        elif what == 3:
                            if x == parts[0]:
                                dve.wait_ge(pair_in[1 - p], it * 96 + 96 * (1 + p))
                            split_hi(q + 1, 1 - p, *x)
                        else:
                            rows(q, x, (q + PAIRS - 1) % PAIRS if steps[x][1] in LATE else q)
            for k, i in enumerate(LATE):
                dve.wait_ge(s_done, ready(PAIRS * N + AHEAD + k))
                nc.vector.tensor_reduce(keep.row_max[:, PAIRS - 1, i * ST:(i + 1) * ST, :].rearrange("p c h -> p h c"),
                                        s_ps[k][:, :, :].rearrange("p h (c k) -> p h c k", k=P), AX.X, ALU.max).then_inc(row_done, 1)

        @block.tensor
        def _(pe):
            for s in (s_done, av_done):
                pe.sem_inc(s, CREDIT)
            pe.wait_ge(part_done, CREDIT + 1)

            def turn_maxima(s, ring):
                for h in range(2):
                    for c in range(ST):
                        last = nc.tensor.transpose(s_ps[s][:, h, c * P:(c + 1) * P],
                                                   acc[:, ring, h, c * P:(c + 1) * P], keep.ident[:, :])
                last.then_inc(s_done, 1)

            def scores(q, p, n):
                kind, i, s = steps[n]
                k, back = slot_before(n)
                if steps[k][0] == "max":
                    pe.wait_ge(row_done, ready((q - back) * NB + m_of[k]))
                else:
                    pe.wait_ge(sq_done, ready((q - back) * NS + sq_of[k]))
                if kind == "max":
                    if i in LATE:
                        pe.wait_ge(max_done, ready((q - 1) * NS + use_of[last_use[i]]))
                        turn_maxima(slot(n), acc_slot(i, 1 - p))
                    else:
                        pe.wait_ge(max_done, ready(q * NS + use_of[last_use[i]]))
                        turn_maxima(slot(n), acc_slot(i, p))
                    return
                if n == 0:
                    pe.wait_ge(lo_done, ready(q * LO + LO - 1))
                key = s if kind == "off" else i * ST + s
                c = 0 if kind == "off" else s * P
                for h in range(2):
                    for hl in range(2):
                        last = nc.tensor.matmul(s_ps[slot(n)][:, h, c:TB],
                                                k_sb[p][:, hl, key * P:(key + 1) * P].bitcast(F32R),
                                                q_sb[p][:, h * T + i * TB + c:h * T + (i + 1) * TB].bitcast(F32R),
                                                start=(hl == 0), stop=(hl == 1))
                last.then_inc(s_done, 1)

            def values(q, p, n):
                kind, i, s = steps[n]
                g = sq_of[n]
                key = s if kind == "off" else i * ST + s
                c = 0 if kind == "off" else s * P
                if s == 0:
                    if kind == "diag":
                        pe.wait_ge(num_done, free(q * NB + done_of[i], 1))
                    else:
                        pe.wait_ge(part_done, free(q * (NB - 1) + done_of[i], 1))
                if kind == "off":
                    pe.wait_ge(sq_done, ready(q * NS + g))
                else:
                    pe.wait_ge(mul_done, ready(q * ND + mul_of[n]))
                ps = off_ps if kind == "off" else own_ps
                for h in range(2):
                    last = nc.tensor.matmul(ps[h * HD:(h + 1) * HD, c:TB], v_sb[p][:, key, :], a[:, g % A, h, c:TB],
                                            start=(s == 0), stop=(s == (ST * i if kind == "off" else ST) - 1))
                last.then_inc(av_done, 1)

            todo = [(n, 0, n) for n in range(AHEAD, N)] + [(N + n, 1, n) for n in range(AHEAD)]
            todo += [(due(n), 2, n) for n in use_order]
            todo.sort()
            assert todo[0][1] == 0 or todo[0][0] > AHEAD - 1
            for n in range(AHEAD):
                scores(0, 0, n)
            with pe.Fori(0, PAIRS // 2) as it:
                for p in range(2):
                    q = it * 2 + p
                    for _, what, n in todo:
                        if what == 0:
                            scores(q, p, n)
                        elif what == 1:
                            scores(q + 1, 1 - p, n)
                        else:
                            values(q, p, n)
            pe.wait_ge(max_done, ready(PAIRS * NS - 1))
            for k, i in enumerate(LATE):
                turn_maxima(k, acc_slot(i, 1))


def close_attention(nc, keep, x, w_proj, ln_w, w_router, basis, num_rows, h2_rows):
    with ExitStack() as ctx:
        m = Program(nc, ctx, "close")
        w_raw = m.sbuf("w_raw", [P, KVH, D])
        w = m.sbuf("w", [P, KVH, D])
        basis_sb = m.sbuf("basis", [P, P])
        lnw = m.sbuf("lnw", [P, 1])
        wr = m.sbuf("wr", [P, KD, E])
        wr_raw = m.sbuf("wr_raw", [E, D])
        nT = m.sbuf("nT", [P, 2, KVH, P])
        xt = m.sbuf("xt", [P, 2, D])
        num = m.sbuf("num", [P, 2, HEADS, HD])
        sq = m.sbuf("sq", [P, HEADS, HD - 1])
        red = m.sbuf("red", [P, 5, HEADS])
        rinv = m.sbuf("rinv", [P, 2, HEADS])
        y = m.sbuf("y", [P, 2, HEADS, HD])
        yT = m.sbuf("yT", [P, 2, KVH, P])
        gx = m.sbuf("gx", [P, 2, D])
        st6 = m.sbuf("st6", [P, 6])
        mv = m.sbuf("mv", [P, 2, 2])
        rs = m.sbuf("rs", [P, 2, 2])
        xn = m.sbuf("xn", [P, 2, D])
        hs = m.sbuf("hs", [P, 2, D])
        h_st = m.sbuf("h_st", [P, 2, D])
        hT = m.sbuf("hT", [P, 2, KD, P])
        eps = m.sbuf("eps", [P, 1])
        pn = m.psum("pn", [P, HEADS, HD])
        py = m.psum("py", [P, KVH, P])
        pa = m.psum("pa", [P, D])
        ph = m.psum("ph", [P, KD, P])
        pl = m.psum("pl", [P, E])
        pw = m.psum("pw", [P, 2, D])
        w_in, scaled, fold_mm, folded, wr_mm, wr_done, eps_done = (
            m.sem(s) for s in ("w_in", "scaled", "fold_mm", "folded", "wr_mm", "wr", "eps"))
        n_in = [m.sem(f"n_in{i}") for i in range(2)]
        x_in = [m.sem(f"x_in{i}") for i in range(2)]
        h_out = [m.sem(f"h_out{i}") for i in range(2)]
        n_mm, num_done, sq_done, var_done, std_done, r_done, y_done, y_mm, yT_done, a_mm = (
            m.sem(s) for s in ("n_mm", "num", "sq", "var", "std", "r", "y", "y_mm", "yT", "a_mm"))
        gx_done, x1_done, var2_done, std2_done, xn_done, hs_done, h2_done, h_mm, hT_done, l_mm, l_done, head_chain, norm_chain = (
            m.sem(s) for s in ("gx", "x1", "var2", "std2", "xn", "hs", "h2", "h_mm", "hT", "l_mm", "l", "head_chain", "norm_chain"))
        x_t = x.rearrange("b (t p) d -> (b t) p d", p=P)
        num_t = num_rows.rearrange("(b j) p (t c) -> b t p j c", j=KVH, c=P)
        block = ctx.enter_context(nc.Block())

        def turns(eng, turn):
            LAST = 6
            for n in range(LAST):
                turn(n, n % 2, [n >= lag for lag in range(LAST + 1)])
            with eng.Fori(LAST // 2, NTT // 2) as it:
                for p in range(2):
                    turn(it * 2 + p, p, [True] * (LAST + 1))
            for n in range(NTT, NTT + LAST):
                turn(n, n % 2, [n - lag < NTT for lag in range(LAST + 1)])

        @block.sync
        def _(sp):
            sp.dma_start(w_raw[:, :, :], w_proj.rearrange("(j p) n -> p j n", p=P)).then_inc(w_in, 16)
            sp.dma_start(basis_sb[:, :], basis).then_inc(w_in, 16)
            for h in range(2):
                sp.dma_start(lnw[h * HD:(h + 1) * HD, :], ln_w.rearrange("(d o) -> d o", o=1)).then_inc(w_in, 16)
            sp.dma_start(wr_raw[:, :], w_router).then_inc(w_in, 16)
            for p in range(2):
                sp.sem_inc(h_out[p], 1)
                sp.sem_inc(n_in[p], 1)
                sp.sem_inc(x_in[p], 1)
                sp.dma_start(nT[:, p, :, :], num_t[0, p]).then_inc(n_in[p], 16)
                sp.dma_start(xt[:, p, :], x_t[p]).then_inc(x_in[p], 16)

            def turn(n, p, there):
                if there[0]:
                    m_ = (n + 2) % NTT
                    sp.wait_ge(n_mm, ready(n))
                    apart(sp, keep)
                    sp.dma_start(nT[:, p, :, :], num_t[m_ // NT, m_ % NT]).then_inc(n_in[p], 16)
                if there[5]:
                    sp.wait_ge(h2_done, ready(n - 5))
                    apart(sp, keep)
                    sp.dma_start(h2_rows[n - 5], h_st[:, 1 - p, :]).then_inc(h_out[1 - p], 16)
                if there[3]:
                    sp.wait_ge(x1_done, ready(n - 3))
                    apart(sp, keep)
                    sp.dma_start(xt[:, 1 - p, :], x_t[(n - 1) % NTT]).then_inc(x_in[1 - p], 16)

            turns(sp, turn)
            for p in range(2):
                sp.wait_ge(h_out[p], 1 + 16 * (NTT // 2))
                sp.wait_ge(n_in[p], 1 + 16 * (NTT // 2 + 1))
                sp.wait_ge(x_in[p], 1 + 16 * (NTT // 2 + 1))

        @block.scalar
        def _(act):
            for s in (sq_done, std_done, yT_done, std2_done, hT_done):
                act.sem_inc(s, CREDIT)
            act.wait_ge(eps_done, 1)

            def turn(n, p, there):
                if there[2]:
                    act.wait_ge(y_mm, ready(n - 2))
                    act.wait_ge(a_mm, free(n - 2, 2))
                    nc.scalar.activation(yT[:, p, :, :], py[:, :, :], ACT.Copy).then_inc(yT_done, 1)
                if there[0]:
                    act.wait_ge(num_done, ready(n))
                    act.wait_ge(var_done, free(n, 1))
                    nc.scalar.activation(sq[:, :, :], num[:, p, :, 0:HD - 1], ACT.Square).then_inc(sq_done, 1)
                if there[5]:
                    act.wait_ge(var2_done, ready(n - 5))
                    nc.scalar.activation(rs[:, 1 - p, 0:1], mv[:, 1 - p, 1:2], ACT.Sqrt, bias=eps[:, 0:1]).then_inc(std2_done, 1)
                if there[6]:
                    act.wait_ge(h_mm, ready(n - 6))
                    act.wait_ge(l_mm, free(n - 6, 2))
                    nc.scalar.activation(hT[:, p, :, :], ph[:, :, :], ACT.Copy).then_inc(hT_done, 1)
                if there[0]:
                    act.wait_ge(var_done, ready(n))
                    nc.scalar.activation(red[:, 4, :], red[:, 3, :], ACT.Sqrt).then_inc(std_done, 1)

            turns(act, turn)

        @block.gpsimd
        def _(pool):
            for s in (y_done, x1_done, hs_done, h2_done):
                pool.sem_inc(s, CREDIT)
            nc.gpsimd.memset(eps[:, 0:1], LN_EPS).then_inc(eps_done, 1)

            def turn(n, p, there):
                if there[5]:
                    b = (n - 5) // NT
                    pool.wait_ge(xn_done, ready(n - 5))
                    apart(pool, keep)
                    nc.gpsimd.tensor_tensor(hs[:, 1 - p, :], xn[:, 1 - p, :], keep.mod[:, b, 4, :], ALU.mult).then_inc(hs_done, 1)
                    pool.wait_ge(hs_done, ready(n - 5))
                    pool.wait_ge(h_mm, free(n - 5, 2))
                    pool.wait_ge(h_out[1 - p], (n - 5) // 2 * 16 + 1)
                    apart(pool, keep)
                    nc.gpsimd.tensor_tensor(h_st[:, 1 - p, :], hs[:, 1 - p, :], keep.mod[:, b, 3, :], ALU.add).then_inc(h2_done, 1)
                if there[0]:
                    pool.wait_ge(r_done, ready(n))
                    pool.wait_ge(y_mm, free(n, 2))
                    nc.gpsimd.tensor_tensor(y[:, p, :, :], num[:, p, :, :], rinv[:, p, :, None].to_broadcast([P, HEADS, HD]),
                                            ALU.mult).then_inc(y_done, 1)
                if there[3]:
                    pool.wait_ge(x_in[1 - p], (n - 3) // 2 * 16 + 17)
                    pool.wait_ge(gx_done, ready(n - 3))
                    apart(pool, keep)
                    nc.gpsimd.tensor_tensor(keep.x1[:, n - 3, :], xt[:, 1 - p, :], gx[:, 1 - p, :], ALU.add).then_inc(x1_done, 1)

            turns(pool, turn)

        @block.vector
        def _(dve):
            for s in (num_done, var_done, r_done, gx_done, var2_done, xn_done, l_done):
                dve.sem_inc(s, CREDIT)
            dve.wait_ge(w_in, 80)
            nc.vector.tensor_scalar(w_raw[:, :, :], w_raw[:, :, :], lnw[:, :], None, ALU.mult).then_inc(scaled, 1)
            for g in range(KVH // 2):
                dve.wait_ge(fold_mm, g + 1)
                nc.vector.tensor_copy(w[:, 2 * g:2 * g + 2, :], pw[:, :, :]).then_inc(folded, 1)
            dve.wait_ge(wr_mm, 1)
            nc.vector.tensor_copy(wr[:, :, :], ph[:, :, 0:E]).then_inc(wr_done, 1)
            HEAD_OPS, NORM_OPS = 3, 2

            def turn(n, p, there):
                head = Chain(dve, head_chain, n * HEAD_OPS)
                norm = Chain(dve, norm_chain, (n - 5) * NORM_OPS)
                if there[0]:
                    b, t = n // NT, n % NT
                    row_max = keep.row_max[:, bass.ds(b * KVH, KVH), t, :]
                    dve.wait_ge(n_mm, ready(n))
                    apart(dve, keep)
                    head.link(nc.vector.scalar_tensor_tensor(red[:, 0, :].rearrange("p (j h) -> p j h", h=2), row_max, 1e-6,
                                                             pn[:, :, HD - 1].rearrange("p (j h) -> p j h", h=2), ALU.mult, ALU.add))
                    head.link(nc.vector.reciprocal(red[:, 1, :], red[:, 0, :]))
                    dve.wait_ge(y_done, free(n, 2))
                    nc.vector.tensor_tensor(num[:, p, :, :], pn[:, :, :], red[:, 1, :, None].to_broadcast([P, HEADS, HD]),
                                            ALU.mult).then_inc(num_done, 1)
                if there[5]:
                    dve.wait_ge(x1_done, ready(n - 5))
                    apart(dve, keep)
                    norm.link(nc.vector.bn_stats(st6[:, :], keep.x1[:, n - 5, :]))
                    apart(dve, keep)
                    nc.vector.bn_aggr(mv[:, 1 - p, :], st6[:, :]).then_inc(var2_done, 1)
                if there[0]:
                    dve.wait_ge(sq_done, ready(n))
                    head.link(nc.vector.reduce_sum(red[:, 2, :], sq[:, :, :], AX.X))
                    nc.vector.tensor_scalar(red[:, 3, :], red[:, 2, :], 1.0 / HD, 1e-9, ALU.mult, ALU.add).then_inc(var_done, 1)
                    assert head.n == HEAD_OPS
                if there[5]:
                    dve.wait_ge(std2_done, ready(n - 5))
                    norm.link(nc.vector.reciprocal(rs[:, 1 - p, 1:2], rs[:, 1 - p, 0:1]))
                    dve.wait_ge(hs_done, free(n - 5, 2))
                    apart(dve, keep)
                    nc.vector.tensor_scalar(xn[:, 1 - p, :], keep.x1[:, n - 5, :], mv[:, 1 - p, 0:1], rs[:, 1 - p, 1:2],
                                            ALU.subtract, ALU.mult).then_inc(xn_done, 1)
                    assert norm.n == NORM_OPS
                if there[0]:
                    dve.wait_ge(std_done, ready(n))
                    nc.vector.reciprocal(rinv[:, p, :], red[:, 4, :]).then_inc(r_done, 1)
                if there[3]:
                    dve.wait_ge(a_mm, ready(n - 3))
                    dve.wait_ge(x1_done, free(n - 3, 2))
                    apart(dve, keep)
                    nc.vector.tensor_tensor(gx[:, 1 - p, :], pa[:, :], keep.mod[:, (n - 3) // NT, 2, :], ALU.mult).then_inc(gx_done, 1)
                if there[6]:
                    dve.wait_ge(l_mm, ready(n - 6))
                    apart(dve, keep)
                    nc.vector.tensor_copy(keep.logits[:, n - 6, :], pl[:, :]).then_inc(l_done, 1)

            turns(dve, turn)

        @block.tensor
        def _(pe):
            for s in (n_mm, y_mm, a_mm, h_mm, l_mm):
                pe.sem_inc(s, CREDIT)
            pe.wait_ge(w_in, 80)
            pe.wait_ge(scaled, 1)
            for g in range(KVH // 2):
                if g:
                    pe.wait_ge(folded, g)
                for i in range(2):
                    last = nc.tensor.matmul(pw[:, i, :], basis_sb[:, :], w_raw[:, 2 * g + i, :], start=True, stop=True)
                last.then_inc(fold_mm, 1)
            for k in range(KD):
                last = nc.tensor.transpose(ph[:, k, 0:E], wr_raw[:, k * P:(k + 1) * P], keep.ident[0:E, 0:E])
            last.then_inc(wr_mm, 1)
            pe.wait_ge(folded, KVH // 2)
            pe.wait_ge(wr_done, 1)

            def turn(n, p, there):
                if there[0]:
                    pe.wait_ge(n_in[p], n // 2 * 16 + 17)
                    pe.wait_ge(num_done, free(n, 1))
                    for j in range(KVH):
                        last = nc.tensor.transpose(pn[:, 2 * j:2 * j + 2, :], nT[:, p, j, :], keep.ident[:, :])
                    last.then_inc(n_mm, 1)
                if there[2]:
                    pe.wait_ge(y_done, ready(n - 2))
                    pe.wait_ge(yT_done, free(n - 2, 1))
                    for j in range(KVH):
                        last = nc.tensor.transpose(py[:, j, :], y[:, p, 2 * j:2 * j + 2, :], keep.ident[:, :])
                    last.then_inc(y_mm, 1)
                if there[6]:
                    pe.wait_ge(h2_done, ready(n - 6))
                    pe.wait_ge(hT_done, free(n - 6, 1))
                    for k in range(KD):
                        last = nc.tensor.transpose(ph[:, k, :], h_st[:, p, k * P:(k + 1) * P], keep.ident[:, :])
                    last.then_inc(h_mm, 1)
                if there[3]:
                    pe.wait_ge(yT_done, ready(n - 3))
                    pe.wait_ge(gx_done, free(n - 3, 1))
                    for j in range(KVH):
                        last = nc.tensor.matmul(pa[:, :], yT[:, 1 - p, j, :], w[:, j, :], start=(j == 0), stop=(j == KVH - 1))
                    last.then_inc(a_mm, 1)
                if there[6]:
                    pe.wait_ge(hT_done, ready(n - 6))
                    pe.wait_ge(l_done, free(n - 6, 1))
                    for k in range(KD):
                        last = nc.tensor.matmul(pl[:, :], hT[:, p, k, :], wr[:, k, :], start=(k == 0), stop=(k == KD - 1))
                    last.then_inc(l_mm, 1)

            turns(pe, turn)


def choose(nc, keep, upto, experts_row):
    SH = [P, NTT, E]
    FAR = float(1 << 20)
    with ExitStack() as ctx:
        m = Program(nc, ctx, "choose")
        tri = m.sbuf("tri", [P, P])
        ones = m.sbuf("ones", [P, P])
        er = m.sbuf("er", [P, E])
        ex = m.sbuf("ex", SH)
        pr = m.sbuf("pr", SH)
        tmp = m.sbuf("tmp", SH)
        hot = [m.sbuf(f"hot{i}", SH) for i in range(2)]
        match = m.sbuf("match", SH)
        kept = m.sbuf("kept", SH)
        place = m.sbuf("place", SH)
        r = {x: m.sbuf(x, [P, NTT]) for x in ("mx", "sum", "inv", "best", "s0", "s1", "elig", "run", "pos", "over", "keptk", "placek", "one")}
        lost = m.sbuf("lost", [P, 1])
        pos_ps = m.psum("pos", [P, NTT])
        tot_ps = m.psum("tot", [P, NTT])
        cnt_ps = m.psum("cnt", [P, 1])
        c_in, diff_done, exp_done, elig_done, count_mm, lost_done, lost_mm, chain = (
            m.sem(s) for s in ("in", "diff", "exp", "elig", "count", "lost", "lost_mm", "chain"))
        block = ctx.enter_context(nc.Block())

        @block.sync
        def _(sp):
            sp.dma_start(tri[:, :], upto).then_inc(c_in, 16)
            sp.dma_start(er[:, :], experts_row).then_inc(c_in, 16)

        @block.scalar
        def _(act):
            act.wait_ge(diff_done, 1)
            nc.scalar.activation(ex[:, :, :], tmp[:, :, :], ACT.Exp).then_inc(exp_done, 1)

        @block.tensor
        def _(pe):
            pe.wait_ge(c_in, 32)
            for e in range(E):
                pe.wait_ge(elig_done, e + 1)
                nc.tensor.matmul(pos_ps[:, :], tri[:, :], r["elig"][:, :], start=True, stop=True)
                nc.tensor.matmul(tot_ps[:, :], ones[:, :], r["elig"][:, :], start=True, stop=True).then_inc(count_mm, 1)
            pe.wait_ge(lost_done, 1)
            nc.tensor.matmul(cnt_ps[:, :], ones[:, :], lost[:, :], start=True, stop=True).then_inc(lost_mm, 1)

        @block.vector
        def _(dve):
            c = Chain(dve, chain)
            v = nc.vector

            def wide(x):
                return x[:, :, None].to_broadcast(SH)

            c.link(v.memset(ones[:, :], 1.0))
            c.link(v.memset(r["one"][:, :], 1.0))
            c.link(v.memset(keep.plain[:, :], 1.0))
            c.link(v.tensor_reduce(r["mx"][:, :], keep.logits[:, :, :], AX.X, ALU.max))
            v.tensor_tensor(tmp[:, :, :], keep.logits[:, :, :], wide(r["mx"]), ALU.subtract).then_inc(diff_done, 1)
            dve.wait_ge(exp_done, 1)
            c.link(v.reduce_sum(r["sum"][:, :], ex[:, :, :], AX.X))
            c.link(v.reciprocal(r["inv"][:, :], r["sum"][:, :]))
            c.link(v.tensor_tensor(pr[:, :, :], ex[:, :, :], wide(r["inv"]), ALU.mult))
            dve.wait_ge(c_in, 32)
            lane = er[:, None, :].to_broadcast(SH)
            for k in range(2):
                s = r["s0"] if k == 0 else r["s1"]
                c.link(v.tensor_reduce(s[:, :], pr[:, :, :], AX.X, ALU.max))
                c.link(v.tensor_tensor(tmp[:, :, :], pr[:, :, :], wide(s), ALU.is_equal))
                c.link(v.scalar_tensor_tensor(tmp[:, :, :], lane, -float(E), tmp[:, :, :], ALU.add, ALU.mult))
                c.link(v.tensor_reduce(r["best"][:, :], tmp[:, :, :], AX.X, ALU.min))
                c.link(v.tensor_scalar(r["best"][:, :], r["best"][:, :], float(E), None, ALU.add))
                c.link(v.tensor_tensor(hot[k][:, :, :], lane, wide(r["best"]), ALU.is_equal))
                if k == 0:
                    c.link(v.tensor_scalar(tmp[:, :, :], hot[0][:, :, :], -1.0, 1.0, ALU.mult, ALU.add))
                    c.link(v.tensor_tensor(pr[:, :, :], pr[:, :, :], tmp[:, :, :], ALU.mult))
                    c.link(v.tensor_tensor(pr[:, :, :], pr[:, :, :], hot[0][:, :, :], ALU.subtract))
            c.link(v.tensor_tensor(match[:, :, :], hot[0][:, :, :], hot[1][:, :, :], ALU.add))
            c.link(v.tensor_tensor(r["sum"][:, :], r["s0"][:, :], r["s1"][:, :], ALU.add))
            c.link(v.tensor_scalar(r["sum"][:, :], r["sum"][:, :], 1e-9, None, ALU.max))
            c.link(v.reciprocal(r["inv"][:, :], r["sum"][:, :]))
            for s in ("s0", "s1"):
                c.link(v.tensor_tensor(r[s][:, :], r[s][:, :], r["inv"][:, :], ALU.mult))
            for e in range(E):
                v.tensor_tensor(r["elig"][:, :], match[:, :, e], keep.plain[:, :], ALU.mult).then_inc(elig_done, 1)
                dve.wait_ge(count_mm, e + 1)
                c.link(v.tensor_tensor_scan(r["run"][:, :], r["one"][:, :], tot_ps[:, :], 0.0, ALU.mult, ALU.add))
                c.link(v.tensor_tensor(r["run"][:, :], r["run"][:, :], tot_ps[:, :], ALU.subtract))
                c.link(v.scalar_tensor_tensor(r["pos"][:, :], pos_ps[:, :], -1.0, r["run"][:, :], ALU.add, ALU.add))
                c.link(v.scalar_tensor_tensor(kept[:, :, e], r["pos"][:, :], float(CAP), r["elig"][:, :], ALU.is_lt, ALU.mult))
                c.link(v.tensor_scalar(place[:, :, e], r["pos"][:, :], float(e * CAP), None, ALU.add))
                c.link(v.tensor_tensor(r["over"][:, :], r["elig"][:, :], kept[:, :, e], ALU.subtract))
                c.link(v.tensor_tensor(keep.plain[:, :], keep.plain[:, :], r["over"][:, :], ALU.subtract))
            for k in range(2):
                c.link(v.tensor_tensor(tmp[:, :, :], hot[k][:, :, :], kept[:, :, :], ALU.mult))
                c.link(v.reduce_sum(r["keptk"][:, :], tmp[:, :, :], AX.X))
                c.link(v.tensor_tensor(tmp[:, :, :], tmp[:, :, :], place[:, :, :], ALU.mult))
                c.link(v.reduce_sum(r["placek"][:, :], tmp[:, :, :], AX.X))
                c.link(v.tensor_copy(keep.outof[:, :, k], r["placek"][:, :]))
                c.link(v.tensor_scalar(r["pos"][:, :], r["keptk"][:, :], -FAR, FAR, ALU.mult, ALU.add))
                c.link(v.tensor_tensor(keep.into[:, :, k], r["placek"][:, :], r["pos"][:, :], ALU.add))
                c.link(v.tensor_tensor(r["keptk"][:, :], r["keptk"][:, :], keep.plain[:, :], ALU.mult))
                c.link(v.tensor_tensor(keep.weight[:, k, :], r["keptk"][:, :], r["s0" if k == 0 else "s1"][:, :], ALU.mult))
            c.link(v.tensor_scalar(r["over"][:, :], keep.plain[:, :], -1.0, 1.0, ALU.mult, ALU.add))
            v.reduce_sum(lost[:, :], r["over"][:, :], AX.X).then_inc(lost_done, 1)
            dve.wait_ge(lost_mm, 1)
            c.link(v.tensor_copy(keep.flag[:, :], cnt_ps[:, :]))


def experts(nc, keep, w1, b1, w2, b2, h2_rows, x_slots, y_slots):
    XT = CAP // P
    GT = 2
    NG, W = XT // GT, GT * P
    RING = 4
    SENT = 8
    CUT = 1024
    with ExitStack() as ctx:
        m = Program(nc, ctx, "ffn")
        w_hi = [[m.sbuf(f"w{k}_hi{i}", [P, KD * INNER], F32R) for k in (1, 2)] for i in range(2)]
        w_lo = [[m.sbuf(f"w{k}_lo{i}", [P, KD * INNER], F32R) for k in (1, 2)] for i in range(2)]
        raw = [m.sbuf(f"raw{i}", [P, CUT]) for i in range(2)]
        b1_rows = m.sbuf("b1_rows", [E * KI, P])
        b1_cols = m.sbuf("b1_cols", [P, E * KI])
        b2_sb = [m.sbuf(f"b2_{i}", [P, D]) for i in range(2)]
        xs = [m.sbuf(f"xs{i}", [P, XT, D]) for i in range(2)]
        x_hi = m.sbuf("x_hi", [P, 2, KD, W], F32R)
        x_lo = m.sbuf("x_lo", [P, 2, KD, W], F32R)
        h = m.sbuf("h", [P, RING, W])
        h_hi = m.sbuf("h_hi", [P, 2, KI, W], F32R)
        h_lo = m.sbuf("h_lo", [P, 2, KI, W], F32R)
        ys = m.sbuf("ys", [P, 2, D])
        row = [m.sbuf(f"row{i}", [P, D]) for i in range(SENT)]
        idx = [[m.sbuf(f"idx{i}_{k}", [P, 1], I32) for k in range(2)] for i in range(SENT)]
        px = [m.psum(f"px{i}", [P, KD, P]) for i in range(2)]
        p1 = [m.psum(f"p1_{i}", [P, W]) for i in range(RING)]
        p2 = [m.psum(f"p2_{i}", [P, D]) for i in range(2)]
        row_in = [m.sem(f"row_in{i}") for i in range(SENT)]
        sent = [m.sem(f"sent{i}") for i in range(SENT)]
        idx_done = m.sem("idx")
        raw_in = [m.sem(f"raw_in{i}") for i in range(2)]
        x_in = [m.sem(f"x_in{i}") for i in range(2)]
        y_st = [m.sem(f"y_st{i}") for i in range(2)]
        b1_in, b1_mm, b1_done = m.sem("b1_in"), m.sem("b1_mm"), m.sem("b1")
        w_hi_done, w_lo_done, xT_mm, x_hi_done, x_lo_done, up_mm, up_done, h_hi_done, h_lo_done, y_mm, y_done = (
            m.sem(s) for s in ("w_hi", "w_lo", "xT_mm", "x_hi", "x_lo", "up_mm", "up", "h_hi", "h_lo", "y_mm", "y"))
        cuts = [(k, slice(c, c + CUT)) for k in range(2) for c in range(0, KD * INNER, CUT)]
        NC = len(cuts)
        block = ctx.enter_context(nc.Block())

        def groups(p):
            return [(p * NG + g, p, g) for g in range(NG)]

        @block.sync
        def _(sp):
            for i in range(2):
                sp.sem_inc(y_st[i], 1)

            def load(e, p):
                sp.dma_start(b2_sb[p][:, :], b2[e, None, :].to_broadcast([P, D])).then_inc(x_in[p], 16)
                sp.dma_start(xs[p][:, :, :], x_slots[bass.ds(e * CAP, CAP), :].rearrange("(t p) d -> p t d", p=P)).then_inc(x_in[p], 16)

            for i in range(SENT):
                sp.dma_start(row[i][:, :], h2_rows[i]).then_inc(row_in[i], 16)
            sp.dma_start(b1_rows[:, :], b1.rearrange("e (m p) -> (e m) p", p=P)).then_inc(b1_in, 16)
            with sp.Fori(1, NTT // SENT) as it:
                for i in range(SENT):
                    sp.wait_ge(sent[i], it * 32)
                    sp.dma_start(row[i][:, :], h2_rows[it * SENT + i]).then_inc(row_in[i], 16)
            for i in range(SENT):
                sp.wait_ge(sent[i], 32 * (NTT // SENT))
            load(0, 0)
            with sp.Fori(0, E // 2) as it:
                for p in range(2):
                    e = it * 2 + p
                    sp.wait_ge(y_done, ready(e * XT - 1))
                    apart(sp, keep)
                    load((e + 1) % E, 1 - p)
                    for t in range(XT):
                        sp.wait_ge(y_done, ready(e * XT + t))
                        apart(sp, keep)
                        sp.dma_start(y_slots[bass.ds(e * CAP + t * P, P), :], ys[:, t % 2, :]).then_inc(y_st[t % 2], 16)
            for i in range(2):
                sp.wait_ge(y_st[i], 1 + 16 * E * XT // 2)
            sp.wait_ge(x_in[0], 32 * (E // 2 + 1))

        @block.gpsimd
        def _(pool):
            with pool.Fori(0, NTT // SENT) as it:
                for i in range(SENT):
                    pool.wait_ge(row_in[i], it * 16 + 16)
                    pool.wait_ge(idx_done, ready(it * SENT + i))
                    apart(pool, keep)
                    for k in range(2):
                        nc.gpsimd.indirect_dma_start(x_slots, bass.IndirectOffsetOnAxis(ap=idx[i][k][:, :].bitcast(U32), axis=0),
                                                     row[i][:, :], None, bounds_check=E * CAP - 1,
                                                     oob_is_err=False).then_inc(sent[i], 16)
            with pool.Fori(0, E // 2) as it:
                for p in range(2):
                    e = it * 2 + p + 1
                    for c, (k, at) in enumerate(cuts):
                        pool.wait_ge(w_hi_done, ready(e * NC + c))
                        nc.gpsimd.tensor_tensor(w_lo[1 - p][k][:, at], raw[c % 2][:, :], w_hi[1 - p][k][:, at].bitcast(F32),
                                                ALU.subtract).then_inc(w_lo_done, 1)

        @block.scalar
        def _(act):
            act.sem_inc(up_done, CREDIT)
            act.sem_inc(w_hi_done, CREDIT)

            def fetch(e, c):
                k, at = cuts[c]
                src = w1 if k == 0 else w2
                n = CUT // (INNER if k == 0 else D)
                i = at.start // CUT * n
                act.wait_ge(w_lo_done, ready(e * NC + c - 2))
                apart(act, keep)
                act.dma_start(raw[c % 2][:, :].rearrange("p (k n) -> p k n", k=n),
                              src[e % E].rearrange("(k p) n -> p k n", p=P)[:, i:i + n, :]).then_inc(raw_in[c % 2], 16)

            def round_off(p, c, arrived):
                k, at = cuts[c]
                act.wait_ge(raw_in[c % 2], arrived)
                nc.scalar.activation(w_hi[p][k][:, at], raw[c % 2][:, :], ACT.Copy).then_inc(w_hi_done, 1)

            assert NC == 4
            for c in (0, 2):
                for i in (c, c + 1):
                    fetch(0, i)
                for i in (c, c + 1):
                    round_off(0, i, c * 8 + 16)
            act.wait_ge(b1_done, 1)
            with act.Fori(0, E // 2) as it:
                for p in range(2):
                    e = it * 2 + p
                    for G, _, g in groups(p):
                        for k in range(KI):
                            u = (e * NG + g) * KI + k
                            act.wait_ge(up_mm, ready(u))
                            act.wait_ge(h_lo_done, free(u, RING))
                            apart(act, keep)
                            nc.scalar.activation(h[:, (G * KI + k) % RING, :], p1[(G * KI + k) % RING][:, :], ACT.Gelu,
                                                 bias=b1_cols[:, bass.ds(e * KI + k, 1)]).then_inc(up_done, 1)
                        for c in ((0, 1), (), (2, 3), ())[g % 4] if g < 4 else ():
                            fetch(e + 1, c)
                        for c in ((), (0, 1), (), (2, 3))[g % 4] if g < 4 else ():
                            round_off(1 - p, c, it * 64 + 32 * p + 48 + 16 * (c // 2))

        @block.vector
        def _(dve):
            for s in (idx_done, w_lo_done, x_hi_done, x_lo_done, h_hi_done, h_lo_done, y_done):
                dve.sem_inc(s, CREDIT)

            def places(n, i):
                for k in range(2):
                    last = nc.vector.tensor_copy(idx[i][k][:, :], keep.into[:, n, k:k + 1])
                last.then_inc(idx_done, 1)

            for i in range(SENT):
                places(i, i)
            for c, (k, at) in enumerate(cuts):
                dve.wait_ge(w_hi_done, ready(c))
                nc.vector.tensor_tensor(w_lo[0][k][:, at], raw[c % 2][:, :], w_hi[0][k][:, at].bitcast(F32), ALU.subtract).then_inc(w_lo_done, 1)
            with dve.Fori(1, NTT // SENT) as it:
                for i in range(SENT):
                    dve.wait_ge(sent[i], it * 32)
                    apart(dve, keep)
                    places(it * SENT + i, i)
            dve.wait_ge(b1_mm, 1)
            nc.vector.tensor_copy(b1_cols[:, :], p2[0][:, 0:E * KI]).then_inc(b1_done, 1)
            with dve.Fori(0, E // 2) as it:

                def inputs(p, G, g):
                    e = it * 2 + p
                    for i in range(GT):
                        n = e * XT + g * GT + i
                        at = slice(i * P, (i + 1) * P)
                        dve.wait_ge(xT_mm, ready(n))
                        if i == 0:
                            dve.wait_ge(up_mm, ready((e * NG + g - 1) * KI - 1))
                        nc.vector.tensor_copy(x_hi[:, G % 2, :, at], px[i][:, :, :]).then_inc(x_hi_done, 1)
                        dve.wait_ge(x_hi_done, ready(n))
                        nc.vector.tensor_tensor(x_lo[:, G % 2, :, at], px[i][:, :, :], x_hi[:, G % 2, :, at].bitcast(F32),
                                                ALU.subtract).then_inc(x_lo_done, 1)

                def hidden(p, G, g):
                    e = it * 2 + p
                    for k in range(KI):
                        u = (e * NG + g) * KI + k
                        piece = h[:, (G * KI + k) % RING, :]
                        dve.wait_ge(up_done, ready(u))
                        if k == 0:
                            dve.wait_ge(y_mm, ready((e * NG + g - 1) * GT - 1))
                        nc.vector.tensor_copy(h_hi[:, G % 2, k, :], piece).then_inc(h_hi_done, 1)
                        dve.wait_ge(h_hi_done, ready(u))
                        nc.vector.tensor_tensor(h_lo[:, G % 2, k, :], piece, h_hi[:, G % 2, k, :].bitcast(F32), ALU.subtract).then_inc(h_lo_done, 1)

                def outputs(p, G, g):
                    e = it * 2 + p
                    if g == 0:
                        dve.wait_ge(x_in[p], it * 32 + 32)
                    for i in range(GT):
                        t = g * GT + i
                        dve.wait_ge(y_mm, ready(e * XT + t))
                        dve.wait_ge(y_st[t % 2], (e * XT // 2 + t // 2) * 16 + 1)
                        nc.vector.tensor_tensor(ys[:, t % 2, :], p2[t % 2][:, :], b2_sb[p][:, :], ALU.add).then_inc(y_done, 1)

                both = groups(0) + groups(1)
                inputs(0, 0, 0)
                for G, p, g in both:
                    hidden(p, G, g)
                    if G + 1 < 2 * NG:
                        inputs(both[G + 1][1], G + 1, both[G + 1][2])
                    if G:
                        outputs(both[G - 1][1], G - 1, both[G - 1][2])
                outputs(1, 2 * NG - 1, NG - 1)

        @block.tensor
        def _(pe):
            for s in (xT_mm, up_mm, y_mm):
                pe.sem_inc(s, CREDIT)
            pe.wait_ge(b1_in, 16)
            nc.tensor.transpose(p2[0][:, 0:E * KI], b1_rows[:, :], keep.ident[0:E * KI, 0:E * KI]).then_inc(b1_mm, 1)
            pe.wait_ge(b1_done, 1)
            with pe.Fori(0, E // 2) as it:

                def turn(p, g):
                    e = it * 2 + p
                    if g == 0:
                        pe.wait_ge(x_in[p], it * 32 + 32)
                    for i in range(GT):
                        n = e * XT + g * GT + i
                        pe.wait_ge(x_lo_done, free(n, 2))
                        for k in range(KD):
                            last = nc.tensor.transpose(px[i][:, k, :], xs[p][:, g * GT + i, k * P:(k + 1) * P], keep.ident[:, :])
                        last.then_inc(xT_mm, 1)

                def up(p, G, g):
                    e = it * 2 + p
                    if g == 0:
                        pe.wait_ge(w_lo_done, ready(e * NC + NC - 1))
                    pe.wait_ge(x_lo_done, ready((e * NG + g) * GT + GT - 1))
                    for j in range(KI):
                        u = (e * NG + g) * KI + j
                        pe.wait_ge(up_done, free(u, RING))
                        terms = [(a, b, k) for a, b in ((w_hi[p][0], x_hi), (w_hi[p][0], x_lo), (w_lo[p][0], x_hi)) for k in range(KD)]
                        for i, (a, b, k) in enumerate(terms):
                            at = slice(k * INNER + j * P, k * INNER + (j + 1) * P)
                            last = nc.tensor.matmul(p1[(G * KI + j) % RING][:, :], a[:, at].bitcast(F32R), b[:, G % 2, k, :],
                                                    start=(i == 0), stop=(i == len(terms) - 1))
                        last.then_inc(up_mm, 1)

                def down(p, G, g):
                    e = it * 2 + p
                    pe.wait_ge(h_lo_done, ready((e * NG + g) * KI + KI - 1))
                    for i in range(GT):
                        t = g * GT + i
                        pe.wait_ge(y_done, free(e * XT + t, 2))
                        terms = [(a, b, j) for a, b in ((h_hi, w_hi[p][1]), (h_lo, w_hi[p][1]), (h_hi, w_lo[p][1])) for j in range(KI)]
                        for o, (a, b, j) in enumerate(terms):
                            last = nc.tensor.matmul(p2[t % 2][:, :], a[:, G % 2, j, i * P:(i + 1) * P],
                                                    b[:, j * D:(j + 1) * D].bitcast(F32R), start=(o == 0), stop=(o == len(terms) - 1))
                        last.then_inc(y_mm, 1)

                both = groups(0) + groups(1)
                turn(0, 0)
                for G, p, g in both:
                    up(p, G, g)
                    if G + 1 < 2 * NG:
                        turn(both[G + 1][1], both[G + 1][2])
                    if G:
                        down(both[G - 1][1], G - 1, both[G - 1][2])
                down(1, 2 * NG - 1, NG - 1)


def combine(nc, keep, y_slots, out):
    RING = 4
    with ExitStack() as ctx:
        m = Program(nc, ctx, "comb")
        rows = [[m.sbuf(f"rows{i}_{k}", [P, D]) for k in range(2)] for i in range(RING)]
        idx = [[m.sbuf(f"idx{i}_{k}", [P, 1], I32) for k in range(2)] for i in range(RING)]
        ta = m.sbuf("ta", [P, D])
        tb = m.sbuf("tb", [P, D])
        tc = m.sbuf("tc", [P, D])
        o = m.sbuf("o", [P, RING, D])
        got = [m.sem(f"got{i}") for i in range(RING)]
        o_st = [m.sem(f"o_st{i}") for i in range(RING)]
        idx_done, used, o_done, chain = m.sem("idx"), m.sem("used"), m.sem("o"), m.sem("chain")
        out_t = out.rearrange("b (t p) d -> (b t) p d", p=P)
        block = ctx.enter_context(nc.Block())

        @block.scalar
        def _(act):
            act.sem_inc(idx_done, CREDIT)
            with act.Fori(0, NTT // RING) as it:
                for i in range(RING):
                    n = it * RING + i
                    act.wait_ge(used, free(n, RING))
                    for k in range(2):
                        last = nc.scalar.activation(idx[i][k][:, :], keep.outof[:, n, k:k + 1], ACT.Copy)
                    last.then_inc(idx_done, 1)

        @block.gpsimd
        def _(pool):
            with pool.Fori(0, NTT // RING) as it:
                for i in range(RING):
                    n = it * RING + i
                    pool.wait_ge(idx_done, ready(n))
                    pool.wait_ge(used, free(n, RING))
                    apart(pool, keep)
                    for k in range(2):
                        nc.gpsimd.indirect_dma_start(rows[i][k][:, :], None, y_slots,
                                                     bass.IndirectOffsetOnAxis(ap=idx[i][k][:, :].bitcast(U32), axis=0),
                                                     bounds_check=E * CAP - 1, oob_is_err=True).then_inc(got[i], 16)

        @block.vector
        def _(dve):
            for s in (used, o_done):
                dve.sem_inc(s, CREDIT)
            with dve.Fori(0, NTT // RING) as it:
                for i in range(RING):
                    n = it * RING + i
                    c = Chain(dve, chain, n * 2)
                    dve.wait_ge(got[i], it * 32 + 32)
                    c.link(nc.vector.tensor_scalar(ta[:, :], rows[i][0][:, :], keep.weight[:, 0, bass.ds(n, 1)], None, ALU.mult))
                    nc.vector.scalar_tensor_tensor(tb[:, :], rows[i][1][:, :], keep.weight[:, 1, bass.ds(n, 1)], ta[:, :],
                                                   ALU.mult, ALU.add).then_inc(used, 1)
                    dve.wait_ge(used, ready(n))
                    c.link(nc.vector.tensor_tensor(tc[:, :], tb[:, :], keep.mod[:, n // NT, 5, :], ALU.mult))
                    dve.wait_ge(o_st[i], it * 16 + 1)
                    nc.vector.tensor_tensor(o[:, i, :], tc[:, :], keep.x1[:, n, :], ALU.add).then_inc(o_done, 1)

        @block.sync
        def _(sp):
            for i in range(RING):
                sp.sem_inc(o_st[i], 1)
            with sp.Fori(0, NTT // RING) as it:
                for i in range(RING):
                    n = it * RING + i
                    sp.wait_ge(o_done, ready(n))
                    sp.dma_start(out_t[n], o[:, i, :]).then_inc(o_st[i], 16)
            for i in range(RING):
                sp.wait_ge(o_st[i], 1 + 16 * (NTT // RING))


def fall_back(nc, keep, fw1, fb1, fw2, fb2, h2_rows, out):
    with ExitStack() as ctx:
        m = Program(nc, ctx, "fall")
        w1 = m.sbuf("w1", [P, KD, INNER])
        w2 = m.sbuf("w2", [P, KI, D])
        b1_rows = m.sbuf("b1_rows", [KI, P])
        b1_cols = m.sbuf("b1_cols", [P, KI])
        b2 = m.sbuf("b2", [P, D])
        x = m.sbuf("x", [P, D])
        o = m.sbuf("o", [P, D])
        xT = m.sbuf("xT", [P, KD, P])
        hT = m.sbuf("hT", [P, KI, P])
        y = m.sbuf("y", [P, D])
        missing = m.sbuf("missing", [P, NTT])
        px = m.psum("px", [P, KD, P])
        p1 = m.psum("p1", [P, KI, P])
        p2 = m.psum("p2", [P, D])
        w_in, t_in, t_st = m.sem("w_in"), m.sem("t_in"), m.sem("t_st")
        b1_mm, b1_done, xT_mm, xT_done, up_mm, up_done, y_mm, o_done, chain = (
            m.sem(s) for s in ("b1_mm", "b1", "xT_mm", "xT", "up_mm", "up", "y_mm", "o", "chain"))
        h_t = h2_rows
        out_t = out.rearrange("b (t p) d -> (b t) p d", p=P)
        block = ctx.enter_context(nc.Block())

        def overflowed(eng):
            return eng.If(eng.value_load(keep.flag[0:1, 0:1], min_val=0, max_val=NTOK) > 0)

        @block.sync
        def _(sp):
            with overflowed(sp):
                sp.dma_start(w1[:, :, :], fw1.rearrange("(k p) n -> p k n", p=P)).then_inc(w_in, 16)
                sp.dma_start(w2[:, :, :], fw2.rearrange("(m p) n -> p m n", p=P)).then_inc(w_in, 16)
                sp.dma_start(b1_rows[:, :], fb1.rearrange("(m p) -> m p", p=P)).then_inc(w_in, 16)
                sp.dma_start(b2[:, :], fb2[None, :].to_broadcast([P, D])).then_inc(w_in, 16)
                sp.sem_inc(t_st, 1)
                with sp.Fori(0, NTT) as n:
                    sp.wait_ge(t_st, n * 16 + 1)
                    sp.dma_start(x[:, :], h_t[n]).then_inc(t_in, 16)
                    sp.dma_start(o[:, :], out_t[n]).then_inc(t_in, 16)
                    sp.wait_ge(o_done, n + 1)
                    sp.dma_start(out_t[n], o[:, :]).then_inc(t_st, 16)
                sp.wait_ge(t_st, 1 + 16 * NTT)

        @block.scalar
        def _(act):
            with overflowed(act):
                act.wait_ge(b1_done, 1)
                with act.Fori(0, NTT) as n:
                    act.wait_ge(up_mm, n + 1)
                    for k in range(KI):
                        last = nc.scalar.activation(hT[:, k, :], p1[:, k, :], ACT.Gelu, bias=b1_cols[:, k:k + 1])
                    last.then_inc(up_done, 1)

        @block.vector
        def _(dve):
            with overflowed(dve):
                c = Chain(dve, chain)
                dve.wait_ge(b1_mm, 1)
                nc.vector.tensor_copy(b1_cols[:, :], px[:, 0, 0:KI]).then_inc(b1_done, 1)
                c.link(nc.vector.tensor_scalar(missing[:, :], keep.plain[:, :], -1.0, 1.0, ALU.mult, ALU.add))
                with dve.Fori(0, NTT) as n:
                    c = Chain(dve, chain, n * 3 + 1)
                    dve.wait_ge(xT_mm, n + 1)
                    nc.vector.tensor_copy(xT[:, :, :], px[:, :, :]).then_inc(xT_done, 1)
                    dve.wait_ge(y_mm, n + 1)
                    c.link(nc.vector.tensor_tensor(y[:, :], p2[:, :], b2[:, :], ALU.add))
                    c.link(nc.vector.tensor_scalar(y[:, :], y[:, :], missing[:, bass.ds(n, 1)], None, ALU.mult))
                    c.link(nc.vector.tensor_tensor(y[:, :], y[:, :], keep.mod[:, n // NT, 5, :], ALU.mult))
                    dve.wait_ge(t_in, n * 32 + 32)
                    nc.vector.tensor_tensor(o[:, :], o[:, :], y[:, :], ALU.add).then_inc(o_done, 1)

        @block.tensor
        def _(pe):
            with overflowed(pe):
                pe.wait_ge(w_in, 64)
                nc.tensor.transpose(px[:, 0, 0:KI], b1_rows[:, :], keep.ident[0:KI, 0:KI]).then_inc(b1_mm, 1)
                pe.wait_ge(b1_done, 1)
                with pe.Fori(0, NTT) as n:
                    pe.wait_ge(t_in, n * 32 + 32)
                    for k in range(KD):
                        last = nc.tensor.transpose(px[:, k, :], x[:, k * P:(k + 1) * P], keep.ident[:, :])
                    last.then_inc(xT_mm, 1)
                    pe.wait_ge(xT_done, n + 1)
                    for j in range(KI):
                        for k in range(KD):
                            last = nc.tensor.matmul(p1[:, j, :], w1[:, k, j * P:(j + 1) * P], xT[:, k, :], start=(k == 0), stop=(k == KD - 1))
                    last.then_inc(up_mm, 1)
                    pe.wait_ge(up_done, n + 1)
                    for j in range(KI):
                        last = nc.tensor.matmul(p2[:, :], hT[:, j, :], w2[:, j, :], start=(j == 0), stop=(j == KI - 1))
                    last.then_inc(y_mm, 1)


class Keep:
    pass


def build(nc, dr):
    with ExitStack() as ctx:
        keep = Keep()
        m = Program(nc, ctx, "keep")
        keep.weight = m.sbuf("weight", [P, 2, NTT])
        keep.into = m.sbuf("into", [P, NTT, 2], I32)
        keep.outof = m.sbuf("outof", [P, NTT, 2], I32)
        keep.plain = m.sbuf("plain", [P, NTT])
        keep.flag = m.sbuf("flag", [P, 1], I32)
        keep.ident = m.sbuf("ident", [P, P])
        keep.before = m.sbuf("before", [P, P])
        keep.mod = m.sbuf("mod", [P, B, 6, D])
        keep.sign = m.sbuf("sign", [P, D])
        keep.shift1 = m.sbuf("shift1", [P, B, KD])
        keep.scale1 = m.sbuf("scale1", [P, B, KD])
        keep.neg_half = m.sbuf("neg_half", [P, PAIRS, NT])
        keep.row_max = m.sbuf("row_max", [P, PAIRS, NT, 2])
        keep.logits = m.sbuf("logits", [P, NTT, E])
        scratch = lambda name, shape: nc.dram_tensor(name, shape, F32, kind="Internal").ap()
        q_rows = scratch("q_rows", (B, HEADS, HD, T))
        k_rows = scratch("k_rows", (B, KVH, HD, T))
        v_cent = scratch("v_cent", (B, KVH, P, NT, HD))
        gate_logit = scratch("gate_logit", (B, KVH, T))
        half_log = scratch("half_log", (PAIRS, T))
        x_slots = scratch("x_slots", (E * CAP, D))
        num_rows = scratch("num_rows", (PAIRS, P, T))
        constants(nc, keep, dr)
        with ExitStack() as until_projected:
            early = early_memory(nc, until_projected)
            modulation(nc, keep, early, dr["L0_c"], dr["L0_wmod"], dr["L0_attn_x"], dr["L0_attn_w_attn"], dr["rope"], dr["basis"])
            project(nc, keep, early, dr["L0_attn_x"], q_rows, k_rows, v_cent, gate_logit)
        decays(nc, keep, gate_logit, half_log)
        attend(nc, keep, q_rows, k_rows, v_cent, half_log, num_rows, x_slots)
        keep.x1 = m.sbuf("x1", [P, NTT, D])
        h2_rows = scratch("h2_rows", (NTT, P, D))
        close_attention(nc, keep, dr["L0_attn_x"], dr["L0_attn_w_proj"], dr["L0_attn_ln_w"], dr["L0_ffn_Wr"], dr["basis"],
                        num_rows, h2_rows)
        y_slots = scratch("y_slots", (E * CAP, D))
        choose(nc, keep, dr["upto"], dr["experts"])
        experts(nc, keep, dr["L0_ffn_W1"], dr["L0_ffn_b1"], dr["L0_ffn_W2"], dr["L0_ffn_b2"], h2_rows, x_slots, y_slots)
        combine(nc, keep, y_slots, dr["out"])
        fall_back(nc, keep, dr["L0_ffn_fw1"], dr["L0_ffn_fb1"], dr["L0_ffn_fw2"], dr["L0_ffn_fb2"], h2_rows, dr["out"])


def constants(nc, keep, dr):
    with ExitStack() as ctx:
        m = Program(nc, ctx, "const")
        keep.passed = m.sem("passed")
        c_in = m.sem("in")
        block = ctx.enter_context(nc.Block())

        @block.sync
        def _(sp):
            sp.sem_inc(c_in, 16)
            sp.dma_start(keep.ident[:, :], dr["ident"]).then_inc(c_in, 16)
            sp.dma_start(keep.before[:, :], dr["before"]).then_inc(c_in, 16)
            sp.wait_ge(c_in, 48)


_INS = ['L0_attn_x', 'L0_attn_w_attn', 'L0_attn_w_proj', 'L0_attn_ln_w', 'L0_ffn_Wr', 'L0_ffn_W1', 'L0_ffn_b1',
        'L0_ffn_W2', 'L0_ffn_b2', 'L0_ffn_fw1', 'L0_ffn_fb1', 'L0_ffn_fw2', 'L0_ffn_fb2', 'L0_c', 'L0_wmod']


def shape_constants():
    import numpy as np
    div = (2.0 * np.pi / float(T) ** (np.arange(0, HD, 2, dtype=np.float32) / HD)).astype(np.float32)
    ang = (np.arange(T, dtype=np.float32)[:, None] * div[None, :]).astype(np.float64)
    cos = np.repeat(np.cos(ang), 2, axis=1)
    sin = np.repeat(np.sin(ang), 2, axis=1)
    sin[:, 0::2] *= -1.0
    scale = HD ** -0.5
    tab = np.stack([cos * scale, sin * scale, cos, sin]).astype(np.float32)
    rope = np.ascontiguousarray(tab.reshape(4, NT, P, HD).transpose(2, 0, 1, 3))
    r = np.arange(P)
    ch = P // PAIRS
    before = ((r[:, None] // ch == r[None, :] // ch) & (r[:, None] < r[None, :])).astype(np.float32)
    d = np.arange(HD)
    cosines = np.sqrt(2.0 / HD) * np.cos(np.pi * (d[:, None] + 0.5) * (d[None, :] + 1) / HD)
    cosines[:, HD - 1] = 0.0
    basis = np.zeros((P, P), np.float32)
    for h in range(2):
        basis[h * HD:(h + 1) * HD, h * HD:(h + 1) * HD] = cosines
    upto = (r[:, None] <= r[None, :]).astype(np.float32)
    experts_row = np.ascontiguousarray(np.broadcast_to(np.arange(E, dtype=np.float32), (P, E)))
    return {"upto": upto, "experts": experts_row, "basis": basis, "rope": rope, "ident": np.eye(P, dtype=np.float32), "before": before}


def kernel(**inputs):
    import numpy as np
    import concourse.bacc as bacc
    from concourse.bass_utils import run_bass_kernel_spmd

    nc = bacc.Bacc("TRN2", target_bir_lowering=False, num_devices=1)
    arrays = {name: np.ascontiguousarray(inputs[name]) for name in _INS} | shape_constants()
    dr = {name: nc.dram_tensor(name, a.shape, mybir.dt.from_np(a.dtype), kind="ExternalInput").ap() for name, a in arrays.items()}
    dr["out"] = nc.dram_tensor("out", (B, T, D), F32, kind="ExternalOutput").ap()
    build(nc, dr)
    r = run_bass_kernel_spmd(nc, [arrays], core_ids=[0])
    return r.results[0]["out"]
```

```python
from contextlib import ExitStack

import concourse.bass as bass
from concourse import mybir
from concourse.alu_op_type import AluOpType as ALU

F32 = mybir.dt.float32
F32R = mybir.dt.float32r
U32 = mybir.dt.uint32
I32 = mybir.dt.int32
ACT = mybir.ActivationFunctionType
AX = mybir.AxisListType

P = 128
B, T, D = 2, 2048, 256
NTOK = B * T
NT = T // P
NTT = NTOK // P
KD = D // P
HEADS, KVH, HD = 16, 8, 64
QW, KW = HEADS * HD, KVH * HD
QKV = QW + 2 * KW
PAIRS = B * KVH
TB = 512
NB = T // TB
ST = TB // P
E, INNER, CAP = 8, 1024, 1280
KI = INNER // P
GATE_BIAS = 6.906768
LN_EPS = 1e-5
CREDIT = 16


def ready(k):
    return k + (CREDIT + 1)


def free(k, depth):
    return k + (CREDIT + 1 - depth)


class Program:

    def __init__(self, nc, ctx, tag):
        self.nc, self.ctx, self.tag, self.sems = nc, ctx, tag, []

    def sbuf(self, name, shape, dt=F32):
        return self.ctx.enter_context(self.nc.sbuf_tensor(f"{self.tag}_sb_{name}", shape, dt))

    def psum(self, name, shape, dt=F32):
        return self.ctx.enter_context(self.nc.psum_tensor(f"{self.tag}_ps_{name}", shape, dt))

    def sem(self, name):
        self.sems.append(self.nc.alloc_semaphore(f"{self.tag}_{name}"))
        return self.sems[-1]


def apart(eng, keep):
    eng.sem_inc(keep.passed, 1)


class Chain:

    def __init__(self, eng, sem, base=0):
        self.eng, self.sem, self.base, self.n = eng, sem, base, 0

    def link(self, ins):
        self.n += 1
        ins.then_inc(self.sem, 1)
        self.eng.wait_ge(self.sem, self.base + self.n)


def early_memory(nc, ctx):
    early = Keep()
    m = Program(nc, ctx, "early")
    early.w = m.sbuf("w", [P, KD, QKV + KVH])
    early.tab = m.sbuf("tab", [P, 4, NT, HD])
    early.basis = m.sbuf("basis", [P, P])
    early.xt = m.sbuf("xt", [P, 2, D])
    early.w_in = m.sem("w_in")
    early.tab_in = m.sem("tab_in")
    early.x_in = [m.sem(f"x_in{i}") for i in range(2)]
    return early


def rows_memory(nc, ctx):
    rows = Keep()
    m = Program(nc, ctx, "rows")
    rows.silu = m.sbuf("silu", [P, B, KD, P])
    rows.w = m.sbuf("w", [P, KD, 6 * D])
    rows.w_in = m.sem("w_in")
    return rows


def modulation(nc, keep, early, rows, cond, wmod, x, w_attn, rope, basis, ident, before):
    with ExitStack() as ctx:
        m = Program(nc, ctx, "mod")
        cT = m.sbuf("cT", [P, B, KD])
        sT = m.sbuf("sT", [P, B, KD])
        w = rows.w
        pc = m.psum("pc", [P, 2 * KD, B])
        sem_in, silu_done, cols_done = (m.sem(x) for x in ("in", "silu", "cols"))
        block = ctx.enter_context(nc.Block())

        @block.sync
        def _(sp):
            for b in range(B):
                for k in range(KD):
                    sp.dma_start(cT[:, b, k:k + 1], cond[b, k * P:(k + 1) * P].rearrange("(p o) -> p o", o=1)).then_inc(sem_in, 16)
            wmod_t = wmod.rearrange("(k p) n -> p k n", p=P)
            sp.dma_start(w[:, :, 0:2 * D], wmod_t[:, :, 0:2 * D]).then_inc(sem_in, 16)
            for i in range(2):
                sp.dma_start(early.xt[:, i, :], x[0, i * P:(i + 1) * P, :]).then_inc(early.x_in[i], 16)
            sp.dma_start(early.w[:, :, :], w_attn.rearrange("(k p) n -> p k n", p=P)).then_inc(early.w_in, 16)
            sp.dma_start(early.basis[:, :], basis).then_inc(early.w_in, 16)
            sp.dma_start(keep.ident[:, :], ident).then_inc(early.w_in, 16)
            sp.dma_start(keep.before[:, :], before).then_inc(early.w_in, 16)
            sp.dma_start(early.tab[:, :, :, :], rope).then_inc(early.tab_in, 16)
            sp.dma_start(w[:, :, 2 * D:], wmod_t[:, :, 2 * D:]).then_inc(rows.w_in, 16)

        @block.scalar
        def _(act):
            act.wait_ge(sem_in, 16 * (B * KD + 1))
            nc.scalar.activation(sT[:, :, :], cT[:, :, :], ACT.Silu).then_inc(silu_done, 1)

        @block.tensor
        def _(pe):
            pe.wait_ge(sem_in, 16 * (B * KD + 1))
            pe.wait_ge(silu_done, 1)
            for mm in range(2 * KD):
                for k in range(KD):
                    last = nc.tensor.matmul(pc[:, mm, :], w[:, k, mm * P:(mm + 1) * P], sT[:, :, k],
                                            start=(k == 0), stop=(k == KD - 1))
            last.then_inc(cols_done, 1)

        @block.vector
        def _(dve):
            dve.wait_ge(silu_done, 1)
            nc.vector.tensor_copy(rows.silu[:, :, :, :], sT[:, :, :, None].to_broadcast([P, B, KD, P]))
            dve.wait_ge(cols_done, 1)
            nc.vector.tensor_copy(keep.shift1[:, :, :], pc[:, 0:KD, :].rearrange("p k b -> p b k"))
            nc.vector.tensor_scalar(keep.scale1[:, :, :], pc[:, KD:2 * KD, :].rearrange("p k b -> p b k"), 1.0, None, ALU.add)


def project(nc, keep, early, x, q_rows, k_rows, v_cent, gate_logit):
    with ExitStack() as ctx:
        m = Program(nc, ctx, "proj")
        w, tab, basis_sb, xt, w_in, x_in = early.w, early.tab, early.basis, early.xt, early.w_in, early.x_in
        w_hi = m.sbuf("w_hi", [P, KD, QKV], F32R)
        w_lo = m.sbuf("w_lo", [P, KD, QKV], F32R)
        wv_T = m.sbuf("wv_T", [P, KD, KW])
        st6 = m.sbuf("st6", [P, 6])
        mv = m.sbuf("mv", [P, 2, 2])
        rs = m.sbuf("rs", [P, 2, 2])
        xn = m.sbuf("xn", [P, 2, D])
        h = m.sbuf("h", [P, 2, KD, P])
        h_hi = m.sbuf("h_hi", [P, 2, KD, P], F32R)
        h_lo = m.sbuf("h_lo", [P, 2, KD, P], F32R)
        z = m.sbuf("z", [P, 3, KVH, HD])
        t1 = m.sbuf("t1", [P, 3, KVH, HD])
        t2 = m.sbuf("t2", [P, 3, KVH, HD])
        r = m.sbuf("r", [P, 3, KVH * HD])
        rT = m.sbuf("rT", [P, 3, 4, P])
        vt = m.sbuf("vt", [P, 2, KVH, HD])
        gs = m.sbuf("gs", [KVH, 2, P])
        eps = m.sbuf("eps", [P, 1])
        pc = [m.psum(f"pc{i}", [P, 512]) for i in range(4)]
        pr = [m.psum(f"pr{i}", [P, 4, P]) for i in range(2)]
        px = m.psum("px", [P, KD, P])
        pg = m.psum("pg", [KVH, P])
        wv_turned, wv_T_done, wv_mm, wv_done, w_hi_done, w_lo_done = (
            m.sem(s) for s in ("wv_turned", "wv_T", "wv_mm", "wv", "w_hi", "w_lo"))
        var_done, std_done, rstd_done, xn_done, xnT_done, h_done, h_hi_done, h_lo_done = (
            m.sem(s) for s in ("var", "std", "rstd", "xn", "xnT", "h", "h_hi", "h_lo"))
        gate_mm, gate_out = m.sem("gate_mm"), m.sem("gate_out")
        chunk_mm, z_done, t1_done, t2_done, kr_done, qr_done, rot_done, rT_done, v_done = (
            m.sem(s) for s in ("chunk", "z", "t1", "t2", "kr", "qr", "rot", "rT", "v"))
        r_st = [m.sem(f"r_st{i}") for i in range(3)]
        v_st = [m.sem(f"v_st{i}") for i in range(2)]
        g_st = [m.sem(f"g_st{i}") for i in range(2)]
        ones_done, st_done = m.sem("ones"), m.sem("st")
        cols = [QW, 0, 512, QW + KW]
        x_t = x.rearrange("b (t p) d -> (b t) p d", p=P)
        block = ctx.enter_context(nc.Block())

        def turns(eng, turn):
            for n in range(2):
                turn(n, n % 2, True, n > 0, True)
            with eng.Fori(1, NTT // 2 - 1) as it:
                for p in range(2):
                    turn(it * 2 + p, p, True, True, True)
            for n in range(NTT - 2, NTT + 1):
                turn(n, n % 2, n < NTT, True, n + 1 < NTT)

        @block.sync
        def _(sp):
            for s in r_st + v_st + g_st:
                sp.sem_inc(s, 1)

            def rows(n, c):
                b, t = n // NT, n % NT
                dst, h0 = (k_rows, 0) if c == 0 else (q_rows, 8 * (c - 1))
                sp.wait_ge(rT_done, ready(n * 3 + c))
                apart(sp, keep)
                sp.dma_start(dst[b, h0:h0 + 8, :, bass.ds(t * P, P)].rearrange("(c hh) d t -> (hh d) c t", hh=2),
                             rT[:, c, :, :]).then_inc(r_st[c], 16)

            def turn(n, p, this, before, after):
                if this:
                    sp.wait_ge(gate_out, ready(n))
                    apart(sp, keep)
                    sp.dma_start(gate_logit[n // NT, :, bass.ds(n % NT * P, P)], gs[:, p, :]).then_inc(g_st[p], 16)
                if before:
                    rows(n - 1, 1)
                    rows(n - 1, 2)
                if this:
                    sp.wait_ge(v_done, ready(n))
                    apart(sp, keep)
                    sp.dma_start(v_cent[n // NT, :, :, n % NT, :].rearrange("j p d -> p j d"), vt[:, p, :, :]).then_inc(v_st[p], 16)
                    rows(n, 0)

            turns(sp, turn)
            for c in range(3):
                sp.wait_ge(r_st[c], 1 + 16 * NTT)
            for i in range(2):
                sp.wait_ge(v_st[i], 1 + 16 * (NTT // 2))
                sp.wait_ge(g_st[i], 1 + 16 * (NTT // 2))

        @block.scalar
        def _(act):
            for s in (std_done, h_done, h_hi_done, gate_out, z_done, rT_done, v_done):
                act.sem_inc(s, CREDIT)
            def std(n, p):
                act.wait_ge(var_done, ready(n))
                nc.scalar.activation(rs[:, p, 0:1], mv[:, p, 1:2], ACT.Sqrt, bias=eps[:, :]).then_inc(std_done, 1)

            def modulate(n, p):
                act.wait_ge(xnT_done, ready(n))
                act.wait_ge(chunk_mm, n * 4 + (CREDIT + 1 - 5))
                act.wait_ge(h_lo_done, free(n, 2))
                apart(act, keep)
                for k in range(KD):
                    last = nc.scalar.activation(h[:, p, k, :], px[:, k, :], ACT.Identity,
                                                scale=keep.scale1[:, n // NT, k:k + 1], bias=keep.shift1[:, n // NT, k:k + 1])
                last.then_inc(h_done, 1)
                act.wait_ge(h_done, ready(n))
                nc.scalar.activation(h_hi[:, p, :, :], h[:, p, :, :], ACT.Copy).then_inc(h_hi_done, 1)

            def evacuate(n, c):
                act.wait_ge(chunk_mm, ready(n * 4 + c))
                act.wait_ge(t1_done, free(n * 3 + c, 3))
                act.wait_ge(t2_done, free(n * 3 + c, 3))
                nc.scalar.activation(z[:, c, :, :], pc[c][:, :].rearrange("p (h d) -> p h d", d=HD), ACT.Copy).then_inc(z_done, 1)

            def turned(n, p, c):
                act.wait_ge(rot_done, ready(n * 3 + c))
                act.wait_ge(r_st[c], n * 16 + 1)
                nc.scalar.activation(rT[:, c, :, :], pr[(p + c) % 2][:, :, :], ACT.Copy).then_inc(rT_done, 1)

            act.wait_ge(ones_done, 1)
            std(0, 0)
            act.wait_ge(w_in, 64)
            for c in range(4):
                if c == 2:
                    modulate(0, 0)
                if c == 3:
                    act.wait_ge(wv_done, 1)
                nc.scalar.activation(w_hi[:, :, cols[c]:cols[c] + 512], w[:, :, cols[c]:cols[c] + 512], ACT.Copy).then_inc(w_hi_done, 1)

            def turn(n, p, this, before, after):
                if this:
                    act.wait_ge(gate_mm, ready(n))
                    act.wait_ge(g_st[p], n // 2 * 16 + 1)
                    nc.scalar.activation(gs[:, p, :], pg[:, :], ACT.Copy).then_inc(gate_out, 1)
                    evacuate(n, 0)
                if after:
                    std(n + 1, 1 - p)
                if before:
                    turned(n - 1, 1 - p, 1)
                if this:
                    evacuate(n, 1)
                if before:
                    turned(n - 1, 1 - p, 2)
                if this:
                    act.wait_ge(xn_done, ready(n))
                    apart(act, keep)
                    act.dma_start(xt[:, p, :], x_t[(n + 2) % NTT]).then_inc(x_in[p], 16)
                    evacuate(n, 2)
                if after:
                    modulate(n + 1, 1 - p)
                if this:
                    act.wait_ge(chunk_mm, ready(n * 4 + 3))
                    act.wait_ge(v_st[p], n // 2 * 16 + 1)
                    nc.scalar.activation(vt[:, p, :, 0:HD - 1], pc[3][:, :].rearrange("p (h d) -> p h d", d=HD)[:, :, 0:HD - 1],
                                         ACT.Copy).then_inc(v_done, 1)
                    turned(n, p, 0)

            turns(act, turn)
            for i in range(2):
                act.wait_ge(x_in[i], 16 + 16 * (NTT // 2))

        @block.gpsimd
        def _(pool):
            for s in (t1_done, qr_done):
                pool.sem_inc(s, CREDIT)
            nc.gpsimd.memset(eps[:, :], LN_EPS)
            nc.gpsimd.memset(vt[:, :, :, HD - 1:HD], 1.0).then_inc(ones_done, 1)
            pool.wait_ge(early.tab_in, 16)

            def cosine(n, c):
                k = n * 3 + c
                cos = tab[:, 2 if c == 0 else 0, n % NT, None, :].to_broadcast([P, KVH, HD])
                pool.wait_ge(z_done, ready(k))
                if c == 0:
                    pool.wait_ge(kr_done, free(n, 1))
                apart(pool, keep)
                nc.gpsimd.tensor_tensor(t1[:, c, :, :], z[:, c, :, :], cos, ALU.mult).then_inc(t1_done, 1)

            with pool.Fori(0, NTT) as n:
                cosine(n, 0)
                for c in range(1, 3):
                    k = n * 3 + c
                    cosine(n, c)
                    pool.wait_ge(t1_done, ready(k))
                    pool.wait_ge(t2_done, ready(k))
                    pool.wait_ge(rot_done, free(k, 3))
                    nc.gpsimd.tensor_tensor(r[:, c, :].rearrange("p (h d) -> p h d", d=HD), t1[:, c, :, :], t2[:, c, :, :],
                                            ALU.add).then_inc(qr_done, 1)

        @block.vector
        def _(dve):
            for s in (var_done, st_done, rstd_done, xn_done, t2_done, kr_done, h_lo_done):
                dve.sem_inc(s, CREDIT)
            def variance(n, p):
                dve.wait_ge(x_in[p], n // 2 * 16 + 16)
                nc.vector.bn_stats(st6[:, :], xt[:, p, :]).then_inc(st_done, 1)
                dve.wait_ge(st_done, ready(n))
                apart(dve, keep)
                nc.vector.bn_aggr(mv[:, p, :], st6[:, :]).then_inc(var_done, 1)

            def norm(n, p):
                dve.wait_ge(std_done, ready(n))
                nc.vector.reciprocal(rs[:, p, 1:2], rs[:, p, 0:1]).then_inc(rstd_done, 1)
                dve.wait_ge(rstd_done, ready(n))
                dve.wait_ge(xnT_done, free(n, 2))
                nc.vector.tensor_scalar(xn[:, p, :], xt[:, p, :], mv[:, p, 0:1], rs[:, p, 1:2],
                                        ALU.subtract, ALU.mult).then_inc(xn_done, 1)

            def rest(n, p):
                dve.wait_ge(h_hi_done, ready(n))
                nc.vector.tensor_tensor(h_lo[:, p, :, :], h[:, p, :, :], h_hi[:, p, :, :].bitcast(F32), ALU.subtract).then_inc(h_lo_done, 1)

            def sine(n, c):
                k = n * 3 + c
                sin = tab[:, 3 if c == 0 else 1, n % NT, :]
                dve.wait_ge(z_done, ready(k))
                if c:
                    dve.wait_ge(qr_done, free(n * 2 + c - 1, 2))
                else:
                    dve.wait_ge(kr_done, free(n, 1))
                nc.vector.tensor_tensor(t2[:, c, :, 0::2], z[:, c, :, 1::2],
                                        sin[:, None, 0::2].to_broadcast([P, KVH, HD // 2]), ALU.mult)
                nc.vector.tensor_tensor(t2[:, c, :, 1::2], z[:, c, :, 0::2],
                                        sin[:, None, 1::2].to_broadcast([P, KVH, HD // 2]), ALU.mult).then_inc(t2_done, 1)

            def weights_rest(c):
                dve.wait_ge(w_hi_done, c + 1)
                nc.vector.tensor_tensor(w_lo[:, :, cols[c]:cols[c] + 512], w[:, :, cols[c]:cols[c] + 512],
                                        w_hi[:, :, cols[c]:cols[c] + 512].bitcast(F32), ALU.subtract).then_inc(w_lo_done, 1)

            variance(0, 0)
            norm(0, 0)
            dve.wait_ge(wv_turned, 1)
            for k in range(KD):
                last = nc.vector.tensor_copy(wv_T[:, k, :], pc[k][:, :])
            last.then_inc(wv_T_done, 1)
            weights_rest(0)
            dve.wait_ge(wv_mm, 1)
            for k in range(KD):
                last = nc.vector.tensor_copy(w[:, k, QW + KW:QKV], pc[KD + k][:, :])
            last.then_inc(wv_done, 1)
            dve.wait_ge(wv_done, 1)
            rest(0, 0)
            for c in range(1, 4):
                weights_rest(c)
            dve.wait_ge(early.tab_in, 16)

            def turn(n, p, this, before, after):
                if after:
                    variance(n + 1, 1 - p)
                if this:
                    sine(n, 0)
                if after:
                    norm(n + 1, 1 - p)
                if this:
                    sine(n, 1)
                    dve.wait_ge(t1_done, ready(n * 3))
                    dve.wait_ge(t2_done, ready(n * 3))
                    dve.wait_ge(rot_done, free(n * 3, 3))
                    nc.vector.tensor_tensor(r[:, 0, :].rearrange("p (h d) -> p h d", d=HD), t1[:, 0, :, :], t2[:, 0, :, :],
                                            ALU.add).then_inc(kr_done, 1)
                    sine(n, 2)
                if after:
                    rest(n + 1, 1 - p)

            turns(dve, turn)

        @block.tensor
        def _(pe):
            for s in (xnT_done, gate_mm, chunk_mm, rot_done):
                pe.sem_inc(s, CREDIT)
            pe.wait_ge(w_in, 64)
            for k in range(KD):
                for j in range(0, KW, P):
                    last = nc.tensor.transpose(pc[k][:, j:j + P], w[:, k, QW + KW + j:QW + KW + j + P], keep.ident[:, :])
            last.then_inc(wv_turned, 1)
            def transpose_in(n, p):
                pe.wait_ge(xn_done, ready(n))
                pe.wait_ge(h_done, free(n, 1))
                for k in range(KD):
                    last = nc.tensor.transpose(px[:, k, :], xn[:, p, k * P:(k + 1) * P], keep.ident[:, :])
                last.then_inc(xnT_done, 1)

            def chunk(n, p, c, first):
                if first:
                    pe.wait_ge(w_lo_done, c + 1)
                if c < 3:
                    pe.wait_ge(z_done, free(n * 3 + c, 3))
                else:
                    pe.wait_ge(v_done, free(n, 1))
                at = slice(cols[c], cols[c] + 512)
                terms = [(a, b, k) for a, b in ((h_hi, w_hi), (h_hi, w_lo), (h_lo, w_hi)) for k in range(KD)]
                if c == 0:
                    pe.wait_ge(h_hi_done, ready(n))
                for i, (a, b, k) in enumerate(terms):
                    if c == 0 and i == 2 * KD:
                        pe.wait_ge(h_lo_done, ready(n))
                    last = nc.tensor.matmul(pc[c][:, :], a[:, p, k, :], b[:, k, at], start=(i == 0), stop=(i == len(terms) - 1))
                last.then_inc(chunk_mm, 1)

            def rotated(n, p, c):
                if c:
                    pe.wait_ge(qr_done, ready(n * 2 + c - 1))
                else:
                    pe.wait_ge(kr_done, ready(n))
                pe.wait_ge(rT_done, free(n * 3 + c, 2))
                for j in range(4):
                    last = nc.tensor.transpose(pr[(p + c) % 2][:, j, :], r[:, c, j * P:(j + 1) * P], keep.ident[:, :])
                last.then_inc(rot_done, 1)

            transpose_in(0, 0)
            pe.wait_ge(wv_T_done, 1)
            for k in range(KD):
                for j in range(0, KW, P):
                    last = nc.tensor.matmul(pc[KD + k][:, j:j + P], wv_T[:, k, j:j + P], basis_sb[:, :], start=True, stop=True)
            last.then_inc(wv_mm, 1)

            def turn(n, p, this, before, after):
                if this:
                    pe.wait_ge(h_done, ready(n))
                    pe.wait_ge(gate_out, free(n, 1))
                    for k in range(KD):
                        last = nc.tensor.matmul(pg[:, :], w[:, k, QKV:QKV + KVH], h[:, p, k, :], start=(k == 0), stop=(k == KD - 1))
                    last.then_inc(gate_mm, 1)
                    chunk(n, p, 0, not before)
                if before:
                    rotated(n - 1, 1 - p, 1)
                if this:
                    chunk(n, p, 1, not before)
                if before:
                    rotated(n - 1, 1 - p, 2)
                if this:
                    chunk(n, p, 2, not before)
                if after:
                    transpose_in(n + 1, 1 - p)
                if this:
                    chunk(n, p, 3, not before)
                    rotated(n, p, 0)

            turns(pe, turn)
        return m.sems


def first_pair_memory(nc, ctx):
    first = Keep()
    m = Program(nc, ctx, "first")
    first.q = m.sbuf("q", [P, 2 * T])
    first.k = m.sbuf("k", [P, 2, T])
    first.v = m.sbuf("v", [P, NT, HD])
    first.pair_in = m.sem("pair_in")
    return first


def load_pair(sp, b, j, q_rows, k_rows, v_cent, q_sb, k_sb, v_sb, pair_in):
    for half in range(2):
        at = slice(half * HD, (half + 1) * HD)
        sp.dma_start(q_sb[at, :].rearrange("d (h t) -> d h t", h=2),
                     q_rows[b, bass.ds(j * 2, 2), :, :].rearrange("h d t -> d h t")).then_inc(pair_in, 16)
        sp.dma_start(k_sb[at, 1, :], k_rows[b, j, :, :]).then_inc(pair_in, 16)
    sp.dma_start(v_sb[:, :, :], v_cent[b, j, :, :, :]).then_inc(pair_in, 16)


def decays(nc, keep, first, rows, used_up, gate_logit, half_log, q_rows, k_rows, v_cent):
    CH = P // PAIRS
    CL = T // CH
    with ExitStack() as ctx:
        m = Program(nc, ctx, "dec")
        names = ("x", "mag", "e", "w", "lnw", "u", "sc")
        g = {s: m.sbuf(s, [P, CL]) for s in names}
        inv = m.sbuf("inv", [P, CL])
        one = m.sbuf("one", [P, CL])
        tot = m.sbuf("tot", [P, 1])
        pt = m.psum("pt", [P, 1])
        pn = [m.psum(f"pn{i}", [P, P]) for i in range(CL // P)]
        RR = 4
        RW = 2 * D
        pr = [m.psum(f"pr{i}", [P, RW]) for i in range(RR)]
        chunks = [(b, n) for b in range(B) for n in range(6 * D // RW)]
        row_mm, row_done = m.sem("row_mm"), m.sem("row")
        x_in, mag_done, e_done, w_done, ln_done, scan_done, carry_mm, sum_done, turned, stored, chain = (
            m.sem(s) for s in ("x_in", "mag", "e", "w", "ln", "scan", "carry", "sum", "turned", "stored", "chain"))
        block = ctx.enter_context(nc.Block())

        @block.sync
        def _(sp):
            sp.dma_start(g["x"][:, :], gate_logit.rearrange("b h (c t) -> (b h c) t", t=CL)).then_inc(x_in, 16)
            load_pair(sp, 0, 0, q_rows, k_rows, v_cent, first.q, first.k, first.v, first.pair_in)
            sp.wait_ge(sum_done, 1)
            sp.dma_start(half_log.rearrange("r (c t) -> (r c) t", t=CL), g["sc"][:, :]).then_inc(stored, 16)
            sp.wait_ge(stored, 16)

        @block.gpsimd
        def _(pool):
            nc.clear_and_free_semaphores(used_up)

        @block.scalar
        def _(act):
            def copy_row(i):
                b, n = chunks[i]
                act.wait_ge(row_mm, i + 1)
                nc.scalar.activation(keep.mod[:, b, 2 * n:2 * n + 2, :], pr[i % RR][:, :].rearrange("p (s d) -> p s d", s=2),
                                     ACT.Copy).then_inc(row_done, 1)

            act.wait_ge(mag_done, 1)
            nc.scalar.activation(g["e"][:, :], g["mag"][:, :], ACT.Exp, scale=-1.0).then_inc(e_done, 1)
            act.wait_ge(w_done, 1)
            nc.scalar.activation(g["lnw"][:, :], g["w"][:, :], ACT.Ln).then_inc(ln_done, 1)
            for i in range(RR):
                copy_row(i)
            act.wait_ge(turned, 1)
            for i in range(CL // P):
                nc.scalar.activation(keep.neg_half[:, :, i::CL // P],
                                     pn[i][:, :].rearrange("p (r c) -> p r c", r=PAIRS), ACT.Copy, scale=-1.0)
            for i in range(RR, len(chunks)):
                copy_row(i)

        @block.vector
        def _(dve):
            c = Chain(dve, chain)
            c.link(nc.vector.memset(one[:, :], 1.0))
            dve.wait_ge(x_in, 16)
            c.link(nc.vector.tensor_scalar(g["x"][:, :], g["x"][:, :], GATE_BIAS, None, ALU.add))
            nc.vector.scalar_tensor_tensor(g["mag"][:, :], g["x"][:, :], -1.0, g["x"][:, :], ALU.mult, ALU.max).then_inc(mag_done, 1)
            dve.wait_ge(e_done, 1)
            nc.vector.tensor_scalar(g["w"][:, :], g["e"][:, :], 1.0, None, ALU.add).then_inc(w_done, 1)
            dve.wait_ge(w_done, 1)
            c.link(nc.vector.reciprocal(inv[:, :], g["w"][:, :]))
            c.link(nc.vector.scalar_tensor_tensor(g["u"][:, :], g["w"][:, :], -1.0, g["e"][:, :], ALU.add, ALU.subtract))
            c.link(nc.vector.tensor_tensor(g["u"][:, :], g["u"][:, :], inv[:, :], ALU.mult))
            dve.wait_ge(ln_done, 1)
            c.link(nc.vector.tensor_tensor(g["u"][:, :], g["u"][:, :], g["lnw"][:, :], ALU.subtract))
            c.link(nc.vector.scalar_tensor_tensor(g["u"][:, :], g["x"][:, :], 0.0, g["u"][:, :], ALU.min, ALU.add))
            c.link(nc.vector.tensor_scalar(g["u"][:, :], g["u"][:, :], 0.5, None, ALU.mult))
            c.link(nc.vector.tensor_tensor_scan(g["mag"][:, :], one[:, :], g["u"][:, :], 0.0, ALU.mult, ALU.add))
            nc.vector.tensor_copy(tot[:, :], g["mag"][:, CL - 1:CL]).then_inc(scan_done, 1)
            dve.wait_ge(carry_mm, 1)
            c.link(nc.vector.tensor_copy(tot[:, :], pt[:, :]))
            nc.vector.tensor_scalar(g["sc"][:, :], g["mag"][:, :], tot[:, :], None, ALU.add).then_inc(sum_done, 1)

        @block.tensor
        def _(pe):
            def row(i):
                b, n = chunks[i]
                if i >= RR:
                    pe.wait_ge(row_done, i - RR + 1)
                for k in range(KD):
                    last = nc.tensor.matmul(pr[i % RR][:, :], rows.silu[:, b, k, :], rows.w[:, k, n * RW:(n + 1) * RW],
                                            start=(k == 0), stop=(k == KD - 1))
                last.then_inc(row_mm, 1)

            pe.wait_ge(rows.w_in, 16)
            for i in range(RR):
                row(i)
            pe.wait_ge(scan_done, 1)
            nc.tensor.matmul(pt[:, :], keep.before[:, :], tot[:, :], start=True, stop=True).then_inc(carry_mm, 1)
            pe.wait_ge(sum_done, 1)
            for i in range(CL // P):
                last = nc.tensor.transpose(pn[i][:, :], g["sc"][:, i * P:(i + 1) * P], keep.ident[:, :])
            last.then_inc(turned, 1)
            for i in range(RR, len(chunks)):
                row(i)


LATE = (2, 1)
LATE_AT = (3, 6)
OWN_0_AT = (5, 7, 9, 11)
OWN_3_AT = 2
MAX_0_AT = 5
MAX_3_AT = 1
SQUARES = 8
AHEAD = 3
LAG = 6.5
GUARD = 1e-15


def attention_steps():
    off = {i: [("off", i, s) for s in range(ST * i)] for i in range(1, NB)}
    diag = {i: [("diag", i, j) for j in range(ST)] for i in range(NB)}
    steps = []
    for n, st in enumerate(off[3]):
        if n in LATE_AT:
            steps.append(("max", LATE[LATE_AT.index(n)], 0))
        steps.append(st)
        if n in OWN_0_AT:
            steps.append(diag[0][OWN_0_AT.index(n)])
    for n, st in enumerate(off[2]):
        steps.append(st)
        if OWN_3_AT <= n < OWN_3_AT + ST:
            steps.append(diag[3][n - OWN_3_AT])
        if n == MAX_0_AT:
            steps.append(("max", 0, 0))
    for n, st in enumerate(off[1]):
        steps.append(st)
        steps.append(diag[2][n])
        if n == MAX_3_AT:
            steps.append(("max", 3, 0))
    return steps + diag[1]


def attend(nc, keep, first, q_rows, k_rows, v_cent, half_log, num_rows):
    steps = attention_steps()
    N = len(steps)
    squares = [n for n in range(N) if steps[n][0] != "max"]
    diags = [n for n in range(N) if steps[n][0] == "diag"]
    maxes = [n for n in range(N) if steps[n][0] == "max"]
    sq_of = {n: g for g, n in enumerate(squares)}
    mul_of = {n: d for d, n in enumerate(diags)}
    m_of = {n: r for r, n in enumerate(maxes)}
    NS, ND = len(squares), len(diags)

    def due(n):
        d = n + (AHEAD + 0.5 if steps[n][0] == "off" else LAG)
        return min(d if int(d) % 2 else d + 1, N + AHEAD - 0.7)

    use_order = sorted(squares, key=lambda n: (due(n), n))
    use_of = {n: u for u, n in enumerate(use_order)}
    done_order = (0, 3, 2, 1)
    done_of = {i: d for d, i in enumerate(done_order)}
    last_off = {i: n for n in range(N) for k, i, _ in [steps[n]] if k == "off"}
    last_use = {i: n for n in use_order for k, i, _ in [steps[n]]}
    after = {n: [] for n in range(N)}
    at = {st: n for n, st in enumerate(steps)}
    QCH = 1024
    QCN, KCN = 2 * T // QCH, 2
    for j in range(ST):
        after[at["off", 3, 1 + j]].append(("decay", 0, j))
        after[at[("off", 3, 6 + 2 * j) if j < 3 else ("off", 2, 1)]].append(("decay", 3, j))
        after[at["off", 2, 4 + j]].append(("decay", 2, j))
        after[at[("off", 1, 1 + j) if j < 3 else ("diag", 2, 3)]].append(("decay", 1, j))
    for c in range(KCN):
        after[at["off", 3, 9 + 2 * c]].append(("split_k", c))
    for c in range(QCN):
        after[at["off", 2, c]].append(("split_q", c))
    after[at["off", 1, 3]].append(("factors",))
    A, R, SR = SQUARES, 3, 3
    HI, LO = QCN + KCN, QCN + KCN
    decay_base = {0: 0, 3: ST, 2: 2 * ST, 1: 3 * ST}
    assert N % 2 == 0 and NS % A == 0 and list(decay_base) == list(done_order)
    assert all(sq_of[n] < sq_of[k] for n, k in zip(diags, diags[1:]))

    def et_slot(i, p):
        return (NB - 1 - i + p) % 2

    def slot(n):
        return n % SR

    def slot_before(n):
        return (n - SR, 0) if n >= SR else (max(k for k in range(N) if slot(k) == slot(n)), 1)

    def own_slot(i):
        return done_of[i] % 2

    def acc_slot(i, p):
        return {3: (0, 0), 0: (1, 2), 2: (2, 1), 1: (1, 2)}[i][p]

    with ExitStack() as ctx:
        m = Program(nc, ctx, "att")
        q_sb = [first.q, m.sbuf("q1", [P, 2 * T])]
        k_sb = [first.k, m.sbuf("k1", [P, 2, T])]
        v_sb = [first.v, m.sbuf("v1", [P, NT, HD])]
        hb = [m.sbuf(f"hb{i}", [P, T]) for i in range(2)]
        nh = m.sbuf("nh", [P, 2, NT])
        nfull = m.sbuf("nfull", [P, 2, NT])
        f = m.sbuf("f", [P, 2, NB - 1, NT - ST])
        fg = m.sbuf("fg", [P, 2, NB - 1, NT - ST])
        neg2 = m.sbuf("neg2", [P, 2, NB])
        guard = m.sbuf("guard", [P, 1])
        head = m.sbuf("head", [P, 2, QCH], F32R)
        et = m.sbuf("et", [P, 2, TB])
        dec = m.sbuf("dec", [P, 2, ST, TB])
        a = m.sbuf("a", [P, A, 2, TB])
        acc = m.sbuf("acc", [P, R, 2, TB])
        part = m.sbuf("part", [P, 2, TB])
        num = m.sbuf("num", [P, 2, TB])
        s_ps = [m.psum(f"s{i}", [P, 2, TB]) for i in range(SR)]
        off_ps = m.psum("off", [P, TB])
        own_ps = m.psum("own", [P, TB])
        guard_done, share_done = m.sem("guard"), m.sem("share")
        pair_in = [first.pair_in, m.sem("pair_in1")]
        num_st = [m.sem(f"num_st{i}") for i in range(2)]
        up_done, hi_done, lo_done, prep_done, et_done, exp_done, dec_done = (m.sem(s) for s in ("up", "hi", "lo", "prep", "et", "exp", "dec"))
        s_done, sq_done, mul_done, av_done, max_done, row_done, num_done, scaled, part_done = (
            m.sem(s) for s in ("s", "sq", "mul", "av", "max", "row", "num", "scaled", "part"))
        block = ctx.enter_context(nc.Block())

        @block.sync
        def _(sp):
            for i in range(2):
                sp.sem_inc(num_st[i], 1)

            def load_logs(q, p):
                sp.dma_start(hb[p][:, :], half_log[q, None, :].to_broadcast([P, T])).then_inc(pair_in[p], 16)

            load_logs(0, 0)
            with sp.Fori(0, PAIRS // 2) as it:
                for p in range(2):
                    q = it * 2 + p
                    sp.wait_ge(av_done, ready(q * NS - 1))
                    sp.wait_ge(lo_done, ready(q * LO + LO - 1))
                    apart(sp, keep)
                    after_it = (q + 1) % PAIRS
                    load_pair(sp, after_it // KVH, after_it % KVH, q_rows, k_rows, v_cent, q_sb[1 - p], k_sb[1 - p], v_sb[1 - p], pair_in[1 - p])
                    load_logs(after_it, 1 - p)
                    for d, i in enumerate(done_order):
                        sp.wait_ge(num_done, ready(q * NB + d))
                        apart(sp, keep)
                        sp.dma_start(num_rows[q, :, i * TB:(i + 1) * TB], num[:, d % 2, :]).then_inc(num_st[d % 2], 16)
            for i in range(2):
                sp.wait_ge(num_st[i], 1 + 16 * PAIRS * NB // 2)

        def queries(p, c):
            return q_sb[p][:, c * QCH:(c + 1) * QCH]

        def keys(p, hl, c):
            return k_sb[p][:, hl, c * (T // KCN):(c + 1) * (T // KCN)]

        def split_up(q, p, what, c):
            if what == "split_q":
                nc.scalar.wait_ge(lo_done, ready(q * LO + KCN + c - 2 if c >= 2 else (q - 1) * LO + KCN + QCN - 2 + c))
                nc.scalar.activation(head[HD:P, c % 2, :], queries(p, c)[HD:P, :], ACT.Copy).then_inc(up_done, 1)

        def split_hi(p, what, c):
            if what == "split_k":
                nc.vector.tensor_copy(keys(p, 0, c).bitcast(F32R), keys(p, 1, c)).then_inc(hi_done, 1)
            else:
                nc.vector.tensor_copy(queries(p, c)[0:HD, :].bitcast(F32R), queries(p, c)[0:HD, :]).then_inc(hi_done, 1)

        def split_lo(q, p, what, c):
            if what == "split_k":
                nc.gpsimd.wait_ge(hi_done, ready(q * HI + c))
                nc.gpsimd.tensor_tensor(keys(p, 1, c).bitcast(F32R), keys(p, 1, c), keys(p, 0, c), ALU.subtract).then_inc(lo_done, 1)
            else:
                nc.gpsimd.wait_ge(hi_done, ready(q * HI + KCN + c))
                nc.gpsimd.wait_ge(up_done, ready(q * QCN + c))
                nc.gpsimd.tensor_tensor(queries(p, c).bitcast(F32R), queries(p, c), head[:, c % 2, :].bitcast(F32),
                                        ALU.subtract).then_inc(lo_done, 1)

        FIRST_HI = [("split_q", 0), ("split_k", 0), ("split_q", 1), ("split_q", 2), ("split_k", 1), ("split_q", 3)]
        FIRST_LO = [("split_q", 0), ("split_k", 0), ("split_q", 2)]
        FIRST_LO_DVE = [("split_q", 1), ("split_k", 1), ("split_q", 3)]

        def first_lo(eng, v, what, c):
            eng.wait_ge(hi_done, ready(FIRST_HI.index((what, c))))
            if what == "split_k":
                return v.tensor_tensor(keys(0, 1, c).bitcast(F32R), keys(0, 1, c), keys(0, 0, c), ALU.subtract)
            eng.wait_ge(up_done, ready(c))
            return v.tensor_tensor(queries(0, c).bitcast(F32R), queries(0, c), head[:, c % 2, :].bitcast(F32), ALU.subtract)

        parts = [("split_k", c) for c in range(KCN)] + [("split_q", c) for c in range(QCN)]

        @block.gpsimd
        def _(pool):
            for s in (dec_done, mul_done, lo_done):
                pool.sem_inc(s, CREDIT)
            nc.gpsimd.memset(head[:, :, :].bitcast(F32), 0.0)
            nc.gpsimd.memset(guard[:, :], GUARD).then_inc(guard_done, 1)

            def mask(q, i, j):
                pool.wait_ge(exp_done, ready(q * ND + decay_base[i] + j))
                apart(pool, keep)
                tile = dec[:, own_slot(i), j, 0:P]
                nc.gpsimd.affine_select(out=tile, in_=tile, compare_op=ALU.is_ge, fill=0.0, base=0,
                                        pattern=[[1, P]], channel_multiplier=-1).then_inc(dec_done, 1)

            for what in FIRST_LO:
                first_lo(pool, nc.gpsimd, *what).then_inc(lo_done, 1)
            pool.wait_ge(share_done, len(FIRST_LO_DVE))
            pool.sem_inc(lo_done, len(FIRST_LO_DVE))
            with pool.Fori(0, PAIRS // 2) as it:
                for p in range(2):
                    q = it * 2 + p
                    for n in range(N):
                        kind, i, j = steps[n]
                        if kind == "diag":
                            g = sq_of[n]
                            pool.wait_ge(dec_done, ready(q * ND + decay_base[i] + j))
                            pool.wait_ge(sq_done, ready(q * NS + g))
                            x = a[:, g % A, :, j * P:TB]
                            nc.gpsimd.tensor_tensor(x, x, dec[:, own_slot(i), j, None, 0:TB - j * P].to_broadcast([P, 2, TB - j * P]),
                                                    ALU.mult).then_inc(mul_done, 1)
                        for what in after[n]:
                            if what[0] == "decay":
                                mask(q, *what[1:])
                            elif what in parts:
                                split_lo(q + 1, 1 - p, *what)

        @block.scalar
        def _(act):
            for s in (up_done, prep_done, et_done, exp_done, sq_done):
                act.sem_inc(s, CREDIT)

            def factors(q, p):
                k = q % PAIRS
                nc.scalar.activation(nh[:, p, :], keep.neg_half[:, k, :], ACT.Copy)
                nc.scalar.activation(nfull[:, p, :], keep.neg_half[:, k, :], ACT.Copy, scale=2.0).then_inc(prep_done, 1)
                act.wait_ge(prep_done, ready(q * 3))
                for i in range(1, NB):
                    last = nc.scalar.activation(f[:, p, i - 1, 0:ST * i], nh[:, p, 0:ST * i], ACT.Exp,
                                                bias=hb[p][:, i * TB:i * TB + 1])
                last.then_inc(prep_done, 1)
                act.wait_ge(prep_done, ready(q * 3 + 1))
                for i in range(1, NB):
                    nc.scalar.activation(fg[:, p, i - 1, 0:ST * i], f[:, p, i - 1, 0:ST * i], ACT.Copy, scale=GUARD)
                nc.scalar.activation(neg2[:, p, :], hb[p][:, 0::TB], ACT.Copy, scale=-2.0).then_inc(prep_done, 1)

            def query_factor(q, p, i):
                act.wait_ge(prep_done, ready(q * 3 + 2))
                act.wait_ge(part_done, free(q * (NB - 1) + NB - 1 - i + 1, 2))
                act.wait_ge(scaled, free(q * (NB - 1) + NB - 1 - i, 2))
                nc.scalar.activation(et[:, et_slot(i, p), :], hb[p][:, i * TB:(i + 1) * TB], ACT.Exp, scale=2.0,
                                     bias=neg2[:, p, i:i + 1]).then_inc(et_done, 1)

            def decay(q, p, i, j):
                d = decay_base[i]
                if j == 0:
                    act.wait_ge(mul_done, ready(q * ND + d - ST - 1))
                w = TB - j * P
                nc.scalar.activation(dec[:, own_slot(i), j, 0:w], hb[p][:, i * TB + j * P:(i + 1) * TB], ACT.Exp,
                                     scale=2.0, bias=nfull[:, p, i * ST + j:i * ST + j + 1]).then_inc(exp_done, 1)

            act.wait_ge(guard_done, 1)
            act.wait_ge(pair_in[0], 80)
            for c in range(QCN):
                if c == 2:
                    act.wait_ge(lo_done, ready(FIRST_LO.index(("split_q", 0))))
                if c == 3:
                    act.wait_ge(share_done, FIRST_LO_DVE.index(("split_q", 1)) + 1)
                nc.scalar.activation(head[HD:P, c % 2, :], queries(0, c)[HD:P, :], ACT.Copy).then_inc(up_done, 1)
            act.wait_ge(pair_in[0], 96)
            factors(0, 0)
            act.wait_ge(prep_done, ready(2))
            with act.Fori(0, PAIRS // 2) as it:
                for p in range(2):
                    q = it * 2 + p
                    for n in range(N):
                        kind, i, s = steps[n]
                        if kind != "max":
                            g = sq_of[n]
                            last = use_of[squares[(g - A) % NS]] + (q if g >= A else q - 1) * NS
                            act.wait_ge(av_done, ready(last))
                            act.wait_ge(max_done, ready(last))
                            act.wait_ge(s_done, ready(q * N + n))
                            if kind == "off":
                                nc.scalar.activation(a[:, g % A, :, :], s_ps[slot(n)][:, :, :], ACT.Square,
                                                     scale=f[:, p, i - 1, s:s + 1], bias=fg[:, p, i - 1, s:s + 1]).then_inc(sq_done, 1)
                                if s == 0:
                                    query_factor(q, p, i)
                            else:
                                nc.scalar.activation(a[:, g % A, :, s * P:TB], s_ps[slot(n)][:, :, s * P:TB], ACT.Square,
                                                     bias=guard[:, :]).then_inc(sq_done, 1)
                        for what in after[n]:
                            if what[0] == "decay":
                                decay(q, p, *what[1:])
                            elif what[0] == "factors":
                                factors(q + 1, 1 - p)
                                act.wait_ge(prep_done, ready((q + 1) * 3 + 2))
                            elif what in parts:
                                if what == parts[0]:
                                    act.wait_ge(pair_in[1 - p], it * 96 + 96 * (1 + p))
                                split_up(q + 1, 1 - p, *what)

        @block.vector
        def _(dve):
            for s in (hi_done, max_done, row_done, num_done, scaled, part_done):
                dve.sem_inc(s, CREDIT)
            dve.wait_ge(pair_in[0], 80)
            for what, c in FIRST_HI:
                split_hi(0, what, c)
            for what in FIRST_LO_DVE:
                first_lo(dve, nc.vector, *what).then_inc(share_done, 1)
            for i in range(R):
                last = nc.vector.memset(acc[:, i, :, :], 0.0)
            last.then_inc(part_done, 1)
            dve.wait_ge(part_done, CREDIT + 1)
            def maximum(q, p, n):
                kind, i, s = steps[n]
                g, u = sq_of[n], use_of[n]
                if kind == "off":
                    dve.wait_ge(sq_done, ready(q * NS + g))
                else:
                    dve.wait_ge(mul_done, ready(q * ND + mul_of[n]))
                x = acc[:, acc_slot(i, p), :, :]
                c = s * P if kind == "diag" else 0
                if s == 0 and (kind == "off" or i == 0):
                    nc.vector.tensor_copy(x, a[:, g % A, :, :]).then_inc(max_done, 1)
                else:
                    before = max(use_of[k] for k in squares if steps[k][1] == i and use_of[k] < u)
                    dve.wait_ge(max_done, ready(q * NS + before))
                    if kind == "diag" and s == 0:
                        dve.wait_ge(scaled, ready(q * (NB - 1) + NB - 1 - i))
                    nc.vector.tensor_tensor(x[:, :, c:TB], x[:, :, c:TB], a[:, g % A, :, c:TB], ALU.max).then_inc(max_done, 1)
                if last_off.get(i) == n:
                    dve.wait_ge(max_done, ready(q * NS + u))
                    dve.wait_ge(et_done, ready(q * (NB - 1) + NB - 1 - i))
                    nc.vector.tensor_tensor(x, x, et[:, et_slot(i, p), None, :].to_broadcast([P, 2, TB]), ALU.mult).then_inc(scaled, 1)

            def before_own(q, p, i):
                dve.wait_ge(av_done, ready(q * NS + use_of[last_off[i]]))
                dve.wait_ge(et_done, ready(q * (NB - 1) + NB - 1 - i))
                dve.wait_ge(num_done, ready((q * NB + done_of[i] - 2) if done_of[i] > 1 else (q - 1) * NB + 2))
                nc.vector.tensor_tensor(part[:, et_slot(i, p), :], off_ps[:, :], et[:, et_slot(i, p), :], ALU.mult).then_inc(part_done, 1)

            def total(q, p, i):
                d = done_of[i]
                dve.wait_ge(av_done, ready(q * NS + use_of[last_use[i]]))
                dve.wait_ge(num_st[d % 2], (q * (NB // 2) + d // 2) * 16 + 1)
                if i == 0:
                    nc.vector.tensor_copy(num[:, d % 2, :], own_ps[:, :]).then_inc(num_done, 1)
                else:
                    dve.wait_ge(part_done, ready(q * (NB - 1) + d))
                    nc.vector.tensor_tensor(num[:, d % 2, :], part[:, et_slot(i, p), :], own_ps[:, :], ALU.add).then_inc(num_done, 1)

            def rows(q, n, pair):
                i = steps[n][1]
                dve.wait_ge(s_done, ready(q * N + n))
                apart(dve, keep)
                nc.vector.tensor_reduce(keep.row_max[:, pair, i * ST:(i + 1) * ST, :].rearrange("p c h -> p h c"),
                                        s_ps[slot(n)][:, :, :].rearrange("p h (c k) -> p h c k", k=P), AX.X, ALU.max).then_inc(row_done, 1)

            todo = [(due(n), 0, n) for n in use_order]
            todo += [(due(last_use[i]) + 0.1, 1, i) for i in range(NB)]
            todo += [(due(last_off[i]) + 0.05, 4, i) for i in range(1, NB)]
            todo += [(n + 0.6, 2, n) for n in maxes]
            todo += [(n + 1.4, 3, what) for n in range(N) for what in after[n] if what in parts]
            todo.sort()
            with dve.Fori(0, PAIRS // 2) as it:
                for p in range(2):
                    q = it * 2 + p
                    for _, what, x in todo:
                        if what == 0:
                            maximum(q, p, x)
                        elif what == 1:
                            total(q, p, x)
                        elif what == 4:
                            before_own(q, p, x)
                        elif what == 3:
                            if x == parts[0]:
                                dve.wait_ge(pair_in[1 - p], it * 96 + 96 * (1 + p))
                            split_hi(1 - p, *x)
                        else:
                            rows(q, x, (q + PAIRS - 1) % PAIRS if steps[x][1] in LATE else q)
            for k, i in enumerate(LATE):
                dve.wait_ge(s_done, ready(PAIRS * N + AHEAD + k))
                nc.vector.tensor_reduce(keep.row_max[:, PAIRS - 1, i * ST:(i + 1) * ST, :].rearrange("p c h -> p h c"),
                                        s_ps[k][:, :, :].rearrange("p h (c k) -> p h c k", k=P), AX.X, ALU.max).then_inc(row_done, 1)

        @block.tensor
        def _(pe):
            for s in (s_done, av_done):
                pe.sem_inc(s, CREDIT)

            def turn_maxima(s, ring):
                for h in range(2):
                    for c in range(ST):
                        last = nc.tensor.transpose(s_ps[s][:, h, c * P:(c + 1) * P],
                                                   acc[:, ring, h, c * P:(c + 1) * P], keep.ident[:, :])
                last.then_inc(s_done, 1)

            def scores(q, p, n):
                kind, i, s = steps[n]
                k, back = slot_before(n)
                if steps[k][0] == "max":
                    pe.wait_ge(row_done, ready((q - back) * NB + m_of[k]))
                else:
                    pe.wait_ge(sq_done, ready((q - back) * NS + sq_of[k]))
                if kind == "max":
                    if i in LATE:
                        pe.wait_ge(max_done, ready((q - 1) * NS + use_of[last_use[i]]))
                        turn_maxima(slot(n), acc_slot(i, 1 - p))
                    else:
                        pe.wait_ge(max_done, ready(q * NS + use_of[last_use[i]]))
                        turn_maxima(slot(n), acc_slot(i, p))
                    return
                if n == 0:
                    pe.wait_ge(lo_done, ready(q * LO + LO - 1))
                key = s if kind == "off" else i * ST + s
                c = 0 if kind == "off" else s * P
                for h in range(2):
                    for hl in range(2):
                        last = nc.tensor.matmul(s_ps[slot(n)][:, h, c:TB],
                                                k_sb[p][:, hl, key * P:(key + 1) * P].bitcast(F32R),
                                                q_sb[p][:, h * T + i * TB + c:h * T + (i + 1) * TB].bitcast(F32R),
                                                start=(hl == 0), stop=(hl == 1))
                last.then_inc(s_done, 1)

            def values(q, p, n):
                kind, i, s = steps[n]
                g = sq_of[n]
                key = s if kind == "off" else i * ST + s
                c = 0 if kind == "off" else s * P
                if s == 0:
                    if kind == "diag":
                        pe.wait_ge(num_done, free(q * NB + done_of[i], 1))
                    else:
                        pe.wait_ge(part_done, free(q * (NB - 1) + done_of[i], 1))
                if kind == "off":
                    pe.wait_ge(sq_done, ready(q * NS + g))
                else:
                    pe.wait_ge(mul_done, ready(q * ND + mul_of[n]))
                ps = off_ps if kind == "off" else own_ps
                for h in range(2):
                    last = nc.tensor.matmul(ps[h * HD:(h + 1) * HD, c:TB], v_sb[p][:, key, :], a[:, g % A, h, c:TB],
                                            start=(s == 0), stop=(s == (ST * i if kind == "off" else ST) - 1))
                last.then_inc(av_done, 1)

            todo = [(n, 0, n) for n in range(AHEAD, N)] + [(N + n, 1, n) for n in range(AHEAD)]
            todo += [(due(n), 2, n) for n in use_order]
            todo.sort()
            assert todo[0][1] == 0 or todo[0][0] > AHEAD - 1
            for n in range(AHEAD):
                scores(0, 0, n)
            pe.wait_ge(part_done, CREDIT + 1)
            with pe.Fori(0, PAIRS // 2) as it:
                for p in range(2):
                    q = it * 2 + p
                    for _, what, n in todo:
                        if what == 0:
                            scores(q, p, n)
                        elif what == 1:
                            scores(q + 1, 1 - p, n)
                        else:
                            values(q, p, n)
            pe.wait_ge(max_done, ready(PAIRS * NS - 1))
            for k, i in enumerate(LATE):
                turn_maxima(k, acc_slot(i, 1))


def close_attention(nc, keep, x, w_proj, ln_w, w_router, basis, num_rows, h2_rows):
    with ExitStack() as ctx:
        m = Program(nc, ctx, "close")
        w_raw = m.sbuf("w_raw", [P, KVH, D])
        w = m.sbuf("w", [P, KVH, D])
        basis_sb = m.sbuf("basis", [P, P])
        lnw = m.sbuf("lnw", [P, 1])
        wr = m.sbuf("wr", [P, KD, E])
        wr_raw = m.sbuf("wr_raw", [E, D])
        nT = m.sbuf("nT", [P, 2, KVH, P])
        xt = m.sbuf("xt", [P, 2, D])
        num = m.sbuf("num", [P, 2, HEADS, HD])
        sq = m.sbuf("sq", [P, HEADS, HD - 1])
        red = m.sbuf("red", [P, 5, HEADS])
        rinv = m.sbuf("rinv", [P, 2, HEADS])
        y = m.sbuf("y", [P, 2, HEADS, HD])
        yT = m.sbuf("yT", [P, 2, KVH, P])
        gx = m.sbuf("gx", [P, 2, D])
        st6 = m.sbuf("st6", [P, 6])
        mv = m.sbuf("mv", [P, 2, 2])
        rs = m.sbuf("rs", [P, 2, 2])
        xn = m.sbuf("xn", [P, 2, D])
        hs = m.sbuf("hs", [P, 2, D])
        h_st = m.sbuf("h_st", [P, 2, D])
        hT = m.sbuf("hT", [P, 2, KD, P])
        eps = m.sbuf("eps", [P, 1])
        pn = m.psum("pn", [P, HEADS, HD])
        py = m.psum("py", [P, KVH, P])
        pa = m.psum("pa", [P, D])
        ph = m.psum("ph", [P, KD, P])
        pl = m.psum("pl", [P, E])
        pw = m.psum("pw", [P, 2, D])
        w_in, scaled, fold_mm, folded, wr_mm, wr_done, eps_done = (
            m.sem(s) for s in ("w_in", "scaled", "fold_mm", "folded", "wr_mm", "wr", "eps"))
        n_in = [m.sem(f"n_in{i}") for i in range(2)]
        x_in = [m.sem(f"x_in{i}") for i in range(2)]
        h_out = [m.sem(f"h_out{i}") for i in range(2)]
        n_mm, num_done, sq_done, var_done, std_done, r_done, y_done, y_mm, yT_done, a_mm = (
            m.sem(s) for s in ("n_mm", "num", "sq", "var", "std", "r", "y", "y_mm", "yT", "a_mm"))
        gx_done, x1_done, var2_done, std2_done, xn_done, hs_done, h2_done, h_mm, hT_done, l_mm, l_done, head_chain, norm_chain, mod_chain = (
            m.sem(s) for s in ("gx", "x1", "var2", "std2", "xn", "hs", "h2", "h_mm", "hT", "l_mm", "l", "head_chain", "norm_chain", "mod_chain"))
        ROW_OPS = 9
        x_t = x.rearrange("b (t p) d -> (b t) p d", p=P)
        num_t = num_rows.rearrange("(b j) p (t c) -> b t p j c", j=KVH, c=P)
        block = ctx.enter_context(nc.Block())

        def turns(eng, turn, fold=None):
            LAST = 7
            for n in range(LAST + 1):
                turn(n, n % 2, [n >= lag for lag in range(LAST + 1)])
                if fold and n < 3:
                    fold(((0, 1), (2,), (3,))[n])
            with eng.Fori((LAST + 1) // 2, NTT // 2) as it:
                for p in range(2):
                    turn(it * 2 + p, p, [True] * (LAST + 1))
            for n in range(NTT, NTT + LAST):
                turn(n, n % 2, [n - lag < NTT for lag in range(LAST + 1)])

        @block.sync
        def _(sp):
            for p in range(2):
                sp.sem_inc(h_out[p], 1)
                sp.sem_inc(n_in[p], 1)
                sp.sem_inc(x_in[p], 1)
                sp.dma_start(nT[:, p, :, :], num_t[0, p]).then_inc(n_in[p], 16)
                sp.dma_start(xt[:, p, :], x_t[p]).then_inc(x_in[p], 16)
            sp.dma_start(w_raw[:, :, :], w_proj.rearrange("(j p) n -> p j n", p=P)).then_inc(w_in, 16)
            sp.dma_start(basis_sb[:, :], basis).then_inc(w_in, 16)
            for h in range(2):
                sp.dma_start(lnw[h * HD:(h + 1) * HD, :], ln_w.rearrange("(d o) -> d o", o=1)).then_inc(w_in, 16)
            sp.dma_start(wr_raw[:, :], w_router).then_inc(w_in, 16)

            def turn(n, p, there):
                if there[0]:
                    m_ = (n + 2) % NTT
                    sp.wait_ge(n_mm, ready(n))
                    apart(sp, keep)
                    sp.dma_start(nT[:, p, :, :], num_t[m_ // NT, m_ % NT]).then_inc(n_in[p], 16)
                if there[5]:
                    sp.wait_ge(h2_done, ready(n - 5))
                    apart(sp, keep)
                    sp.dma_start(h2_rows[n - 5], h_st[:, 1 - p, :]).then_inc(h_out[1 - p], 16)
                if there[4]:
                    sp.wait_ge(x1_done, ready(n - 4))
                    apart(sp, keep)
                    sp.dma_start(xt[:, p, :], x_t[(n - 2) % NTT]).then_inc(x_in[p], 16)

            turns(sp, turn)
            for p in range(2):
                sp.wait_ge(h_out[p], 1 + 16 * (NTT // 2))
                sp.wait_ge(n_in[p], 1 + 16 * (NTT // 2 + 1))
                sp.wait_ge(x_in[p], 1 + 16 * (NTT // 2 + 1))

        @block.scalar
        def _(act):
            for s in (sq_done, std_done, yT_done, std2_done, hT_done):
                act.sem_inc(s, CREDIT)
            act.wait_ge(eps_done, 1)

            def turn(n, p, there):
                if there[7]:
                    act.wait_ge(h_mm, ready(n - 7))
                    act.wait_ge(l_mm, free(n - 7, 2))
                    nc.scalar.activation(hT[:, 1 - p, :, :], ph[:, :, :], ACT.Copy).then_inc(hT_done, 1)
                if there[2]:
                    act.wait_ge(y_mm, ready(n - 2))
                    act.wait_ge(a_mm, free(n - 2, 2))
                    nc.scalar.activation(yT[:, p, :, :], py[:, :, :], ACT.Copy).then_inc(yT_done, 1)
                if there[0]:
                    act.wait_ge(num_done, ready(n))
                    act.wait_ge(var_done, free(n, 1))
                    nc.scalar.activation(sq[:, :, :], num[:, p, :, 0:HD - 1], ACT.Square).then_inc(sq_done, 1)
                if there[5]:
                    act.wait_ge(var2_done, ready(n - 5))
                    nc.scalar.activation(rs[:, 1 - p, 0:1], mv[:, 1 - p, 1:2], ACT.Sqrt, bias=eps[:, 0:1]).then_inc(std2_done, 1)
                if there[0]:
                    act.wait_ge(var_done, ready(n))
                    nc.scalar.activation(red[:, 4, :], red[:, 3, :], ACT.Sqrt).then_inc(std_done, 1)

            turns(act, turn)

        @block.gpsimd
        def _(pool):
            for s in (y_done, x1_done, hs_done, h2_done):
                pool.sem_inc(s, CREDIT)
            nc.gpsimd.memset(eps[:, 0:1], LN_EPS).then_inc(eps_done, 1)

            def turn(n, p, there):
                if there[4]:
                    pool.wait_ge(x_in[p], (n - 4) // 2 * 16 + 17)
                    pool.wait_ge(gx_done, ready(n - 4))
                    apart(pool, keep)
                    nc.gpsimd.tensor_tensor(keep.x1[:, n - 4, :], xt[:, p, :], gx[:, p, :], ALU.add).then_inc(x1_done, 1)
                if there[5]:
                    b = (n - 5) // NT
                    pool.wait_ge(mod_chain, ROW_OPS * B)
                    pool.wait_ge(xn_done, ready(n - 5))
                    apart(pool, keep)
                    nc.gpsimd.tensor_tensor(hs[:, 1 - p, :], xn[:, 1 - p, :], keep.mod[:, b, 4, :], ALU.mult).then_inc(hs_done, 1)
                    pool.wait_ge(hs_done, ready(n - 5))
                    pool.wait_ge(h_mm, free(n - 5, 2))
                    pool.wait_ge(h_out[1 - p], (n - 5) // 2 * 16 + 1)
                    apart(pool, keep)
                    nc.gpsimd.tensor_tensor(h_st[:, 1 - p, :], hs[:, 1 - p, :], keep.mod[:, b, 3, :], ALU.add).then_inc(h2_done, 1)
                if there[0]:
                    pool.wait_ge(r_done, ready(n))
                    pool.wait_ge(y_mm, free(n, 2))
                    nc.gpsimd.tensor_tensor(y[:, p, :, :], num[:, p, :, :], rinv[:, p, :, None].to_broadcast([P, HEADS, HD]),
                                            ALU.mult).then_inc(y_done, 1)

            turns(pool, turn)

        @block.vector
        def _(dve):
            for s in (num_done, var_done, r_done, gx_done, var2_done, xn_done, l_done):
                dve.sem_inc(s, CREDIT)

            def complete(b):
                c = Chain(dve, mod_chain, b * ROW_OPS)
                c.link(nc.vector.tensor_scalar(keep.mod[:, b, 4, :], keep.mod[:, b, 4, :], 1.0, None, ALU.add))
                for g in (2, 5):
                    c.link(nc.vector.tensor_scalar(keep.sign[:, :], keep.mod[:, b, g, :], 0.0, 2.0, ALU.is_ge, ALU.mult))
                    c.link(nc.vector.scalar_tensor_tensor(keep.mod[:, b, g, :], keep.mod[:, b, g, :], -1.0, keep.mod[:, b, g, :],
                                                          ALU.mult, ALU.max))
                    c.link(nc.vector.tensor_scalar(keep.mod[:, b, g, :], keep.mod[:, b, g, :], 0.25, None, ALU.max))
                    c.link(nc.vector.scalar_tensor_tensor(keep.mod[:, b, g, :], keep.sign[:, :], -1.0, keep.mod[:, b, g, :],
                                                          ALU.add, ALU.mult))
                assert c.n == ROW_OPS

            complete(0)

            def fold(parts):
                if parts[0] == 0:
                    dve.wait_ge(w_in, 80)
                    nc.vector.tensor_scalar(w_raw[:, :, :], w_raw[:, :, :], lnw[:, :], None, ALU.mult).then_inc(scaled, 1)
                for g in parts:
                    dve.wait_ge(fold_mm, g + 1)
                    nc.vector.tensor_copy(w[:, 2 * g:2 * g + 2, :], pw[:, :, :]).then_inc(folded, 1)
                if g == KVH // 2 - 1:
                    dve.wait_ge(wr_mm, 1)
                    nc.vector.tensor_copy(wr[:, :, :], ph[:, :, 0:E]).then_inc(wr_done, 1)
                    complete(1)

            HEAD_OPS, NORM_OPS = 3, 2

            def turn(n, p, there):
                head = Chain(dve, head_chain, n * HEAD_OPS)
                norm = Chain(dve, norm_chain, (n - 5) * NORM_OPS)
                if there[4]:
                    dve.wait_ge(a_mm, ready(n - 4))
                    dve.wait_ge(x1_done, free(n - 4, 2))
                    apart(dve, keep)
                    nc.vector.tensor_tensor(gx[:, p, :], pa[:, :], keep.mod[:, (n - 4) // NT, 2, :], ALU.mult).then_inc(gx_done, 1)
                if there[0]:
                    b, t = n // NT, n % NT
                    row_max = keep.row_max[:, bass.ds(b * KVH, KVH), t, :]
                    dve.wait_ge(n_mm, ready(n))
                    apart(dve, keep)
                    head.link(nc.vector.scalar_tensor_tensor(red[:, 0, :].rearrange("p (j h) -> p j h", h=2), row_max, 1e-6,
                                                             pn[:, :, HD - 1].rearrange("p (j h) -> p j h", h=2), ALU.mult, ALU.add))
                    head.link(nc.vector.reciprocal(red[:, 1, :], red[:, 0, :]))
                    dve.wait_ge(y_done, free(n, 2))
                    nc.vector.tensor_tensor(num[:, p, :, :], pn[:, :, :], red[:, 1, :, None].to_broadcast([P, HEADS, HD]),
                                            ALU.mult).then_inc(num_done, 1)
                if there[5]:
                    dve.wait_ge(x1_done, ready(n - 5))
                    apart(dve, keep)
                    norm.link(nc.vector.bn_stats(st6[:, :], keep.x1[:, n - 5, :]))
                    apart(dve, keep)
                    nc.vector.bn_aggr(mv[:, 1 - p, :], st6[:, :]).then_inc(var2_done, 1)
                if there[7]:
                    dve.wait_ge(l_mm, ready(n - 7))
                    apart(dve, keep)
                    nc.vector.tensor_copy(keep.logits[:, n - 7, :], pl[:, :]).then_inc(l_done, 1)
                if there[0]:
                    dve.wait_ge(sq_done, ready(n))
                    head.link(nc.vector.reduce_sum(red[:, 2, :], sq[:, :, :], AX.X))
                    nc.vector.tensor_scalar(red[:, 3, :], red[:, 2, :], 1.0 / HD, 1e-9, ALU.mult, ALU.add).then_inc(var_done, 1)
                    assert head.n == HEAD_OPS
                if there[5]:
                    dve.wait_ge(std2_done, ready(n - 5))
                    norm.link(nc.vector.reciprocal(rs[:, 1 - p, 1:2], rs[:, 1 - p, 0:1]))
                    dve.wait_ge(hs_done, free(n - 5, 2))
                    apart(dve, keep)
                    nc.vector.tensor_scalar(xn[:, 1 - p, :], keep.x1[:, n - 5, :], mv[:, 1 - p, 0:1], rs[:, 1 - p, 1:2],
                                            ALU.subtract, ALU.mult).then_inc(xn_done, 1)
                    assert norm.n == NORM_OPS
                if there[0]:
                    dve.wait_ge(std_done, ready(n))
                    nc.vector.reciprocal(rinv[:, p, :], red[:, 4, :]).then_inc(r_done, 1)

            turns(dve, turn, fold)

        @block.tensor
        def _(pe):
            for s in (n_mm, y_mm, a_mm, h_mm, l_mm):
                pe.sem_inc(s, CREDIT)

            def fold(parts):
                if parts[0] == 0:
                    pe.wait_ge(w_in, 80)
                    pe.wait_ge(scaled, 1)
                for g in parts:
                    if g:
                        pe.wait_ge(folded, g)
                    for i in range(2):
                        last = nc.tensor.matmul(pw[:, i, :], basis_sb[:, :], w_raw[:, 2 * g + i, :], start=True, stop=True)
                    last.then_inc(fold_mm, 1)
                if g == KVH // 2 - 1:
                    for k in range(KD):
                        last = nc.tensor.transpose(ph[:, k, 0:E], wr_raw[:, k * P:(k + 1) * P], keep.ident[0:E, 0:E])
                    last.then_inc(wr_mm, 1)
                    pe.wait_ge(folded, KVH // 2)
                    pe.wait_ge(wr_done, 1)

            def turn(n, p, there):
                if there[0]:
                    pe.wait_ge(n_in[p], n // 2 * 16 + 17)
                    pe.wait_ge(num_done, free(n, 1))
                    for j in range(KVH):
                        last = nc.tensor.transpose(pn[:, 2 * j:2 * j + 2, :], nT[:, p, j, :], keep.ident[:, :])
                    last.then_inc(n_mm, 1)
                if there[7]:
                    pe.wait_ge(hT_done, ready(n - 7))
                    pe.wait_ge(l_done, free(n - 7, 1))
                    for k in range(KD):
                        last = nc.tensor.matmul(pl[:, :], hT[:, 1 - p, k, :], wr[:, k, :], start=(k == 0), stop=(k == KD - 1))
                    last.then_inc(l_mm, 1)
                if there[2]:
                    pe.wait_ge(y_done, ready(n - 2))
                    pe.wait_ge(yT_done, free(n - 2, 1))
                    for j in range(KVH):
                        last = nc.tensor.transpose(py[:, j, :], y[:, p, 2 * j:2 * j + 2, :], keep.ident[:, :])
                    last.then_inc(y_mm, 1)
                if there[3]:
                    pe.wait_ge(yT_done, ready(n - 3))
                    pe.wait_ge(gx_done, free(n - 3, 1))
                    for j in range(KVH):
                        last = nc.tensor.matmul(pa[:, :], yT[:, 1 - p, j, :], w[:, j, :], start=(j == 0), stop=(j == KVH - 1))
                    last.then_inc(a_mm, 1)
                if there[6]:
                    pe.wait_ge(h2_done, ready(n - 6))
                    pe.wait_ge(hT_done, free(n - 6, 1))
                    for k in range(KD):
                        last = nc.tensor.transpose(ph[:, k, :], h_st[:, p, k * P:(k + 1) * P], keep.ident[:, :])
                    last.then_inc(h_mm, 1)

            turns(pe, turn, fold)


def choose(nc, keep, lanes, upto, total):
    SH = [P, NTT, E]
    FAR = float(1 << 20)
    with ExitStack() as ctx:
        m = Program(nc, ctx, "choose")
        tri_raw = m.sbuf("tri_raw", [P, P])
        tri = m.sbuf("tri", [P, P], F32R)
        one_r = m.sbuf("one_r", [P, P], F32R)
        ones = m.sbuf("ones", [P, P])
        ex = m.sbuf("ex", SH)
        pr = m.sbuf("pr", SH)
        tmp = m.sbuf("tmp", SH)
        hot = [m.sbuf(f"hot{i}", SH) for i in range(2)]
        match = m.sbuf("match", SH)
        elig = m.sbuf("elig", SH, F32R)
        kept = m.sbuf("kept", SH)
        place = m.sbuf("place", SH)
        r = {x: m.sbuf(x, [P, NTT]) for x in ("mx", "sum", "inv", "best", "s0", "s1", "run", "pos", "over", "keptk", "placek", "one")}
        lost = m.sbuf("lost", [P, 1])
        pos_ps = m.psum("pos", [P, NTT])
        tot_ps = m.psum("tot", [P, NTT])
        cnt_ps = m.psum("cnt", [P, 1])
        x1_st, c_in, diff_done, exp_done, elig_done, count_mm, lost_done, lost_mm, chain = (
            m.sem(s) for s in ("x1_st", "in", "diff", "exp", "elig", "count", "lost", "lost_mm", "chain"))
        block = ctx.enter_context(nc.Block())

        @block.sync
        def _(sp):
            sp.dma_start(tri_raw[:, :], upto).then_inc(c_in, 16)
            sp.dma_start(keep.lanes[:, :], lanes).then_inc(c_in, 16)
            rows = total.rearrange("(n p) d -> p n d", p=P)
            sp.dma_start(rows[:, 0:NTT, :], keep.x1[:, :, :]).then_inc(x1_st, 16)
            sp.dma_start(rows[:, NTT:, :], keep.x1[:, 0:CAP // P, :]).then_inc(x1_st, 16)
            sp.wait_ge(x1_st, 32)

        @block.scalar
        def _(act):
            act.wait_ge(diff_done, 1)
            nc.scalar.activation(ex[:, :, :], tmp[:, :, :], ACT.Exp).then_inc(exp_done, 1)

        @block.tensor
        def _(pe):
            for e in range(E):
                pe.wait_ge(elig_done, e + 1)
                nc.tensor.matmul(pos_ps[:, :], tri[:, :], elig[:, :, e], start=True, stop=True)
                nc.tensor.matmul(tot_ps[:, :], one_r[:, :], elig[:, :, e], start=True, stop=True).then_inc(count_mm, 1)
            pe.wait_ge(lost_done, 1)
            nc.tensor.matmul(cnt_ps[:, :], ones[:, :], lost[:, :], start=True, stop=True).then_inc(lost_mm, 1)

        @block.vector
        def _(dve):
            c = Chain(dve, chain)
            v = nc.vector

            def wide(x):
                return x[:, :, None].to_broadcast(SH)

            c.link(v.memset(ones[:, :], 1.0))
            c.link(v.memset(r["one"][:, :], 1.0))
            c.link(v.memset(keep.plain[:, :], 1.0))
            c.link(v.tensor_reduce(r["mx"][:, :], keep.logits[:, :, :], AX.X, ALU.max))
            v.tensor_tensor(tmp[:, :, :], keep.logits[:, :, :], wide(r["mx"]), ALU.subtract).then_inc(diff_done, 1)
            dve.wait_ge(exp_done, 1)
            c.link(v.reduce_sum(r["sum"][:, :], ex[:, :, :], AX.X))
            c.link(v.reciprocal(r["inv"][:, :], r["sum"][:, :]))
            c.link(v.tensor_tensor(pr[:, :, :], ex[:, :, :], wide(r["inv"]), ALU.mult))
            dve.wait_ge(c_in, 32)
            v.tensor_copy(tri[:, :], tri_raw[:, :])
            c.link(v.tensor_copy(one_r[:, :], ones[:, :]))
            lane = keep.lanes[:, None, 0:E].to_broadcast(SH)
            for k in range(2):
                s = r["s0"] if k == 0 else r["s1"]
                c.link(v.tensor_reduce(s[:, :], pr[:, :, :], AX.X, ALU.max))
                c.link(v.tensor_tensor(tmp[:, :, :], pr[:, :, :], wide(s), ALU.is_equal))
                c.link(v.scalar_tensor_tensor(tmp[:, :, :], lane, -float(E), tmp[:, :, :], ALU.add, ALU.mult))
                c.link(v.tensor_reduce(r["best"][:, :], tmp[:, :, :], AX.X, ALU.min))
                c.link(v.tensor_scalar(r["best"][:, :], r["best"][:, :], float(E), None, ALU.add))
                c.link(v.tensor_tensor(hot[k][:, :, :], lane, wide(r["best"]), ALU.is_equal))
                if k == 0:
                    c.link(v.tensor_scalar(tmp[:, :, :], hot[0][:, :, :], -1.0, 1.0, ALU.mult, ALU.add))
                    c.link(v.tensor_tensor(pr[:, :, :], pr[:, :, :], tmp[:, :, :], ALU.mult))
                    c.link(v.tensor_tensor(pr[:, :, :], pr[:, :, :], hot[0][:, :, :], ALU.subtract))
            c.link(v.tensor_tensor(match[:, :, :], hot[0][:, :, :], hot[1][:, :, :], ALU.add))
            c.link(v.tensor_tensor(r["sum"][:, :], r["s0"][:, :], r["s1"][:, :], ALU.add))
            c.link(v.tensor_scalar(r["sum"][:, :], r["sum"][:, :], 1e-9, None, ALU.max))
            c.link(v.reciprocal(r["inv"][:, :], r["sum"][:, :]))
            for s in ("s0", "s1"):
                c.link(v.tensor_tensor(r[s][:, :], r[s][:, :], r["inv"][:, :], ALU.mult))
            c.link(v.memset(r["run"][:, 0:1], 0.0))
            for e in range(E):
                v.tensor_tensor(elig[:, :, e], match[:, :, e], keep.plain[:, :], ALU.mult).then_inc(elig_done, 1)
                dve.wait_ge(count_mm, e + 1)
                c.link(v.tensor_tensor_scan(r["run"][:, 1:], r["one"][:, 1:], tot_ps[:, 0:NTT - 1], 0.0, ALU.mult, ALU.add))
                c.link(v.scalar_tensor_tensor(place[:, :, e], pos_ps[:, :], -1.0, r["run"][:, :], ALU.add, ALU.add))
                c.link(v.scalar_tensor_tensor(r["over"][:, :], place[:, :, e], float(CAP), elig[:, :, e].bitcast(F32), ALU.is_ge, ALU.mult))
                c.link(v.tensor_tensor(keep.plain[:, :], keep.plain[:, :], r["over"][:, :], ALU.subtract))
            c.link(v.scalar_tensor_tensor(kept[:, :, :], place[:, :, :], float(CAP), elig[:, :, :].bitcast(F32), ALU.is_lt, ALU.mult))
            c.link(v.scalar_tensor_tensor(place[:, :, :], lane, float(CAP), place[:, :, :], ALU.mult, ALU.add))
            for k in range(2):
                c.link(v.tensor_tensor(tmp[:, :, :], hot[k][:, :, :], kept[:, :, :], ALU.mult))
                c.link(v.reduce_sum(r["keptk"][:, :], tmp[:, :, :], AX.X))
                c.link(v.tensor_tensor(tmp[:, :, :], tmp[:, :, :], place[:, :, :], ALU.mult))
                c.link(v.reduce_sum(r["placek"][:, :], tmp[:, :, :], AX.X))
                c.link(v.tensor_scalar(r["pos"][:, :], r["keptk"][:, :], -FAR, FAR, ALU.mult, ALU.add))
                c.link(v.tensor_tensor(keep.place[:, :, k], r["placek"][:, :], r["pos"][:, :], ALU.add))
                c.link(v.tensor_tensor(r["keptk"][:, :], r["keptk"][:, :], keep.plain[:, :], ALU.mult))
                c.link(v.tensor_tensor(keep.weight[:, :, k], r["keptk"][:, :], r["s0" if k == 0 else "s1"][:, :], ALU.mult))
            c.link(v.tensor_scalar(r["over"][:, :], keep.plain[:, :], -1.0, 1.0, ALU.mult, ALU.add))
            v.reduce_sum(lost[:, :], r["over"][:, :], AX.X).then_inc(lost_done, 1)
            dve.wait_ge(lost_mm, 1)
            c.link(v.tensor_copy(keep.flag[:, :], cnt_ps[:, :]))


def experts(nc, keep, w1, b1, w2, b2, token, spare, h2_rows, total):
    XT = CAP // P
    GT = 2
    NG, W = XT // GT, GT * P
    RING = 4
    YR = 4
    CUT = 1024
    LT = (E + 1) * XT
    CH = 4
    LR = 4
    TURNS = 2 * NT // CH
    ROUND = 1.5 * 2.0 ** 23
    with ExitStack() as ctx:
        m = Program(nc, ctx, "ffn")
        w_hi = [[m.sbuf(f"w{k}_hi{i}", [P, KD * INNER], F32R) for k in (1, 2)] for i in range(2)]
        w_lo = [[m.sbuf(f"w{k}_lo{i}", [P, KD * INNER], F32R) for k in (1, 2)] for i in range(2)]
        raw = [m.sbuf(f"raw{i}", [P, CUT]) for i in range(2)]
        b1_rows = m.sbuf("b1_rows", [E * KI, P])
        b1_cols = m.sbuf("b1_cols", [P, E * KI])
        b2_sb = [m.sbuf(f"b2_{i}", [P, D]) for i in range(2)]
        read_row = m.sbuf("read_row", [P, LT], I32)
        add_row = m.sbuf("add_row", [P, LT], I32)
        weight = m.sbuf("weight", [P, B, LT])
        read_now = [m.sbuf(f"read_now{i}", [P, XT], I32) for i in range(2)]
        add_now = [m.sbuf(f"add_now{i}", [P, XT], I32) for i in range(2)]
        xs = [m.sbuf(f"xs{i}", [P, XT, D]) for i in range(2)]
        gate = m.sbuf("gate", [P, YR, D])
        gates = m.sbuf("gates", [P, GT, D])
        y = m.sbuf("y", [P, GT, D])
        ys = m.sbuf("ys", [P, YR, D])
        raw_in = [m.sem(f"raw_in{i}") for i in range(2)]
        b2_in = [m.sem(f"b2_in{i}") for i in range(2)]
        x_in = [[m.sem(f"x_in{i}_{g}") for g in range(NG)] for i in range(2)]
        added = [m.sem(f"added{i}") for i in range(YR)]
        b1_in, b1_mm, b1_done = m.sem("b1_in"), m.sem("b1_mm"), m.sem("b1")
        w_hi_done, w_lo_done, xT_mm, x_hi_done, x_lo_done, up_mm, up_done, h_hi_done, h_lo_done, y_mm, gate_done, y_done = (
            m.sem(s) for s in ("w_hi", "w_lo", "xT_mm", "x_hi", "x_lo", "up_mm", "up", "h_hi", "h_lo", "y_mm", "gate", "y"))
        t_in, prep_done, hot_done, token_done, weight_done, turn_mm, list_mm, read_done, add_done, all_added, chain, sum_done = (
            m.sem(s) for s in ("t_in", "prep", "hot", "token", "weight", "turn_mm", "list_mm", "read", "add", "all_added", "chain", "sum"))
        cuts = [(k, slice(c, c + CUT)) for k in range(2) for c in range(0, KD * INNER, CUT)]
        NC = len(cuts)
        px = [m.psum(f"px{i}", [P, KD, P]) for i in range(2)]
        p2 = [m.psum(f"p2_{i}", [P, D]) for i in range(2)]
        with ExitStack() as until_listed:
            ml = Program(nc, until_listed, "list")
            token_sb = ml.sbuf("token", [P, 2 * NTT])
            spare_sb = ml.sbuf("spare", [P, LT])
            zero = ml.sbuf("zero", [P, 3 * LT])
            low = ml.sbuf("low", [P, 2 * NTT])
            high = ml.sbuf("high", [P, 2 * NTT])
            part = ml.sbuf("part", [P, 2, 2 * NTT])
            hot_low = [ml.sbuf(f"hot_low{i}", [P, CH, P], F32R) for i in range(LR)]
            hot_high = [ml.sbuf(f"hot_high{i}", [P, CH, LT]) for i in range(LR)]
            value = [ml.sbuf(f"value{i}", [P, CH, 3, LT], F32R) for i in range(LR)]
            list_ps = [ml.psum(f"list{i}", [P, 3, LT]) for i in range(B)]
            col = [ml.sbuf(f"col{i}", [P, LT]) for i in range(3)]
        x_hi = m.sbuf("x_hi", [P, 2, KD, W], F32R)
        x_lo = m.sbuf("x_lo", [P, 2, KD, W], F32R)
        h = m.sbuf("h", [P, RING, W])
        h_hi = m.sbuf("h_hi", [P, 2, KI, W], F32R)
        h_lo = m.sbuf("h_lo", [P, 2, KI, W], F32R)
        p1 = [m.psum(f"p1_{i}", [P, W]) for i in range(RING)]
        block = ctx.enter_context(nc.Block())

        def groups(p):
            return [(p * NG + g, p, g) for g in range(NG)]

        both = groups(0) + groups(1)

        def wait_added(eng, it, n):
            if n < YR:
                eng.wait_ge(all_added, ready(it - 1))
            else:
                eng.wait_ge(added[n % YR], (it * (2 * XT // YR) + n // YR) * 16)

        @block.sync
        def _(sp):
            sp.dma_start(token_sb[:, :], token.rearrange("p n k -> p (n k)")).then_inc(t_in, 16)
            sp.dma_start(spare_sb[:, :], spare).then_inc(t_in, 16)
            sp.dma_start(b1_rows[:, :], b1.rearrange("e (m p) -> (e m) p", p=P)).then_inc(b1_in, 16)
            sp.dma_start(b2_sb[0][:, :], b2[0, None, :].to_broadcast([P, D])).then_inc(b2_in[0], 16)
            with sp.Fori(0, E // 2) as it:
                for p in range(2):
                    e = it * 2 + p
                    sp.wait_ge(y_done, ready(e * XT - 1))
                    apart(sp, keep)
                    sp.dma_start(b2_sb[1 - p][:, :], b2[(e + 1) % E, None, :].to_broadcast([P, D])).then_inc(b2_in[1 - p], 16)
            sp.wait_ge(b2_in[0], 16 * (E // 2 + 1))
            for i in range(YR):
                sp.wait_ge(added[i], 16 * E * XT // YR)

        @block.gpsimd
        def _(pool):
            pool.sem_inc(weight_done, CREDIT)
            pool.sem_inc(all_added, CREDIT)
            pool.wait_ge(prep_done, 1)
            for b in range(B):
                with pool.Fori(0, TURNS // LR) as it:
                    for i in range(LR):
                        u = b * TURNS + it * LR + i
                        pool.wait_ge(hot_done, ready(u))
                        apart(pool, keep)
                        for k in range(2):
                            last = nc.gpsimd.tensor_tensor(value[i][:, :, 1 + k, :], hot_high[i][:, :, :],
                                                           part[:, k, bass.ds(u * CH, CH)][:, :, None].to_broadcast([P, CH, LT]), ALU.mult)
                        last.then_inc(weight_done, 1)

            def gather(p, g):
                for t in range(g * GT, (g + 1) * GT):
                    nc.gpsimd.indirect_dma_start(xs[p][:, t, :], None, h2_rows.rearrange("n p d -> (n p) d"),
                                                 bass.IndirectOffsetOnAxis(ap=read_now[p][:, t:t + 1].bitcast(U32), axis=0),
                                                 bounds_check=NTOK - 1, oob_is_err=True).then_inc(x_in[p][g], 16)

            pool.wait_ge(read_done, CREDIT + 1)
            for g in range(NG):
                gather(0, g)
            with pool.Fori(0, E // 2) as it:
                for G, p, g in both:
                    e = it * 2 + p
                    if g == 0:
                        pool.wait_ge(read_done, ready(e + 1))
                    pool.wait_ge(xT_mm, ready((e - 1) * XT + (g + 1) * GT - 1))
                    apart(pool, keep)
                    gather(1 - p, g)
                    if g == 0:
                        for n in range(p * XT, p * XT + YR):
                            wait_added(pool, it, n)
                            apart(pool, keep)
                        pool.wait_ge(add_done, ready(e))
                    for t in range(g * GT, (g + 1) * GT):
                        pool.wait_ge(y_done, ready(e * XT + t))
                        apart(pool, keep)
                        i = (p * XT + t) % YR
                        nc.gpsimd.indirect_dma_start(total, bass.IndirectOffsetOnAxis(ap=add_now[p][:, t:t + 1].bitcast(U32), axis=0),
                                                     ys[:, i, :], None, bounds_check=NTOK + CAP - 1, oob_is_err=True,
                                                     compute_op=ALU.add).then_inc(added[i], 16)
                    for c in ((0, 1), (), (2, 3), ())[g] if g < 4 else ():
                        k, at = cuts[c]
                        pool.wait_ge(w_hi_done, ready((e + 1) * NC + c))
                        nc.gpsimd.tensor_tensor(w_lo[1 - p][k][:, at], raw[c % 2][:, :], w_hi[1 - p][k][:, at].bitcast(F32),
                                                ALU.subtract).then_inc(w_lo_done, 1)
                for i in range(YR):
                    pool.wait_ge(added[i], (it + 1) * (2 * XT // YR * 16))
                    apart(pool, keep)
                pool.sem_inc(all_added, 1)

        @block.scalar
        def _(act):
            act.sem_inc(up_done, CREDIT)
            act.sem_inc(w_hi_done, CREDIT)
            act.sem_inc(gate_done, CREDIT)

            def fetch(e, c):
                k, at = cuts[c]
                src = w1 if k == 0 else w2
                n = CUT // (INNER if k == 0 else D)
                i = at.start // CUT * n
                act.wait_ge(w_lo_done, ready(e * NC + c - 2))
                apart(act, keep)
                act.dma_start(raw[c % 2][:, :].rearrange("p (k n) -> p k n", k=n),
                              src[e % E].rearrange("(k p) n -> p k n", p=P)[:, i:i + n, :]).then_inc(raw_in[c % 2], 16)

            def round_off(p, c, arrived):
                k, at = cuts[c]
                act.wait_ge(raw_in[c % 2], arrived)
                nc.scalar.activation(w_hi[p][k][:, at], raw[c % 2][:, :], ACT.Copy).then_inc(w_hi_done, 1)

            assert NC == 4
            for c in (0, 2):
                for i in (c, c + 1):
                    fetch(0, i)
                for i in (c, c + 1):
                    round_off(0, i, c * 8 + 16)
            act.wait_ge(b1_done, 1)
            with act.Fori(0, E // 2) as it:
                for G, p, g in both:
                    e = it * 2 + p
                    for t in range(g * GT, (g + 1) * GT):
                        act.wait_ge(y_done, free(e * XT + t, YR))
                        apart(act, keep)
                        nc.scalar.activation(gate[:, (p * XT + t) % YR, :], keep.mod[:, 1, 5, :], ACT.Copy,
                                             scale=weight[:, 1, bass.ds(e * XT + t, 1)]).then_inc(gate_done, 1)
                    for k in range(KI):
                        u = (e * NG + g) * KI + k
                        act.wait_ge(up_mm, ready(u))
                        act.wait_ge(h_lo_done, free(u, RING))
                        apart(act, keep)
                        nc.scalar.activation(h[:, (G * KI + k) % RING, :], p1[(G * KI + k) % RING][:, :], ACT.Gelu,
                                             bias=b1_cols[:, bass.ds(e * KI + k, 1)]).then_inc(up_done, 1)
                    for c in ((0, 1), (), (2, 3), ())[g] if g < 4 else ():
                        fetch(e + 1, c)
                    for c in ((), (0, 1), (), (2, 3))[g] if g < 4 else ():
                        round_off(1 - p, c, it * 64 + 32 * p + 48 + 16 * (c // 2))

        @block.vector
        def _(dve):
            for s in (sum_done, hot_done, token_done, read_done, add_done, w_lo_done, x_hi_done, x_lo_done, h_hi_done, h_lo_done, y_done):
                dve.sem_inc(s, CREDIT)
            c = Chain(dve, chain)
            v = nc.vector
            place = keep.place[:, :, :].rearrange("p n k -> p (n k)")
            weights = keep.weight[:, :, :].rearrange("p n k -> p (n k)")
            c.link(v.memset(zero[:, :], 0.0))
            c.link(v.tensor_copy(part[:, 0, :].bitcast(F32R), weights))
            c.link(v.tensor_scalar(high[:, :], place, 1.0 / P, -(P - 1) / (2.0 * P), ALU.mult, ALU.add))
            c.link(v.tensor_scalar(high[:, :], high[:, :], ROUND, None, ALU.add))
            c.link(v.tensor_scalar(high[:, :], high[:, :], -ROUND, None, ALU.add))
            c.link(v.scalar_tensor_tensor(low[:, :], high[:, :], -float(P), place, ALU.mult, ALU.add))
            v.tensor_tensor(part[:, 1, :], weights, part[:, 0, :], ALU.subtract).then_inc(prep_done, 1)

            def numbers(u, i):
                dve.wait_ge(t_in, 32)
                dve.wait_ge(hot_done, ready(u))
                apart(dve, keep)
                v.tensor_tensor(value[i][:, :, 0, :], hot_high[i][:, :, :],
                                token_sb[:, bass.ds(u * CH, CH)][:, :, None].to_broadcast([P, CH, LT]), ALU.mult).then_inc(token_done, 1)

            for b in range(B):
                with dve.Fori(0, TURNS // LR) as it:
                    for i in range(LR):
                        u = b * TURNS + it * LR + i
                        at = bass.ds(u * CH, CH)
                        dve.wait_ge(turn_mm, free(u, LR))
                        apart(dve, keep)
                        v.tensor_tensor(hot_low[i][:, :, :], keep.lanes[:, None, :].to_broadcast([P, CH, P]),
                                        low[:, at][:, :, None].to_broadcast([P, CH, P]), ALU.is_equal)
                        v.tensor_tensor(hot_high[i][:, :, :], keep.lanes[:, None, 0:LT].to_broadcast([P, CH, LT]),
                                        high[:, at][:, :, None].to_broadcast([P, CH, LT]), ALU.is_equal).then_inc(hot_done, 1)
                        if i:
                            numbers(u - 1, i - 1)
                    numbers(b * TURNS + it * LR + LR - 1, LR - 1)
                for i in range(b * NC // B, (b + 1) * NC // B):
                    k, at = cuts[i]
                    dve.wait_ge(w_hi_done, ready(i))
                    nc.vector.tensor_tensor(w_lo[0][k][:, at], raw[i % 2][:, :], w_hi[0][k][:, at].bitcast(F32),
                                            ALU.subtract).then_inc(w_lo_done, 1)
            dve.wait_ge(list_mm, B)
            number, empty, row = (x[:, :] for x in col)
            c.link(v.tensor_copy(row, list_ps[0][:, 0, :]))
            c.link(v.tensor_tensor(number, list_ps[1][:, 0, :], row, ALU.add))
            c.link(v.tensor_scalar(empty, number, 0.0, None, ALU.is_equal))
            c.link(v.scalar_tensor_tensor(row, number, -1.0, empty, ALU.add, ALU.add))
            c.link(v.tensor_copy(read_row[:, :], row))

            def reads(e, p):
                v.tensor_copy(read_now[p][:, :], read_row[:, bass.ds(e * XT, XT)]).then_inc(read_done, 1)

            def adds(e, p):
                v.tensor_copy(add_now[p][:, :], add_row[:, bass.ds(e * XT, XT)]).then_inc(add_done, 1)

            reads(0, 0)
            c.link(v.tensor_tensor(row, empty, spare_sb[:, :], ALU.mult))
            c.link(v.scalar_tensor_tensor(row, number, -1.0, row, ALU.add, ALU.add))
            c.link(v.tensor_copy(add_row[:, :], row))
            adds(0, 0)
            for b in range(B):
                c.link(v.tensor_copy(row, list_ps[b][:, 2, :]))
                c.link(v.tensor_tensor(weight[:, b, :], list_ps[b][:, 1, :], row, ALU.add))
            dve.wait_ge(b1_mm, 1)
            nc.vector.tensor_copy(b1_cols[:, :], p2[0][:, 0:E * KI]).then_inc(b1_done, 1)

            def inputs(e, G, g):
                for i in range(GT):
                    n = e * XT + g * GT + i
                    at = slice(i * P, (i + 1) * P)
                    dve.wait_ge(xT_mm, ready(n))
                    if i == 0:
                        dve.wait_ge(up_mm, ready((e * NG + g - 1) * KI - 1))
                    nc.vector.tensor_copy(x_hi[:, G % 2, :, at], px[i][:, :, :]).then_inc(x_hi_done, 1)
                    dve.wait_ge(x_hi_done, ready(n))
                    nc.vector.tensor_tensor(x_lo[:, G % 2, :, at], px[i][:, :, :], x_hi[:, G % 2, :, at].bitcast(F32),
                                            ALU.subtract).then_inc(x_lo_done, 1)

            inputs(0, 0, 0)
            with dve.Fori(0, E // 2) as it:

                def hidden(p, G, g):
                    e = it * 2 + p
                    for k in range(KI):
                        u = (e * NG + g) * KI + k
                        piece = h[:, (G * KI + k) % RING, :]
                        dve.wait_ge(up_done, ready(u))
                        if k == 0:
                            dve.wait_ge(y_mm, ready((e * NG + g - 1) * GT - 1))
                        nc.vector.tensor_copy(h_hi[:, G % 2, k, :], piece).then_inc(h_hi_done, 1)
                        dve.wait_ge(h_hi_done, ready(u))
                        nc.vector.tensor_tensor(h_lo[:, G % 2, k, :], piece, h_hi[:, G % 2, k, :].bitcast(F32), ALU.subtract).then_inc(h_lo_done, 1)

                def outputs(p, G, g):
                    e = it * 2 + p
                    if g == 0:
                        dve.wait_ge(b2_in[p], it * 16 + 16)
                    tiles = [(e * XT + g * GT + i, (G * GT + i) % YR, i) for i in range(GT)]
                    for n, slot, i in tiles:
                        dve.wait_ge(gate_done, ready(n))
                        dve.wait_ge(y_done, free(n, GT))
                        nc.vector.scalar_tensor_tensor(gates[:, i, :], keep.mod[:, 0, 5, :], weight[:, 0, bass.ds(n, 1)],
                                                       gate[:, slot, :], ALU.mult, ALU.add)
                    for n, slot, i in tiles:
                        dve.wait_ge(y_mm, ready(n))
                        nc.vector.tensor_tensor(y[:, i, :], p2[i][:, :], b2_sb[p][:, :], ALU.add).then_inc(sum_done, 1)
                    for n, slot, i in tiles:
                        dve.wait_ge(sum_done, ready(n))
                        wait_added(dve, it, G * GT + i)
                        nc.vector.tensor_tensor(ys[:, slot, :], y[:, i, :], gates[:, i, :], ALU.mult).then_inc(y_done, 1)
                    if g == 2:
                        adds(e + 1, 1 - p)

                for G, p, g in both:
                    e = it * 2 + p
                    if g == 0:
                        reads(e + 1, 1 - p)
                    inputs(*((e, G + 1, g + 1) if g + 1 < NG else (e + 1, G + 1, 0)))
                    hidden(p, G, g)
                    if G:
                        outputs(both[G - 1][1], G - 1, both[G - 1][2])
                outputs(1, 2 * NG - 1, NG - 1)

        @block.tensor
        def _(pe):
            for s in (turn_mm, xT_mm, up_mm, y_mm):
                pe.sem_inc(s, CREDIT)
            pe.wait_ge(prep_done, 1)
            for b in range(B):
                sums = list_ps[b][:, :, :].rearrange("p k n -> p (k n)")
                nc.tensor.matmul(sums, zero[0:1, 0:P], zero[0:1, :], start=True, stop=False)
                with pe.Fori(0, TURNS // LR) as it:
                    for i in range(LR):
                        u = b * TURNS + it * LR + i
                        pe.wait_ge(token_done, ready(u))
                        pe.wait_ge(weight_done, ready(u))
                        for j in range(CH):
                            last = nc.tensor.matmul(sums, hot_low[i][:, j, :], value[i][:, j, :, :].rearrange("p k n -> p (k n)"),
                                                    start=False, stop=False)
                        last.then_inc(turn_mm, 1)
                nc.tensor.matmul(sums, zero[0:1, 0:P], zero[0:1, :], start=False, stop=True).then_inc(list_mm, 1)
            pe.wait_ge(b1_in, 16)
            nc.tensor.transpose(p2[0][:, 0:E * KI], b1_rows[:, :], keep.ident[0:E * KI, 0:E * KI]).then_inc(b1_mm, 1)
            pe.wait_ge(b1_done, 1)

            def turn(e, p, g, arrived):
                pe.wait_ge(x_in[p][g], arrived)
                for i in range(GT):
                    n = e * XT + g * GT + i
                    pe.wait_ge(x_lo_done, free(n, 2))
                    for k in range(KD):
                        last = nc.tensor.transpose(px[i][:, k, :], xs[p][:, g * GT + i, k * P:(k + 1) * P], keep.ident[:, :])
                    last.then_inc(xT_mm, 1)

            turn(0, 0, 0, 16 * GT)
            with pe.Fori(0, E // 2) as it:

                def up(p, G, g):
                    e = it * 2 + p
                    if g == 0:
                        pe.wait_ge(w_lo_done, ready(e * NC + NC - 1))
                    pe.wait_ge(x_lo_done, ready((e * NG + g) * GT + GT - 1))
                    for j in range(KI):
                        u = (e * NG + g) * KI + j
                        pe.wait_ge(up_done, free(u, RING))
                        terms = [(a, b, k) for a, b in ((w_hi[p][0], x_hi), (w_hi[p][0], x_lo), (w_lo[p][0], x_hi)) for k in range(KD)]
                        for i, (a, b, k) in enumerate(terms):
                            at = slice(k * INNER + j * P, k * INNER + (j + 1) * P)
                            last = nc.tensor.matmul(p1[(G * KI + j) % RING][:, :], a[:, at].bitcast(F32R), b[:, G % 2, k, :],
                                                    start=(i == 0), stop=(i == len(terms) - 1))
                        last.then_inc(up_mm, 1)

                def down(p, G, g):
                    e = it * 2 + p
                    pe.wait_ge(h_lo_done, ready((e * NG + g) * KI + KI - 1))
                    for i in range(GT):
                        t = g * GT + i
                        pe.wait_ge(y_done, free(e * XT + t, 2))
                        terms = [(a, b, j) for a, b in ((h_hi, w_hi[p][1]), (h_lo, w_hi[p][1]), (h_hi, w_lo[p][1])) for j in range(KI)]
                        for o, (a, b, j) in enumerate(terms):
                            last = nc.tensor.matmul(p2[t % 2][:, :], a[:, G % 2, j, i * P:(i + 1) * P],
                                                    b[:, j * D:(j + 1) * D].bitcast(F32R), start=(o == 0), stop=(o == len(terms) - 1))
                        last.then_inc(y_mm, 1)

                for G, p, g in both:
                    e = it * 2 + p
                    if g + 1 < NG:
                        turn(e, p, g + 1, it * 16 * GT + 16 * GT)
                    else:
                        turn(e + 1, 1 - p, 0, (it + p) * 16 * GT + 16 * GT)
                    up(p, G, g)
                    if G:
                        down(both[G - 1][1], G - 1, both[G - 1][2])
                down(1, 2 * NG - 1, NG - 1)


def finish(nc, total, out):
    with ExitStack() as ctx:
        m = Program(nc, ctx, "finish")
        st = m.sem("st")
        out_rows = out.rearrange("b t d -> (b t) d")
        PARTS = 4
        n = NTOK // PARTS
        block = ctx.enter_context(nc.Block())

        def copy(eng, i):
            at = slice(i * n, (i + 1) * n)
            eng.dma_start(out_rows[at, :], total[at, :]).then_inc(st, 16)

        @block.sync
        def _(sp):
            copy(sp, 0)
            copy(sp, 1)
            sp.wait_ge(st, 16 * PARTS)

        @block.scalar
        def _(act):
            copy(act, 2)
            copy(act, 3)


def fall_back(nc, keep, fw1, fb1, fw2, fb2, h2_rows, out):
    with ExitStack() as ctx:
        m = Program(nc, ctx, "fall")
        w1 = m.sbuf("w1", [P, KD, INNER])
        w2 = m.sbuf("w2", [P, KI, D])
        b1_rows = m.sbuf("b1_rows", [KI, P])
        b1_cols = m.sbuf("b1_cols", [P, KI])
        b2 = m.sbuf("b2", [P, D])
        x = m.sbuf("x", [P, D])
        o = m.sbuf("o", [P, D])
        xT = m.sbuf("xT", [P, KD, P])
        hT = m.sbuf("hT", [P, KI, P])
        y = m.sbuf("y", [P, D])
        missing = m.sbuf("missing", [P, NTT])
        px = m.psum("px", [P, KD, P])
        p1 = m.psum("p1", [P, KI, P])
        p2 = m.psum("p2", [P, D])
        w_in, t_in, t_st = m.sem("w_in"), m.sem("t_in"), m.sem("t_st")
        b1_mm, b1_done, xT_mm, xT_done, up_mm, up_done, y_mm, o_done, chain = (
            m.sem(s) for s in ("b1_mm", "b1", "xT_mm", "xT", "up_mm", "up", "y_mm", "o", "chain"))
        h_t = h2_rows
        out_t = out.rearrange("b (t p) d -> (b t) p d", p=P)
        block = ctx.enter_context(nc.Block())

        def overflowed(eng):
            return eng.If(eng.value_load(keep.flag[0:1, 0:1], min_val=0, max_val=NTOK) > 0)

        @block.sync
        def _(sp):
            with overflowed(sp):
                sp.dma_start(w1[:, :, :], fw1.rearrange("(k p) n -> p k n", p=P)).then_inc(w_in, 16)
                sp.dma_start(w2[:, :, :], fw2.rearrange("(m p) n -> p m n", p=P)).then_inc(w_in, 16)
                sp.dma_start(b1_rows[:, :], fb1.rearrange("(m p) -> m p", p=P)).then_inc(w_in, 16)
                sp.dma_start(b2[:, :], fb2[None, :].to_broadcast([P, D])).then_inc(w_in, 16)
                sp.sem_inc(t_st, 1)
                with sp.Fori(0, NTT) as n:
                    sp.wait_ge(t_st, n * 16 + 1)
                    sp.dma_start(x[:, :], h_t[n]).then_inc(t_in, 16)
                    sp.dma_start(o[:, :], out_t[n]).then_inc(t_in, 16)
                    sp.wait_ge(o_done, n + 1)
                    sp.dma_start(out_t[n], o[:, :]).then_inc(t_st, 16)
                sp.wait_ge(t_st, 1 + 16 * NTT)

        @block.scalar
        def _(act):
            with overflowed(act):
                act.wait_ge(b1_done, 1)
                with act.Fori(0, NTT) as n:
                    act.wait_ge(up_mm, n + 1)
                    for k in range(KI):
                        last = nc.scalar.activation(hT[:, k, :], p1[:, k, :], ACT.Gelu, bias=b1_cols[:, k:k + 1])
                    last.then_inc(up_done, 1)

        @block.vector
        def _(dve):
            with overflowed(dve):
                c = Chain(dve, chain)
                dve.wait_ge(b1_mm, 1)
                nc.vector.tensor_copy(b1_cols[:, :], px[:, 0, 0:KI]).then_inc(b1_done, 1)
                c.link(nc.vector.tensor_scalar(missing[:, :], keep.plain[:, :], -1.0, 1.0, ALU.mult, ALU.add))
                with dve.Fori(0, NTT) as n:
                    c = Chain(dve, chain, n * 3 + 1)
                    dve.wait_ge(xT_mm, n + 1)
                    nc.vector.tensor_copy(xT[:, :, :], px[:, :, :]).then_inc(xT_done, 1)
                    dve.wait_ge(y_mm, n + 1)
                    c.link(nc.vector.tensor_tensor(y[:, :], p2[:, :], b2[:, :], ALU.add))
                    c.link(nc.vector.tensor_scalar(y[:, :], y[:, :], missing[:, bass.ds(n, 1)], None, ALU.mult))
                    c.link(nc.vector.tensor_tensor(y[:, :], y[:, :], keep.mod[:, n // NT, 5, :], ALU.mult))
                    dve.wait_ge(t_in, n * 32 + 32)
                    nc.vector.tensor_tensor(o[:, :], o[:, :], y[:, :], ALU.add).then_inc(o_done, 1)

        @block.tensor
        def _(pe):
            with overflowed(pe):
                pe.wait_ge(w_in, 64)
                nc.tensor.transpose(px[:, 0, 0:KI], b1_rows[:, :], keep.ident[0:KI, 0:KI]).then_inc(b1_mm, 1)
                pe.wait_ge(b1_done, 1)
                with pe.Fori(0, NTT) as n:
                    pe.wait_ge(t_in, n * 32 + 32)
                    for k in range(KD):
                        last = nc.tensor.transpose(px[:, k, :], x[:, k * P:(k + 1) * P], keep.ident[:, :])
                    last.then_inc(xT_mm, 1)
                    pe.wait_ge(xT_done, n + 1)
                    for j in range(KI):
                        for k in range(KD):
                            last = nc.tensor.matmul(p1[:, j, :], w1[:, k, j * P:(j + 1) * P], xT[:, k, :], start=(k == 0), stop=(k == KD - 1))
                    last.then_inc(up_mm, 1)
                    pe.wait_ge(up_done, n + 1)
                    for j in range(KI):
                        last = nc.tensor.matmul(p2[:, :], hT[:, j, :], w2[:, j, :], start=(j == 0), stop=(j == KI - 1))
                    last.then_inc(y_mm, 1)


class Keep:
    pass


def build(nc, dr):
    with ExitStack() as ctx:
        keep = Keep()
        m = Program(nc, ctx, "keep")
        keep.weight = m.sbuf("weight", [P, NTT, 2])
        keep.place = m.sbuf("place", [P, NTT, 2])
        keep.lanes = m.sbuf("lanes", [P, P])
        keep.plain = m.sbuf("plain", [P, NTT])
        keep.flag = m.sbuf("flag", [P, 1], I32)
        keep.ident = m.sbuf("ident", [P, P])
        keep.before = m.sbuf("before", [P, P])
        keep.mod = m.sbuf("mod", [P, B, 6, D])
        keep.sign = m.sbuf("sign", [P, D])
        keep.shift1 = m.sbuf("shift1", [P, B, KD])
        keep.scale1 = m.sbuf("scale1", [P, B, KD])
        keep.neg_half = m.sbuf("neg_half", [P, PAIRS, NT])
        keep.row_max = m.sbuf("row_max", [P, PAIRS, NT, 2])
        keep.logits = m.sbuf("logits", [P, NTT, E])
        scratch = lambda name, shape: nc.dram_tensor(name, shape, F32, kind="Internal").ap()
        q_rows = scratch("q_rows", (B, HEADS, HD, T))
        k_rows = scratch("k_rows", (B, KVH, HD, T))
        v_cent = scratch("v_cent", (B, KVH, P, NT, HD))
        gate_logit = scratch("gate_logit", (B, KVH, T))
        half_log = scratch("half_log", (PAIRS, T))
        num_rows = scratch("num_rows", (PAIRS, P, T))
        keep.passed = m.sem("passed")
        with ExitStack() as until_attended:
            rows = rows_memory(nc, until_attended)
            with ExitStack() as until_projected:
                early = early_memory(nc, until_projected)
                modulation(nc, keep, early, rows, dr["L0_c"], dr["L0_wmod"], dr["L0_attn_x"], dr["L0_attn_w_attn"],
                           dr["rope"], dr["basis"], dr["ident"], dr["before"])
                used_up = project(nc, keep, early, dr["L0_attn_x"], q_rows, k_rows, v_cent, gate_logit)
            first = first_pair_memory(nc, until_attended)
            decays(nc, keep, first, rows, used_up, gate_logit, half_log, q_rows, k_rows, v_cent)
            attend(nc, keep, first, q_rows, k_rows, v_cent, half_log, num_rows)
        h2_rows = scratch("h2_rows", (NTT, P, D))
        total = scratch("total", (NTOK + CAP, D))
        with ExitStack() as until_chosen:
            keep.x1 = Program(nc, until_chosen, "keep").sbuf("x1", [P, NTT, D])
            close_attention(nc, keep, dr["L0_attn_x"], dr["L0_attn_w_proj"], dr["L0_attn_ln_w"], dr["L0_ffn_Wr"], dr["basis"],
                            num_rows, h2_rows)
            choose(nc, keep, dr["lanes"], dr["upto"], total)
        experts(nc, keep, dr["L0_ffn_W1"], dr["L0_ffn_b1"], dr["L0_ffn_W2"], dr["L0_ffn_b2"], dr["token"], dr["spare"],
                h2_rows, total)
        finish(nc, total, dr["out"])
        fall_back(nc, keep, dr["L0_ffn_fw1"], dr["L0_ffn_fb1"], dr["L0_ffn_fw2"], dr["L0_ffn_fb2"], h2_rows, dr["out"])


_INS = ['L0_attn_x', 'L0_attn_w_attn', 'L0_attn_w_proj', 'L0_attn_ln_w', 'L0_ffn_Wr', 'L0_ffn_W1', 'L0_ffn_b1',
        'L0_ffn_W2', 'L0_ffn_b2', 'L0_ffn_fw1', 'L0_ffn_fb1', 'L0_ffn_fw2', 'L0_ffn_fb2', 'L0_c', 'L0_wmod']


def shape_constants():
    import numpy as np
    div = (2.0 * np.pi / float(T) ** (np.arange(0, HD, 2, dtype=np.float32) / HD)).astype(np.float32)
    ang = (np.arange(T, dtype=np.float32)[:, None] * div[None, :]).astype(np.float64)
    cos = np.repeat(np.cos(ang), 2, axis=1)
    sin = np.repeat(np.sin(ang), 2, axis=1)
    sin[:, 0::2] *= -1.0
    scale = HD ** -0.5
    tab = np.stack([cos * scale, sin * scale, cos, sin]).astype(np.float32)
    rope = np.ascontiguousarray(tab.reshape(4, NT, P, HD).transpose(2, 0, 1, 3))
    r = np.arange(P)
    ch = P // PAIRS
    before = ((r[:, None] // ch == r[None, :] // ch) & (r[:, None] < r[None, :])).astype(np.float32)
    d = np.arange(HD)
    cosines = np.sqrt(2.0 / HD) * np.cos(np.pi * (d[:, None] + 0.5) * (d[None, :] + 1) / HD)
    cosines[:, HD - 1] = 0.0
    basis = np.zeros((P, P), np.float32)
    for h in range(2):
        basis[h * HD:(h + 1) * HD, h * HD:(h + 1) * HD] = cosines
    upto = (r[:, None] <= r[None, :]).astype(np.float32)
    lanes = np.ascontiguousarray(np.broadcast_to(np.arange(P, dtype=np.float32), (P, P)))
    token = np.repeat((np.arange(NTT)[None, :, None] * P + r[:, None, None] + 1).astype(np.float32), 2, axis=2)
    t = np.arange((E + 1) * CAP // P) % (CAP // P)
    spare = (NTOK + t[None, :] * P + r[:, None] + 1).astype(np.float32)
    return {"upto": upto, "lanes": lanes, "token": token, "spare": spare, "basis": basis, "rope": rope,
            "ident": np.eye(P, dtype=np.float32), "before": before}


def kernel(**inputs):
    import numpy as np
    import concourse.bacc as bacc
    from concourse.bass_utils import run_bass_kernel_spmd

    nc = bacc.Bacc("TRN2", target_bir_lowering=False, num_devices=1)
    arrays = {name: np.ascontiguousarray(inputs[name]) for name in _INS} | shape_constants()
    dr = {name: nc.dram_tensor(name, a.shape, mybir.dt.from_np(a.dtype), kind="ExternalInput").ap() for name, a in arrays.items()}
    dr["out"] = nc.dram_tensor("out", (B, T, D), F32, kind="ExternalOutput").ap()
    build(nc, dr)
    r = run_bass_kernel_spmd(nc, [arrays], core_ids=[0])
    return r.results[0]["out"]
```
